# Optimizing a Trainium2 kernel written in Bass

```python
import numpy as np
import jax
import jax.numpy as jnp

def _softmax(x, axis=-1):
    return jax.nn.softmax(x, axis=axis)

def _gelu(x):
    return jax.nn.gelu(x, approximate=True)

def _silu(x):
    return jax.nn.silu(x)

def _sigmoid(x):
    return jax.nn.sigmoid(x)

def _layernorm(x, axis=-1, eps=1e-05):
    m = jnp.mean(x, axis=axis, keepdims=True)
    v = jnp.var(x, axis=axis, keepdims=True)
    return (x - m) / jnp.sqrt(v + eps)

def _scatter_add(tgt, idx, src, axis=0):
    return tgt.at[idx].add(src)

def _segment_sum(src, seg, n):
    return jax.ops.segment_sum(src, seg, n)
kernel_name = 'mk_gnn_preln_d4_gnn_r8_a1b998'

def setup_inputs(seed: int=0):
    np.random.seed(seed)
    _w = jnp.asarray

    def _rec_inputs():
        import jax
        import jax.numpy as jnp
        _gk = jax.random.key(seed)
        x = -0.0002117 + 1 * jax.random.normal(jax.random.fold_in(_gk, 1), (6250, 256), jnp.float32)
        src = jax.random.randint(jax.random.fold_in(_gk, 2), (100000,), 0, 6250, jnp.int32)
        dst = jax.random.randint(jax.random.fold_in(_gk, 3), (100000,), 0, 6250, jnp.int32)
        _o = jnp.argsort(dst, stable=True)
        src = src[_o]
        dst = dst[_o]
        edge_type_11 = jax.random.randint(jax.random.fold_in(_gk, 13), (100000,), 0, 11, jnp.int32)
        edge_type_8 = jax.random.randint(jax.random.fold_in(_gk, 14), (100000,), 0, 8, jnp.int32)
        return (x, src, dst, edge_type_11, edge_type_8)
    x, src, dst, edge_type_11, edge_type_8 = _rec_inputs()

    def _L0_gnn_setup():
        import jax, jax.numpy as jnp
        import numpy as np
        NUM_NODES = 12500
        HIDDEN = 256
        NUM_EDGES = 200000

        def _sage_conv(x, edge_index, w_l, w_r, b):
            src, dst = (edge_index[0], edge_index[1])
            n = x.shape[0]
            nbr_sum = jax.ops.segment_sum(x[src], dst, num_segments=n)
            deg = jax.ops.segment_sum(jnp.ones((src.shape[0],), x.dtype), dst, num_segments=n)
            nbr_mean = nbr_sum / jnp.maximum(deg, 1.0)[:, None]
            return nbr_mean @ w_l.T + x @ w_r.T + b
        key = jax.random.key(seed)
        ks = jax.random.split(key, 8)

        def glorot(k, shape):
            lim = float(np.sqrt(6.0 / (shape[0] + shape[1])))
            return jax.random.uniform(k, shape, jnp.float32, -lim, lim)
        return {'node_features': jax.random.normal(ks[0], (NUM_NODES, HIDDEN), jnp.float32), 'w1_l': glorot(ks[1], (HIDDEN, HIDDEN)), 'w1_r': glorot(ks[2], (HIDDEN, HIDDEN)), 'b1': jnp.zeros((HIDDEN,), jnp.float32), 'w2_l': glorot(ks[3], (HIDDEN, HIDDEN)), 'w2_r': glorot(ks[4], (HIDDEN, HIDDEN)), 'b2': jnp.zeros((HIDDEN,), jnp.float32), 'edge_index': jax.random.randint(ks[5], (2, NUM_EDGES), 0, NUM_NODES, jnp.int64)}
    _L0_gnn_all = _L0_gnn_setup()
    _L0_gnn_in = {k: v for k, v in _L0_gnn_all.items() if k in ('w1_l', 'w1_r', 'b1', 'w2_l', 'w2_r', 'b2')}
    del _L0_gnn_all

    def _L1_gnn_setup():
        import jax, jax.numpy as jnp
        import numpy as np
        N, E, R, H, D = (3750, 37500, 8, 8, 32)
        IN_F = 256
        NEG_SLOPE = 0.2
        key = jax.random.key(seed)
        k = jax.random.split(key, 6)
        x = jax.random.normal(k[0], (N, IN_F), dtype=jnp.float32)
        W = jax.random.normal(k[1], (R, H * D, IN_F), dtype=jnp.float32) * 0.05
        attn_src = jax.random.normal(k[2], (H, D), dtype=jnp.float32) * 0.1
        attn_dst = jax.random.normal(k[3], (H, D), dtype=jnp.float32) * 0.1
        edge_index = jax.random.randint(k[4], (2, E), 0, N, dtype=jnp.int64) if jax.config.read('jax_enable_x64') else jax.random.randint(k[4], (2, E), 0, N, dtype=jnp.int32)
        edge_type = jax.random.randint(k[5], (E,), 0, R, dtype=edge_index.dtype)
        return dict(x=x, W=W, attn_src=attn_src, attn_dst=attn_dst, edge_index=edge_index, edge_type=edge_type)
    _L1_gnn_all = _L1_gnn_setup()
    _L1_gnn_in = {k: v for k, v in _L1_gnn_all.items() if k in ('W', 'attn_src', 'attn_dst')}
    del _L1_gnn_all

    def _L2_gnn_setup():
        import jax, jax.numpy as jnp
        import numpy as np
        N = 12500
        E = 400000
        D_IN = 256
        D_OUT = 256
        NUM_REL = 10
        key = jax.random.key(seed)
        k1, k2, k3, k4, k5, k6 = jax.random.split(key, 6)
        x = jax.random.normal(k1, (N, D_IN), dtype=jnp.float32)
        edge_index = jax.random.randint(k2, (2, E), 0, N, dtype=jnp.int64)
        rel = jax.random.randint(k3, (E,), 0, NUM_REL + 1, dtype=jnp.int64)
        stdv = 1.0 / np.sqrt(D_OUT)
        weight = jax.random.uniform(k4, (D_IN, D_OUT), dtype=jnp.float32, minval=-stdv, maxval=stdv)
        bias = jax.random.uniform(k5, (D_OUT,), dtype=jnp.float32, minval=-stdv, maxval=stdv)
        alpha = jax.random.normal(k6, (NUM_REL + 1, 1), dtype=jnp.float32)
        alpha = alpha.at[0].set(0.0)
        return {'x': x, 'edge_index': edge_index, 'rel': rel, 'weight': weight, 'bias': bias, 'alpha': alpha}
    _L2_gnn_all = _L2_gnn_setup()
    _L2_gnn_in = {k: v for k, v in _L2_gnn_all.items() if k in ('weight', 'bias', 'alpha')}
    del _L2_gnn_all

    def _L3_gnn_setup():
        import jax, jax.numpy as jnp
        import numpy as np
        N_NODES = 12500
        N_EDGES = 200000
        IN_DIM = 256
        HID = 64
        HEADS = 2
        OUT_DIM = 256
        NEG_SLOPE = 0.2
        key = jax.random.key(seed)
        ks = jax.random.split(key, 10)
        feat = jax.random.normal(ks[0], (N_NODES, IN_DIM), dtype=jnp.float32)
        src = jax.random.randint(ks[1], (N_EDGES,), 0, N_NODES)
        dst = jax.random.randint(ks[2], (N_EDGES,), 0, N_NODES)
        W = jax.random.normal(ks[3], (IN_DIM, HEADS * HID), dtype=jnp.float32) * 0.05
        attn_l = jax.random.normal(ks[4], (HEADS, HID), dtype=jnp.float32) * 0.05
        attn_r = jax.random.normal(ks[5], (HEADS, HID), dtype=jnp.float32) * 0.05
        gat_bias = jnp.zeros((HEADS * HID,), dtype=jnp.float32)
        lin_W = jax.random.normal(ks[6], (HEADS * HID, OUT_DIM), dtype=jnp.float32) * 0.05
        lin_b = jnp.zeros((OUT_DIM,), dtype=jnp.float32)
        return {'feat': feat, 'src': src, 'dst': dst, 'W': W, 'attn_l': attn_l, 'attn_r': attn_r, 'gat_bias': gat_bias, 'lin_W': lin_W, 'lin_b': lin_b}
    _L3_gnn_all = _L3_gnn_setup()
    _L3_gnn_in = {k: v for k, v in _L3_gnn_all.items() if k in ('W', 'attn_l', 'attn_r', 'gat_bias', 'lin_W', 'lin_b')}
    del _L3_gnn_all
    return {'x': x, 'src': src, 'dst': dst, 'edge_type_11': edge_type_11, 'edge_type_8': edge_type_8, 'L0_gnn_w1_l': _L0_gnn_in['w1_l'], 'L0_gnn_w1_r': _L0_gnn_in['w1_r'], 'L0_gnn_b1': _L0_gnn_in['b1'], 'L0_gnn_w2_l': _L0_gnn_in['w2_l'], 'L0_gnn_w2_r': _L0_gnn_in['w2_r'], 'L0_gnn_b2': _L0_gnn_in['b2'], 'L1_gnn_W': _L1_gnn_in['W'], 'L1_gnn_attn_src': _L1_gnn_in['attn_src'], 'L1_gnn_attn_dst': _L1_gnn_in['attn_dst'], 'L2_gnn_weight': _L2_gnn_in['weight'], 'L2_gnn_bias': _L2_gnn_in['bias'], 'L2_gnn_alpha': _L2_gnn_in['alpha'], 'L3_gnn_W': _L3_gnn_in['W'], 'L3_gnn_attn_l': _L3_gnn_in['attn_l'], 'L3_gnn_attn_r': _L3_gnn_in['attn_r'], 'L3_gnn_gat_bias': _L3_gnn_in['gat_bias'], 'L3_gnn_lin_W': _L3_gnn_in['lin_W'], 'L3_gnn_lin_b': _L3_gnn_in['lin_b']}

def reference(x, src, dst, edge_type_11, edge_type_8, L0_gnn_w1_l, L0_gnn_w1_r, L0_gnn_b1, L0_gnn_w2_l, L0_gnn_w2_r, L0_gnn_b2, L1_gnn_W, L1_gnn_attn_src, L1_gnn_attn_dst, L2_gnn_weight, L2_gnn_bias, L2_gnn_alpha, L3_gnn_W, L3_gnn_attn_l, L3_gnn_attn_r, L3_gnn_gat_bias, L3_gnn_lin_W, L3_gnn_lin_b):
    import jax
    import jax.numpy as jnp

    def _L0_gnn_ref(node_features, w1_l, w1_r, b1, w2_l, w2_r, b2, edge_index):
        import jax, jax.numpy as jnp
        import numpy as np
        NUM_NODES = 12500
        HIDDEN = 256
        NUM_EDGES = 200000

        def _sage_conv(x, edge_index, w_l, w_r, b):
            src, dst = (edge_index[0], edge_index[1])
            n = x.shape[0]
            nbr_sum = jax.ops.segment_sum(x[src], dst, num_segments=n)
            deg = jax.ops.segment_sum(jnp.ones((src.shape[0],), x.dtype), dst, num_segments=n)
            nbr_mean = nbr_sum / jnp.maximum(deg, 1.0)[:, None]
            return nbr_mean @ w_l.T + x @ w_r.T + b
        h = _sage_conv(node_features, edge_index, w1_l, w1_r, b1)
        h = jax.nn.relu(h)
        out = _sage_conv(h, edge_index, w2_l, w2_r, b2)
        return out

    def _L1_gnn_ref(x, W, attn_src, attn_dst, edge_index, edge_type):
        import jax, jax.numpy as jnp
        import numpy as np
        N, E, R, H, D = (3750, 37500, 8, 8, 32)
        IN_F = 256
        NEG_SLOPE = 0.2
        n = x.shape[0]
        r = W.shape[0]
        h, d = attn_src.shape
        h_all = jnp.einsum('nf,rof->rno', x, W).reshape(r, n, h, d)
        src, dst = (edge_index[0], edge_index[1])
        h_src = h_all[edge_type, src]
        h_dst = h_all[edge_type, dst]
        scores = jnp.einsum('ehd,hd->eh', h_src, attn_src) + jnp.einsum('ehd,hd->eh', h_dst, attn_dst)
        scores = jnp.where(scores > 0, scores, NEG_SLOPE * scores)
        amax = jnp.maximum(jax.ops.segment_max(scores, dst, num_segments=n), 0.0)
        w = jnp.exp(scores - amax[dst])
        denom = jax.ops.segment_sum(w, dst, num_segments=n) + 1e-12
        w = w / denom[dst]
        msg = h_src * w[..., None]
        out = jax.ops.segment_sum(msg, dst, num_segments=n)
        return out.reshape(n, h * d)

    def _L2_gnn_ref(x, edge_index, rel, weight, bias, alpha):
        import jax, jax.numpy as jnp
        import numpy as np
        N = 12500
        E = 400000
        D_IN = 256
        D_OUT = 256
        NUM_REL = 10
        w = alpha[rel, 0]
        support = x @ weight
        row, col = (edge_index[0], edge_index[1])
        out = jax.ops.segment_sum(w[:, None] * support[col], row, num_segments=x.shape[0])
        out = out + jax.ops.segment_sum(w[:, None] * support[row], col, num_segments=x.shape[0])
        return out + bias

    def _L3_gnn_ref(feat, src, dst, W, attn_l, attn_r, gat_bias, lin_W, lin_b):
        import jax, jax.numpy as jnp
        import numpy as np
        N_NODES = 12500
        N_EDGES = 200000
        IN_DIM = 256
        HID = 64
        HEADS = 2
        OUT_DIM = 256
        NEG_SLOPE = 0.2
        N = feat.shape[0]
        H, D = attn_l.shape
        h = (feat @ W).reshape(N, H, D)
        el = jnp.sum(h * attn_l[None], axis=-1)
        er = jnp.sum(h * attn_r[None], axis=-1)
        e = jax.nn.leaky_relu(el[src] + er[dst], NEG_SLOPE)
        m = jax.ops.segment_max(e, dst, num_segments=N)
        ee = jnp.exp(e - m[dst])
        s = jax.ops.segment_sum(ee, dst, num_segments=N)
        alpha = ee / s[dst]
        out = jax.ops.segment_sum(alpha[:, :, None] * h[src], dst, num_segments=N)
        out = out + gat_bias.reshape(1, H, D)
        out = jax.nn.relu(out.reshape(N, H * D))
        return jax.nn.relu(out @ lin_W + lin_b)
    edge_index = jnp.stack([src, dst])
    h = jnp.maximum(_layernorm(x, axis=-1), 0.0)
    x = x + _L0_gnn_ref(h, L0_gnn_w1_l, L0_gnn_w1_r, L0_gnn_b1, L0_gnn_w2_l, L0_gnn_w2_r, L0_gnn_b2, edge_index)
    h = jnp.maximum(_layernorm(x, axis=-1), 0.0)
    x = x + _L1_gnn_ref(h, L1_gnn_W, L1_gnn_attn_src, L1_gnn_attn_dst, edge_index, edge_type_8)
    h = jnp.maximum(_layernorm(x, axis=-1), 0.0)
    x = x + _L2_gnn_ref(h, edge_index, edge_type_11, L2_gnn_weight, L2_gnn_bias, L2_gnn_alpha)
    h = jnp.maximum(_layernorm(x, axis=-1), 0.0)
    x = x + _L3_gnn_ref(h, src, dst, L3_gnn_W, L3_gnn_attn_l, L3_gnn_attn_r, L3_gnn_gat_bias, L3_gnn_lin_W, L3_gnn_lin_b)
    return x

_drawn_inputs = setup_inputs


def setup_inputs(seed=0):
    import zlib

    import numpy as np

    out = dict(_drawn_inputs(seed))
    spreads = {'L0_gnn_b1': (0.0, 0.1),
     'L0_gnn_b2': (0.0, 0.1),
     'L3_gnn_gat_bias': (0.0, 0.8),
     'L3_gnn_lin_b': (0.0, 0.686)}
    factors = {'L1_gnn_attn_src': 2.861,
     'L1_gnn_attn_dst': 3.577,
     'L2_gnn_bias': 8.0,
     'L3_gnn_W': 3.541,
     'L3_gnn_attn_l': 8.0,
     'L3_gnn_attn_r': 8.0,
     'L3_gnn_lin_W': 2.897}
    for name, (base, spread) in spreads.items():
        noise = np.random.default_rng([zlib.crc32(name.encode()), seed]).standard_normal(out[name].shape)
        drawn = base * np.exp(spread * noise) if base else spread * noise
        out[name] = jnp.asarray(drawn.astype(out[name].dtype))
    for name, factor in factors.items():
        out[name] = (out[name] * factor).astype(out[name].dtype)
    return out
```

```python
import math
from contextlib import ExitStack, contextmanager

import concourse.bass as bass
from concourse import mybir

F32 = mybir.dt.float32
BF16 = mybir.dt.bfloat16
I32 = mybir.dt.int32
ALU = mybir.AluOpType
ACT = mybir.ActivationFunctionType
AX_X = mybir.AxisListType.X

P = 128
N, D, E = 6250, 256, 100000
NB = -(-N // P)
NPAD = NB * P
LAST = N - (NB - 1) * P
EC = E // P
EREST = E - EC * P
CE = EC + 1
G = 8
RING = 2 * G
T = -(-(E // P + NB) // RING) * RING
NIT = T // RING
U = 7
NI = NB // U
R8, H1, D1 = 8, 8, 32
R11 = 11
H3, D3 = 2, 64
F3 = H3 * D3
ACCW = D + H1
NEG = 1e30
EPS = 1e-5
SCAT_HALVES = ((0, 6), (6, 11))
SG = 11
NSG = EC // SG


class Box:

    def __init__(self, nc, tag):
        self.nc, self.tag, self.stack, self.sems = nc, tag, ExitStack(), []

    def __enter__(self):
        return self

    def __exit__(self, *a):
        if self.sems and a[0] is None:
            self.nc.clear_and_free_semaphores(self.sems)
            self.nc.all_engine_barrier()
        return self.stack.__exit__(*a)

    def sb(self, name, shape, dt=F32):
        return self.stack.enter_context(self.nc.sbuf_tensor(f"{self.tag}_{name}", shape, dt))

    def ps(self, name, shape, dt=F32):
        return self.stack.enter_context(self.nc.psum_tensor(f"{self.tag}_{name}", shape, dt))

    def sem(self, name):
        self.sems.append(self.nc.alloc_semaphore(f"{self.tag}_{name}"))
        return self.sems[-1]


def setup_constants(nc, box, c):
    c.iota = box.sb("iota", [P, P])
    c.ident = box.sb("ident", [P, P])
    c.identb = box.sb("identb", [P, P], BF16)
    c.below = box.sb("below", [P, P])
    c.upto = box.sb("upto", [P, P])
    c.ones = box.sb("ones", [P, P])
    diff = box.sb("diff", [P, P])
    made = box.sem("indices_made")
    with nc.Block() as block:

        @block.gpsimd
        def _(pool):
            pool.iota(c.iota[:, :], pattern=[[1, P]], base=0, channel_multiplier=0,
                      allow_small_or_imprecise_dtypes=True).then_inc(made, 1)
            pool.iota(diff[:, :], pattern=[[1, P]], base=0, channel_multiplier=-1,
                      allow_small_or_imprecise_dtypes=True).then_inc(made, 1)

        @block.vector
        def _(dve):
            nc.vector.memset(c.ones[:, :], 1.0)
            dve.wait_ge(made, 2)
            nc.vector.tensor_scalar(c.ident[:, :], diff[:, :], 0.0, None, ALU.is_equal)
            nc.vector.tensor_scalar(c.identb[:, :], diff[:, :], 0.0, None, ALU.is_equal)
            nc.vector.tensor_scalar(c.below[:, :], diff[:, :], 0.0, None, ALU.is_gt)
            nc.vector.tensor_scalar(c.upto[:, :], diff[:, :], 0.0, None, ALU.is_ge)


def sort_edges(nc, tag, c, key_d, other_d, t8_d, t11_d, alpha_d, rec_d, out):
    with Box(nc, tag) as box:
        key = box.sb("key", [P, CE], I32)
        bucket_i = box.sb("bucket_i", [P, CE], I32)
        bucket = box.sb("bucket", [P, CE])
        rec = box.sb("rec", [P, CE, 4], I32)
        pads = box.sb("pads", [P, T, 4], I32)
        onesw = box.sb("onesw", [P, CE], BF16)
        match = box.sb("match", [P, CE])
        run = box.sb("run", [P, CE])
        pos = box.sb("pos", [P, CE])
        posi = box.sb("posi", [P, CE], I32)
        slot_t = box.sb("slot_t", [P, CE], I32)
        addr = box.sb("addr", [P, CE], I32)
        cnt = box.sb("cnt", [P, NB])
        tot_i = box.sb("tot_i", [P, NB], I32)
        tiles = box.sb("tiles", [P, NB])
        ends = box.sb("ends", [P, NB])
        start = box.sb("start", [P, NB])
        nT_i = box.sb("nT_i", [NB, 1], I32)
        nT = box.sb("nT", [NB, 1])
        endT = box.sb("endT", [NB, 1])
        tile_no = box.sb("tile_no", [NB, T])
        after = box.sb("after", [NB, T])
        alpha = box.sb("alpha", [P, R11])
        scratch = box.sb("scratch", [P, T])
        rec_ring = box.sb("rec_ring", [P, SG, 4], I32)
        addr_ring = box.sb("addr_ring", [P, SG], I32)
        ps_tot = box.ps("ps_tot", [P, 512])[:, 0:NB]
        ps_low = box.ps("ps_low", [P, 512])[:, 0:NB]
        ps_nT = box.ps("ps_nT", [P, 512])[0:NB, 0:1]
        ps_end = box.ps("ps_end", [P, 512])[0:NB, 0:1]
        ps_bk = box.ps("ps_bk", [P, 512])[0:1, 0:T // 2]
        ps_bk2 = box.ps("ps_bk2", [P, 512])[0:1, 0:T // 2]
        filled, loaded, padded, counted, summed, nt_ready, end_summed, after_ready, bk_summed, iota_made = (
            box.sem(x) for x in ("filled", "loaded", "padded", "counted", "summed", "nt_ready",
                                 "end_summed", "after_ready", "bk_summed", "iota_made"))
        placed, ring_full, reloaded = box.sem("placed"), box.sem("ring_full"), box.sem("reloaded")
        scattered = [box.sem(f"scattered{h}") for h in range(2)]
        last_out, held = box.sem("last_out"), box.sem("held")
        with nc.Block() as block:

            @block.sync
            def _(sp):
                sp.wait_ge(filled, 1)
                sources = ((key_d, key[:, :]), (other_d, posi[:, :]), (t8_d, slot_t[:, :]), (t11_d, addr[:, :]))
                for d, s in sources:
                    sp.dma_start(s[:, 0:EC], d[0:EC * P].rearrange("(p c) -> p c", p=P)).then_inc(loaded, 16)
                    sp.dma_start(s[0:EREST, EC:CE], d[EC * P:E].rearrange("(p c) -> p c", c=1)).then_inc(loaded, 16)
                sp.dma_start(alpha[:, :], alpha_d.rearrange("r o -> o r").broadcast_to([P, R11])).then_inc(loaded, 16)
                sp.dma_start(rec_d.rearrange("(p t) f -> p t f", p=P), pads[:, :, :]).then_inc(padded, 16)
                for h, (a, b) in enumerate(SCAT_HALVES):
                    sp.wait_ge(scattered[h], 16 * (b - a) * NSG)
                sp.wait_ge(last_out, 16)
                sp.dma_start(pads[:, :, :], rec_d.rearrange("(p t) f -> p t f", p=P)).then_inc(reloaded, 16)

            @block.gpsimd
            def _(pool):
                pool.iota(tile_no[:, :], pattern=[[1, T]], base=0, channel_multiplier=0,
                          allow_small_or_imprecise_dtypes=True).then_inc(iota_made, 1)
                pool.wait_ge(padded, 16)
                with nc.gpsimd.Fori(0, NSG) as g:
                    for h, (a, b) in enumerate(SCAT_HALVES):
                        hold(pool, ring_full, g * 2 + (h + 1), held)
                        for u in range(a, b):
                            pool.indirect_dma_start(
                                out=rec_d, out_offset=bass.IndirectOffsetOnAxis(ap=addr_ring[:, u:u + 1], axis=0),
                                in_=rec_ring[:, u, :], in_offset=None).then_inc(scattered[h], 16)
                pool.indirect_dma_start(
                    out=rec_d, out_offset=bass.IndirectOffsetOnAxis(ap=addr[0:EREST, EC:CE], axis=0),
                    in_=rec[0:EREST, EC, :], in_offset=None).then_inc(last_out, 16)

            @block.scalar
            def _(act):
                act.wait_ge(placed, 1)

                def stage(g, a, b):
                    nc.scalar.copy(rec_ring[:, a:b, :].rearrange("p c f -> p (c f)"),
                                   rec[:, :, :].rearrange("p c f -> p (c f)")[:, bass.ds((g * SG + a) * 4, (b - a) * 4)])
                    nc.scalar.copy(addr_ring[:, a:b], addr[:, bass.ds(g * SG + a, b - a)])
                    act.drain().then_inc(ring_full, 1)

                for a, b in SCAT_HALVES:
                    stage(0, a, b)
                with nc.scalar.Fori(0, NSG - 1) as g:
                    for h, (a, b) in enumerate(SCAT_HALVES):
                        act.wait_ge(scattered[h], g * (16 * (b - a)) + 16 * (b - a))
                        stage(g + 1, a, b)

            @block.tensor
            def _(pe):
                pe.wait_ge(counted, 1)
                nc.tensor.matmul(ps_tot[:, :], c.ones[:, :], cnt[:, :], start=True, stop=True)
                nc.tensor.matmul(ps_low[:, :], c.below[:, :], cnt[:, :], start=True, stop=True)
                nc.tensor.matmul(ps_nT[:, :], cnt[:, :], c.ones[:, 0:1], start=True, stop=True).then_inc(summed, 1)
                pe.wait_ge(nt_ready, 1)
                nc.tensor.matmul(ps_end[:, :], c.upto[0:NB, 0:NB], nT[:, :], start=True, stop=True).then_inc(end_summed, 1)
                pe.wait_ge(after_ready, 1)
                nc.tensor.matmul(ps_bk[:, :], c.ones[0:NB, 0:1], after[:, 0:T // 2], start=True, stop=True)
                nc.tensor.matmul(ps_bk2[:, :], c.ones[0:NB, 0:1], after[:, T // 2:T], start=True, stop=True).then_inc(bk_summed, 1)

            @block.vector
            def _(dve):
                nc.vector.memset(key[:, EC:CE], P * (P - 1))
                nc.vector.memset(posi[:, EC:CE], 0)
                nc.vector.memset(slot_t[:, EC:CE], 0)
                nc.vector.memset(addr[:, EC:CE], 0)
                nc.vector.memset(pads[:, :, :], 0)
                dve.drain()
                nc.vector.memset(pads[:, :, 1:2], -1)
                nc.vector.memset(onesw[:, :], 1.0)
                nc.vector.memset(pos[:, :], 0.0)
                dve.drain().then_inc(filled, 1)
                dve.wait_ge(loaded, 16 * 9)
                nc.vector.tensor_scalar(bucket_i[:, :], key[:, :], 7, None, ALU.arith_shift_right)
                nc.vector.tensor_copy(rec[:, :, 0], posi[:, :])
                nc.vector.tensor_scalar(rec[:, :, 1], key[:, :], P - 1, None, ALU.bitwise_and)
                nc.vector.tensor_copy(rec[:, :, 2], slot_t[:, :])
                nc.vector.tensor_copy(rec[:, :, 3], addr[:, :])
                dve.drain()
                nc.vector.tensor_copy(bucket[:, :], bucket_i[:, :])
                dve.drain()
                with nc.vector.Fori(0, NB) as b:
                    nc.vector.tensor_scalar(match[:, :], bucket[:, :], c.iota[:, bass.ds(b, 1)], 0.0,
                                            ALU.is_equal, ALU.add, accum_out=cnt[:, bass.ds(b, 1)])
                    dve.drain()
                dve.drain().then_inc(counted, 1)
                dve.wait_ge(summed, 1)
                nc.vector.tensor_scalar(tot_i[:, :], ps_tot[:, :], float(P - 1), None, ALU.add)
                nc.vector.tensor_scalar(nT_i[:, :], ps_nT[:, :], float(P - 1), None, ALU.add)
                dve.drain()
                nc.vector.tensor_scalar(tot_i[:, :], tot_i[:, :], 7, None, ALU.arith_shift_right)
                nc.vector.tensor_scalar(nT_i[:, :], nT_i[:, :], 7, None, ALU.arith_shift_right)
                dve.drain()
                nc.vector.tensor_copy(tiles[:, :], tot_i[:, :])
                nc.vector.tensor_copy(nT[:, :], nT_i[:, :])
                dve.drain().then_inc(nt_ready, 1)
                nc.vector.tensor_tensor_scan(ends[:, :], onesw[:, 0:NB], tiles[:, :], 0.0, ALU.mult, ALU.add)
                dve.drain()
                nc.vector.tensor_tensor(start[:, :], ends[:, :], tiles[:, :], ALU.subtract)
                dve.drain()
                nc.vector.tensor_scalar(start[:, :], start[:, :], float(P), -1.0, ALU.mult, ALU.add)
                dve.drain()
                nc.vector.tensor_tensor(start[:, :], start[:, :], ps_low[:, :], ALU.add)
                dve.drain()
                with nc.vector.Fori(0, NB) as b:
                    nc.vector.tensor_scalar(match[:, :], bucket[:, :], c.iota[:, bass.ds(b, 1)], None, ALU.is_equal)
                    dve.drain()
                    nc.vector.tensor_tensor_scan(run[:, :], onesw[:, :], match[:, :], start[:, bass.ds(b, 1)],
                                                 ALU.mult, ALU.add)
                    dve.drain()
                    nc.vector.copy_predicated(pos[:, :], match[:, :].bitcast(I32), run[:, :])
                    dve.drain()
                nc.vector.tensor_copy(posi[:, :], pos[:, :])
                dve.drain()
                nc.vector.tensor_scalar(slot_t[:, :], posi[:, :], 7, None, ALU.arith_shift_right)
                nc.vector.tensor_scalar(posi[:, :], posi[:, :], P - 1, None, ALU.bitwise_and)
                dve.drain()
                nc.vector.scalar_tensor_tensor(out=addr[:, :], in0=posi[:, :], scalar=float(T), in1=slot_t[:, :],
                                               op0=ALU.mult, op1=ALU.add)
                dve.drain().then_inc(placed, 1)
                dve.wait_ge(end_summed, 1)
                nc.vector.tensor_copy(endT[:, :], ps_end[:, :])
                dve.wait_ge(iota_made, 1)
                dve.drain()
                nc.vector.tensor_scalar(after[:, :], tile_no[:, :], endT[:, :], None, ALU.is_ge)
                nc.vector.memset(out.tile_bucket[:, :], 0)
                dve.drain().then_inc(after_ready, 1)
                dve.wait_ge(bk_summed, 1)
                nc.vector.tensor_scalar(out.tile_bucket[:, 0:T // 2], ps_bk[:, :], float(NB - 1), None, ALU.min)
                nc.vector.tensor_scalar(out.tile_bucket[:, T // 2:T], ps_bk2[:, :], float(NB - 1), None, ALU.min)
                dve.wait_ge(reloaded, 16)
                nc.vector.memset(out.local[:, T:T + G], -1.0)
                nc.vector.memset(out.other[:, T:], 0)
                nc.vector.tensor_copy(out.other[:, 0:T], pads[:, :, 0])
                nc.vector.tensor_copy(out.local[:, 0:T], pads[:, :, 1])
                nc.vector.memset(out.weight[:, :], 0.0)
                if out.rel_other is not None:
                    nc.vector.scalar_tensor_tensor(out=out.rel_other[:, 0:T], in0=pads[:, :, 0], scalar=float(R8),
                                                   in1=pads[:, :, 2], op0=ALU.mult, op1=ALU.add)
                    nc.vector.memset(out.rel_other[:, T:], 0)
                    nc.vector.memset(out.type8[:, T:T + G], 0.0)
                    nc.vector.tensor_copy(out.type8[:, 0:T], pads[:, :, 2])
                dve.drain()
                for r in range(R11):
                    nc.vector.tensor_scalar(scratch[:, :], pads[:, :, 3], float(r), alpha[:, r:r + 1],
                                            ALU.is_equal, ALU.mult)
                    dve.drain()
                    nc.vector.tensor_tensor(out.weight[:, 0:T], out.weight[:, 0:T], scratch[:, :], ALU.add)
                    dve.drain()


def wait_past(eng, sem, count):
    if not isinstance(count, int) or count > 0:
        eng.wait_ge(sem, count)


def hold(pool, sem, count, held):
    pool.wait_ge(sem, count)
    pool.sem_inc(held, 1)


class Order:
    pass


class Consts:
    pass


def gather_sum(nc, tag, c, order, index, table, acc, width, weighted=False, count=False, clear=True):
    cols = width + (1 if count else 0)
    with Box(nc, tag) as box:
        rows = box.sb("rows", [P, RING, ACCW])
        hot = box.sb("hot", [P, RING, P])
        idx = box.sb("idx", [P, RING], I32)
        part = [box.ps(f"part{k}", [P, 512]) for k in range(4)]
        ready = box.sem("ready")
        staged = box.sem("indices_staged")
        held = box.sem("held")
        landed = [box.sem(f"rows_landed{h}") for h in range(2)]
        hot_made = box.sem("hot_made")
        summed = box.sem("tiles_summed")
        added = box.sem("parts_added")
        with nc.Block() as block:

            @block.gpsimd
            def _(pool):
                pool.wait_ge(ready, 1)
                with nc.gpsimd.Fori(0, NIT) as g:
                    for h in range(2):
                        pool.wait_ge(staged, g * 2 + (h + 1))
                        for u in range(h * G, h * G + G):
                            hold(pool, summed, g * RING + (u + 1), held)
                            pool.indirect_dma_start(
                                out=rows[:, u, 0:width], out_offset=None, in_=table,
                                in_offset=bass.IndirectOffsetOnAxis(ap=idx[:, u:u + 1], axis=0)).then_inc(landed[h], 16)

            @block.scalar
            def _(act):
                with nc.scalar.Fori(0, NIT) as g:
                    for h in range(2):
                        act.wait_ge(summed, g * RING + (h + 1) * G)
                        nc.scalar.copy(idx[:, h * G:h * G + G],
                                       index[:, bass.ds(g * RING + h * G, G)]).then_inc(staged, 1)

            @block.tensor
            def _(pe):
                pe.sem_inc(summed, RING)
                with nc.tensor.Fori(0, NIT) as g:
                    for u in range(RING):
                        if u % G == 0:
                            pe.wait_ge(landed[u // G], g * (16 * G) + 16 * G)
                        pe.wait_ge(hot_made, g * RING + (u + 1))
                        pe.wait_ge(added, g * RING + (u + 1))
                        nc.tensor.matmul(part[u % 4][:, 0:cols], hot[:, u, :], rows[:, u, 0:cols],
                                         start=True, stop=True).then_inc(summed, 1)

            @block.vector
            def _(dve):
                if clear:
                    nc.vector.memset(acc[:, :, :], 0.0)
                if count:
                    nc.vector.memset(rows[:, :, width:width + 1], 1.0)
                dve.drain().then_inc(ready, 1)
                dve.sem_inc(added, 4)

                def one_hots(tile0, h):
                    for u in range(h * G, h * G + G):
                        t = tile0 + (u - h * G)
                        nc.vector.tensor_scalar(hot[:, u, :], c.iota[:, :], order.local[:, bass.ds(t, 1)],
                                                order.weight[:, bass.ds(t, 1)] if weighted else None,
                                                ALU.is_equal, ALU.mult if weighted else ALU.bypass).then_inc(hot_made, 1)

                one_hots(0, 0)
                with nc.vector.Fori(0, NIT) as g:
                    for h in range(2):
                        dve.wait_ge(summed, g * RING + (h + 2) * G)
                        one_hots(g * RING + (h + 1) * G, 1 - h)
                        for u in range(h * G, h * G + G):
                            bucket = dve.value_load(order.tile_bucket[0:1, bass.ds(g * RING + u, 1)], min_val=0, max_val=NB - 1)
                            dve.wait_ge(summed, g * RING + (RING + u + 1))
                            dve.wait_ge(added, g * RING + (u + 4))
                            a = acc[:, bass.ds(bucket, 1), 0:cols].rearrange("p o c -> p (o c)")
                            nc.vector.tensor_tensor(a, a, part[u % 4][:, 0:cols], ALU.add).then_inc(added, 1)


def normalize(nc, tag, c, x, h, table_d):
    with Box(nc, tag) as box:
        stats = box.sb("stats", [P, NB, 6])
        mv = box.sb("mv", [P, NB, 2])
        rstd = box.sb("rstd", [P, NB])
        shift = box.sb("shift", [P, NB])
        var_ready, std_ready, scale_ready, made, stored = (
            box.sem(n) for n in ("var_ready", "std_ready", "scale_ready", "made", "stored"))
        with nc.Block() as block:

            @block.vector
            def _(dve):
                with nc.vector.Fori(0, NI) as i:
                    for u in range(U):
                        nc.vector.bn_stats(stats[:, bass.ds(i * U + u, 1), :].rearrange("p o s -> p (o s)"),
                                           x[:, bass.ds(i * U + u, 1), :].rearrange("p o d -> p (o d)"))
                dve.drain()
                for b in range(NB):
                    nc.vector.bn_aggr(mv[:, b, :], stats[:, b, :])
                dve.drain()
                nc.vector.tensor_scalar(rstd[:, :], mv[:, :, 1], EPS, None, ALU.add)
                dve.drain().then_inc(var_ready, 1)
                dve.wait_ge(std_ready, 1)
                nc.vector.reciprocal(rstd[:, :], rstd[:, :])
                dve.drain()
                nc.vector.scalar_tensor_tensor(out=shift[:, :], in0=mv[:, :, 0], scalar=-1.0, in1=rstd[:, :],
                                               op0=ALU.mult, op1=ALU.mult)
                dve.drain().then_inc(scale_ready, 1)

            @block.scalar
            def _(act):
                act.wait_ge(var_ready, 1)
                nc.scalar.activation(rstd[:, :], rstd[:, :], ACT.Sqrt)
                act.drain().then_inc(std_ready, 1)
                act.wait_ge(scale_ready, 1)
                with nc.scalar.Fori(0, NI) as i:
                    for u in range(U):
                        b = i * U + u
                        nc.scalar.activation(h[:, bass.ds(b, 1), 0:D].rearrange("p o d -> p (o d)"),
                                             x[:, bass.ds(b, 1), :].rearrange("p o d -> p (o d)"),
                                             ACT.Relu, bias=shift[:, bass.ds(b, 1)],
                                             scale=rstd[:, bass.ds(b, 1)]).then_inc(made, 1)

            @block.sync
            def _(sp):
                if table_d is not None:
                    table = table_d.rearrange("(b p) d -> p b d", p=P)
                    for i in range(NI):
                        sp.wait_ge(made, (i + 1) * U)
                        sp.dma_start(table[:, i * U:(i + 1) * U, :], h[:, i * U:(i + 1) * U, :]).then_inc(stored, 16)
                    sp.wait_ge(stored, 16 * NI)


def transpose_weights(nc, tag, c, pairs, raw=None):
    with Box(nc, tag) as box:
        raw = raw or [box.sb(f"raw{k}", [P, w_d.shape[0] // P, w_d.shape[1]]) for k, (w_d, _) in enumerate(pairs)]
        turned = [box.ps(f"turned{k}", [P, 512]) for k in range(2)]
        loaded, turns, copied = box.sem("loaded"), box.sem("turned"), box.sem("copied")
        blocks = [(raw[k][:, oc, fc * P:(fc + 1) * P], wT[:, fc, oc * P:(oc + 1) * P])
                  for k, (w_d, wT) in enumerate(pairs)
                  for fc in range(w_d.shape[1] // P) for oc in range(w_d.shape[0] // P)]
        with nc.Block() as block:

            @block.sync
            def _(sp):
                for k, (w_d, _) in enumerate(pairs):
                    sp.dma_start(raw[k][:, :, :], w_d.rearrange("(c p) f -> p c f", p=P)).then_inc(loaded, 16)

            @block.tensor
            def _(pe):
                pe.wait_ge(loaded, 16 * len(pairs))
                for n, (src, _) in enumerate(blocks):
                    if n >= 2:
                        pe.wait_ge(copied, n - 1)
                    nc.tensor.transpose(turned[n % 2][:, 0:P], src, c.ident[:, :]).then_inc(turns, 1)

            @block.vector
            def _(dve):
                for n, (_, dst) in enumerate(blocks):
                    dve.wait_ge(turns, n + 1)
                    nc.vector.tensor_copy(dst, turned[n % 2][:, 0:P]).then_inc(copied, 1)


def project(nc, tag, c, sources, weights, cols, finish, before=None, load=None):
    chunks = sum(n for _, n, _ in sources)
    with Box(nc, tag) as box:
        stage = box.sb("stage", [P, 4, chunks * P])
        turned_sb = box.sb("turned_sb", [P, 4, chunks * P])
        turned = [box.ps(f"turned{k}", [P, 512]) for k in range(2)]
        result = [box.ps(f"result{k}", [P, 512]) for k in range(2)]
        ready, staged, turns, copied, product, finished, got = (
            box.sem(n) for n in ("ready", "staged", "turned", "copied", "product", "finished", "got"))
        with nc.Block() as block:

            @block.sync
            def _(sp):
                for dst, src in load or []:
                    sp.dma_start(dst, src).then_inc(got, 16)

            @block.scalar
            def _(act):
                act.wait_ge(ready, 1)
                with nc.scalar.Fori(0, NI) as i:
                    for u in range(U):
                        b = i * U + u
                        act.wait_ge(copied, b + (U - 2))
                        at = 0
                        for k, (src, n, scale) in enumerate(sources):
                            a = src[:, bass.ds(b, 1), 0:n * P].rearrange("p o d -> p (o d)")
                            last = nc.scalar.activation(stage[:, u % 4, at:at + n * P], a, ACT.Copy,
                                                        scale=1.0 if scale is None else scale[:, bass.ds(b, 1)])
                            last.then_inc(staged, 1)
                            at += n * P

            @block.tensor
            def _(pe):
                def turn(b, u):
                    pe.wait_ge(staged, b * len(sources) + len(sources))
                    pe.wait_ge(copied, b + (U if u == 0 else U - 1))
                    for k in range(chunks):
                        last = nc.tensor.transpose(turned[u % 2][:, k * P:(k + 1) * P],
                                                   stage[:, u % 4, k * P:(k + 1) * P], c.ident[:, :])
                    last.then_inc(turns, 1)

                pe.wait_ge(ready, 1)
                with nc.tensor.Fori(0, NI) as i:
                    turn(i * U, 0)
                    for u in range(U):
                        b = i * U + u
                        if u + 1 < U:
                            turn(b + 1, u + 1)
                        pe.wait_ge(copied, b + U + 1)
                        pe.wait_ge(finished, b + (2 if u == 0 else 1))
                        for k in range(chunks):
                            last = nc.tensor.matmul(result[u % 2][:, 0:cols], turned_sb[:, u % 4, k * P:(k + 1) * P],
                                                    weights[k], start=(k == 0), stop=(k == chunks - 1))
                        last.then_inc(product, 1)

            @block.vector
            def _(dve):
                if load:
                    dve.wait_ge(got, 16 * len(load))
                if before:
                    before(dve)
                dve.sem_inc(copied, U)
                dve.sem_inc(finished, 2)
                dve.drain().then_inc(ready, 1)

                def copy_turned(b, u):
                    dve.wait_ge(turns, b + 1)
                    nc.vector.tensor_copy(turned_sb[:, u % 4, :], turned[u % 2][:, 0:chunks * P]).then_inc(copied, 1)

                with nc.vector.Fori(0, NI) as i:
                    copy_turned(i * U, 0)
                    for u in range(U):
                        b = i * U + u
                        if u + 1 < U:
                            copy_turned(b + 1, u + 1)
                        dve.wait_ge(product, b + 1)
                        finish(dve, b, result[u % 2][:, 0:cols]).then_inc(finished, 1)


def flat(ap):
    return ap.rearrange("p o d -> p (o d)")


def attention_max(nc, tag, c, order, index, table, H, R, dst_scores, score, top):
    with Box(nc, tag) as box:
        src = box.sb("src", [P, RING, H])
        hot = box.sb("hot", [P, RING, P])
        hotT = box.sb("hotT", [P, G, P])
        other = box.sb("other", [P, RING, P], BF16)
        typed = box.sb("typed", [P, G, R])
        picked = box.sb("picked", [P, G, R, H])
        s = box.sb("s", [P, G, H])
        rest = box.sb("rest", [P, G, H])
        parts = box.sb("parts", [P, G, 3, H], BF16)
        partsT = box.sb("partsT", [3 * H, G * P], BF16)
        sel_v, sel_a = hot[0:3 * H, 0:H, :], hot[0:3 * H, H:2 * H, :]
        sel = box.sb("sel", [3 * H, H, P], BF16)
        tile_top = box.sb("tile_top", [P, G, H])
        idx = box.sb("idx", [P, RING], I32)
        ps_hot = box.ps("ps_hot", [P, 512])
        ps_dst = box.ps("ps_dst", [P, 512])
        ps_parts = box.ps("ps_parts", [P, G * P], BF16)[0:3 * H, :]
        big = [box.ps(f"big{k}", [P, H * P]) for k in range(2)]
        names = ("ready", "staged", "hot_made", "hot_turned", "hot_copied", "dst_spread", "scored", "parts_turned",
                 "parts_copied", "masked", "reduced", "topped", "sel_index")
        (ready, staged, hot_made, hot_turned, hot_copied, dst_spread, scored, parts_turned, parts_copied,
         masked, reduced, topped, sel_index) = (box.sem(n) for n in names)
        held = box.sem("held")
        landed = [box.sem(f"landed{h}") for h in range(2)]
        with nc.Block() as block:

            @block.gpsimd
            def _(pool):
                pool.iota(sel_v, pattern=[[-1, H], [0, P]], base=0,
                          channel_multiplier=1, allow_small_or_imprecise_dtypes=True).then_inc(sel_index, 1)
                pool.wait_ge(ready, 1)
                with nc.gpsimd.Fori(0, NIT) as g:
                    for h in range(2):
                        pool.wait_ge(staged, g * 2 + (h + 1))
                        hold(pool, scored, g * 2 + (h + 1), held)
                        for u in range(h * G, h * G + G):
                            pool.indirect_dma_start(
                                out=src[:, u, :], out_offset=None, in_=table,
                                in_offset=bass.IndirectOffsetOnAxis(ap=idx[:, u:u + 1], axis=0)).then_inc(landed[h], 16)
                pool.wait_ge(staged, 2 * NIT + 1)
                pool.wait_ge(scored, 2 * NIT + 1)
                for u in range(G):
                    pool.indirect_dma_start(
                        out=src[:, u, :], out_offset=None, in_=table,
                        in_offset=bass.IndirectOffsetOnAxis(ap=idx[:, u:u + 1], axis=0)).then_inc(landed[0], 16)

            @block.scalar
            def _(act):
                act.wait_ge(ready, 1)

                def stage_indices(g, h):
                    act.wait_ge(scored, g * 2 + (h + 1))
                    nc.scalar.copy(idx[:, h * G:h * G + G], index[:, bass.ds(g * RING + h * G, G)]).then_inc(staged, 1)

                def copy_hots(k, h):
                    for q in range(2):
                        act.wait_ge(hot_turned, k * 2 + (q + 1))
                        act.wait_ge(dst_spread, k * 2 + (q + 1))
                        nc.scalar.copy(hotT[:, q * 4:q * 4 + 4, :].rearrange("p u e -> p (u e)"), ps_hot[:, :])
                        u = h * G + q * 4
                        act.wait_ge(masked, k * G + (q * 4 + 4))
                        nc.scalar.activation(other[:, u:u + 4, :].rearrange("p u e -> p (u e)"), ps_hot[:, :],
                                             ACT.Copy, scale=NEG, bias=-NEG)
                        act.drain().then_inc(hot_copied, 1)

                def copy_parts(k):
                    act.wait_ge(parts_turned, k + 1)
                    nc.scalar.copy(partsT[:, :], ps_parts[:, :]).then_inc(parts_copied, 1)

                stage_indices(0, 0)
                stage_indices(0, 1)
                copy_hots(0, 0)
                copy_parts(0)
                with nc.scalar.Fori(0, NIT) as g:
                    for h in range(2):
                        copy_hots(g * 2 + (h + 1), 1 - h)
                        copy_parts(g * 2 + (h + 1))
                        act.wait_ge(scored, g * 2 + (h + 3))
                        last = nc.scalar.copy(idx[:, h * G:h * G + G],
                                              index[:, bass.ds((g + 1) * RING + h * G, G)])
                        last.then_inc(staged, 1)

            @block.tensor
            def _(pe):
                pe.wait_ge(ready, 1)
                pe.sem_inc(dst_spread, 2)
                pe.sem_inc(masked, RING)

                def spread(k, h):
                    for q in range(2):
                        wait_past(pe, hot_copied, k * 2 + q)
                        for u in range(4 * q, 4 * q + 4):
                            pe.wait_ge(hot_made, k * G + (u + 1))
                            last = nc.tensor.transpose(ps_hot[:, (u % 4) * P:(u % 4 + 1) * P], hot[:, h * G + u, :],
                                                       c.ident[:, :])
                        last.then_inc(hot_turned, 1)
                        pe.wait_ge(hot_copied, k * 2 + (q + 1))
                        if q == 0:
                            pe.wait_ge(scored, k + 2)
                        for u in range(4 * q, 4 * q + 4):
                            b = pe.value_load(order.tile_bucket[0:1, bass.ds(k * G + u, 1)], min_val=0, max_val=NB - 1)
                            last = nc.tensor.matmul(ps_dst[:, u * R * H:(u + 1) * R * H], hotT[:, u, :],
                                                    flat(dst_scores[:, bass.ds(b, 1), :]), start=True, stop=True)
                        last.then_inc(dst_spread, 1)

                def turn_parts(k):
                    pe.wait_ge(scored, k + 3)
                    wait_past(pe, parts_copied, k)
                    for u in range(G):
                        last = nc.tensor.transpose(ps_parts[:, u * P:(u + 1) * P],
                                                   parts[:, u, :, :].rearrange("p a h -> p (a h)"), c.identb[:, :])
                    last.then_inc(parts_turned, 1)

                spread(0, 0)
                turn_parts(0)
                with nc.tensor.Fori(0, NIT) as g:
                    for h in range(2):
                        k = g * 2 + h
                        spread(k + 1, 1 - h)
                        pe.wait_ge(parts_copied, k + 1)
                        for u in range(G):
                            pe.wait_ge(reduced, k * G + (u + 1))
                            m = big[u % 2]
                            for hd in range(H):
                                at = m[:, hd * P:(hd + 1) * P]
                                nc.tensor.matmul(at, c.identb[:, :], other[:, h * G + u, :], start=True, stop=False)
                                last = nc.tensor.matmul(at, sel[:, hd, :], partsT[:, u * P:(u + 1) * P],
                                                        start=False, stop=True)
                            last.then_inc(masked, 1)
                        turn_parts(k + 1)

            @block.vector
            def _(dve):
                dve.wait_ge(sel_index, 1)
                nc.vector.tensor_scalar(sel_a, sel_v, 0.0, None, ALU.is_equal)
                dve.drain()
                nc.vector.scalar_tensor_tensor(out=sel_a, in0=sel_v, scalar=float(H), in1=sel_a,
                                               op0=ALU.is_equal, op1=ALU.add)
                dve.drain()
                nc.vector.scalar_tensor_tensor(out=sel[:, :, :], in0=sel_v, scalar=float(2 * H),
                                               in1=sel_a, op0=ALU.is_equal, op1=ALU.add)
                dve.sem_inc(scored, 2)
                dve.sem_inc(reduced, 2)
                dve.sem_inc(topped, 1)
                dve.drain().then_inc(ready, 1)

                def one_hots(t0, h):
                    for u in range(G):
                        nc.vector.tensor_scalar(hot[:, h * G + u, :], c.iota[:, :], order.local[:, bass.ds(t0 + u, 1)],
                                                None, ALU.is_equal).then_inc(hot_made, 1)

                def score_half(k, h, landed_at):
                    if R > 1:
                        nc.vector.tensor_tensor(
                            typed[:, :, :], order.type8[:, bass.ds(k * G, G)].rearrange("p (u o) -> p u o", o=1).broadcast_to([P, G, R]),
                            c.iota[:, 0:R].rearrange("p (o r) -> p o r", o=1).broadcast_to([P, G, R]), ALU.is_equal)
                        dve.drain()
                    dve.wait_ge(dst_spread, k * 2 + 4)
                    if R > 1:
                        nc.vector.tensor_tensor(
                            picked[:, :, :, :], ps_dst[:, 0:G * R * H].rearrange("p (u r h) -> p u r h", u=G, r=R),
                            typed[:, :, :].rearrange("p u (r o) -> p u r o", o=1).broadcast_to([P, G, R, H]), ALU.mult)
                        dve.drain()
                        nc.vector.reduce_sum(s[:, :, :], picked[:, :, :, :].rearrange("p u r h -> p u h r"), AX_X)
                        dve.drain()
                    dve.wait_ge(landed[h], landed_at)
                    near = s[:, :, :] if R > 1 else ps_dst[:, 0:G * H].rearrange("p (u h) -> p u h", u=G)
                    nc.vector.tensor_tensor(s[:, :, :], near, src[:, h * G:h * G + G, :], ALU.add)
                    dve.drain()
                    out = score[:, bass.ds(k * G, G), :]
                    nc.vector.scalar_tensor_tensor(out=out, in0=s[:, :, :], scalar=0.2, in1=s[:, :, :],
                                                   op0=ALU.mult, op1=ALU.max)
                    dve.drain()
                    wait_past(dve, parts_turned, k)
                    nc.vector.tensor_scalar(parts[:, :, 0, :], out, 1.0, None, ALU.mult)
                    dve.drain()
                    nc.vector.tensor_tensor(rest[:, :, :], out, parts[:, :, 0, :], ALU.subtract)
                    dve.drain()
                    nc.vector.tensor_copy(parts[:, :, 1, :], rest[:, :, :])
                    dve.drain()
                    nc.vector.tensor_tensor(parts[:, :, 2, :], rest[:, :, :], parts[:, :, 1, :], ALU.subtract)
                    dve.drain().then_inc(scored, 1)

                one_hots(0, 0)
                score_half(0, 0, 16 * G)
                with nc.vector.Fori(0, NIT) as g:
                    for h in range(2):
                        k = g * 2 + h
                        one_hots((k + 1) * G, 1 - h)
                        for u in range(G):
                            dve.wait_ge(masked, k * G + (RING + u + 1))
                            nc.vector.reduce_max(tile_top[:, u, :], big[u % 2][:, :].rearrange("p (h e) -> p h e", h=H),
                                                 AX_X).then_inc(reduced, 1)
                        dve.wait_ge(reduced, k * G + (G + 2))
                        for u in range(G):
                            b = dve.value_load(order.tile_bucket[0:1, bass.ds(k * G + u, 1)], min_val=0, max_val=NB - 1)
                            dve.wait_ge(topped, k * G + (u + 1))
                            a = flat(top[:, bass.ds(b, 1), :])
                            nc.vector.tensor_tensor(a, a, tile_top[:, u, :], ALU.max).then_inc(topped, 1)
                        score_half(k + 1, 1 - h, g * (16 * G) + (16 * G * (2 if h else 1)))


def attention_sum(nc, tag, c, order, index, table, width, H, score, top, acc):
    cols = width + H
    with Box(nc, tag) as box:
        rows = box.sb("rows", [P, RING, ACCW])
        hot = box.sb("hot", [P, RING, P])
        hotT = box.sb("hotT", [P, G, P])
        below = box.sb("below", [P, 2, G, H])
        idx = box.sb("idx", [P, RING], I32)
        ps_hot = box.ps("ps_hot", [P, 512])
        ps_top = box.ps("ps_top", [P, 512])
        part = [box.ps(f"part{k}", [P, 512]) for k in range(4)]
        names = ("ready", "staged", "hot_made", "hot_turned", "hot_copied", "top_spread", "lowered", "weighed",
                 "messages", "summed", "added")
        (ready, staged, hot_made, hot_turned, hot_copied, top_spread, lowered, weighed, messages, summed,
         added) = (box.sem(n) for n in names)
        held = box.sem("held")
        landed = [box.sem(f"landed{h}") for h in range(2)]
        with nc.Block() as block:

            @block.gpsimd
            def _(pool):
                pool.wait_ge(ready, 1)
                with nc.gpsimd.Fori(0, NIT) as g:
                    for h in range(2):
                        pool.wait_ge(staged, g * 2 + (h + 1))
                        for u in range(h * G, h * G + G):
                            hold(pool, summed, g * RING + (u + 1), held)
                            pool.indirect_dma_start(
                                out=rows[:, u, 0:width], out_offset=None, in_=table,
                                in_offset=bass.IndirectOffsetOnAxis(ap=idx[:, u:u + 1], axis=0)).then_inc(landed[h], 16)

            @block.scalar
            def _(act):
                act.wait_ge(ready, 1)

                def stage_indices(k, h):
                    act.wait_ge(summed, k * G + G)
                    nc.scalar.copy(idx[:, h * G:h * G + G], index[:, bass.ds(k * G, G)]).then_inc(staged, 1)

                def weigh(k, h):
                    for q in range(2):
                        act.wait_ge(hot_turned, k * 2 + (q + 1))
                        act.wait_ge(top_spread, k * 2 + (q + 1))
                        nc.scalar.copy(hotT[:, q * 4:q * 4 + 4, :].rearrange("p u e -> p (u e)"),
                                       ps_hot[:, :]).then_inc(hot_copied, 1)
                    act.wait_ge(lowered, k + 1)
                    act.wait_ge(summed, k * G + G)
                    nc.scalar.activation(rows[:, h * G:h * G + G, width:cols], below[:, h, :, :], ACT.Exp).then_inc(weighed, 1)

                stage_indices(0, 0)
                weigh(0, 0)
                with nc.scalar.Fori(0, NIT) as g:
                    for h in range(2):
                        k = g * 2 + h
                        stage_indices(k + 1, 1 - h)
                        weigh(k + 1, 1 - h)

            @block.tensor
            def _(pe):
                pe.wait_ge(ready, 1)
                pe.sem_inc(summed, RING)
                pe.sem_inc(top_spread, 2)

                def spread(k, h):
                    for q in range(2):
                        wait_past(pe, hot_copied, k * 2 + q)
                        for u in range(4 * q, 4 * q + 4):
                            pe.wait_ge(hot_made, k * G + (u + 1))
                            last = nc.tensor.transpose(ps_hot[:, (u % 4) * P:(u % 4 + 1) * P], hot[:, h * G + u, :],
                                                       c.ident[:, :])
                        last.then_inc(hot_turned, 1)
                        pe.wait_ge(hot_copied, k * 2 + (q + 1))
                        if q == 0:
                            wait_past(pe, lowered, k)
                        for u in range(4 * q, 4 * q + 4):
                            b = pe.value_load(order.tile_bucket[0:1, bass.ds(k * G + u, 1)], min_val=0, max_val=NB - 1)
                            last = nc.tensor.matmul(ps_top[:, u * H:(u + 1) * H], hotT[:, u, :],
                                                    flat(top[:, bass.ds(b, 1), :]), start=True, stop=True)
                        last.then_inc(top_spread, 1)

                spread(0, 0)
                with nc.tensor.Fori(0, NIT) as g:
                    for h in range(2):
                        k = g * 2 + h
                        spread(k + 1, 1 - h)
                        for u in range(G):
                            if u % 4 == 0:
                                pe.wait_ge(messages, k * 2 + (u // 4 + 1))
                            pe.wait_ge(added, k * G + (u + 1))
                            nc.tensor.matmul(part[u % 4][:, 0:cols], hot[:, h * G + u, :], rows[:, h * G + u, 0:cols],
                                             start=True, stop=True).then_inc(summed, 1)

            @block.vector
            def _(dve):
                nc.vector.memset(acc[:, :, :], 0.0)
                dve.sem_inc(added, 4)
                dve.drain().then_inc(ready, 1)

                def one_hots(k, h):
                    dve.wait_ge(summed, k * G + G)
                    for u in range(G):
                        nc.vector.tensor_scalar(hot[:, h * G + u, :], c.iota[:, :], order.local[:, bass.ds(k * G + u, 1)],
                                                None, ALU.is_equal).then_inc(hot_made, 1)

                def lower(k, h):
                    dve.wait_ge(top_spread, k * 2 + 4)
                    nc.vector.tensor_tensor(below[:, h, :, :], score[:, bass.ds(k * G, G), :],
                                            ps_top[:, 0:G * H].rearrange("p (u h) -> p u h", u=G), ALU.subtract)
                    dve.drain()
                    nc.vector.tensor_scalar(below[:, h, :, :], below[:, h, :, :], 0.0, None, ALU.min).then_inc(lowered, 1)

                one_hots(0, 0)
                lower(0, 0)
                with nc.vector.Fori(0, NIT) as g:
                    for h in range(2):
                        k = g * 2 + h
                        one_hots(k + 1, 1 - h)
                        dve.wait_ge(landed[h], g * (16 * G) + 16 * G)
                        dve.wait_ge(weighed, k + 1)
                        for u in range(h * G, h * G + G, 4):
                            m = rows[:, u:u + 4, 0:width].rearrange("p u (h d) -> p u h d", h=H)
                            w = rows[:, u:u + 4, width:cols].rearrange("p u (h o) -> p u h o", o=1)
                            nc.vector.tensor_tensor(m, m, w.broadcast_to([P, 4, H, width // H]), ALU.mult).then_inc(messages, 1)
                        lower(k + 1, 1 - h)
                        for u in range(G):
                            b = dve.value_load(order.tile_bucket[0:1, bass.ds(k * G + u, 1)], min_val=0, max_val=NB - 1)
                            dve.wait_ge(summed, k * G + (RING + u + 1))
                            dve.wait_ge(added, k * G + (u + 4))
                            a = acc[:, bass.ds(b, 1), 0:cols].rearrange("p o c -> p (o c)")
                            nc.vector.tensor_tensor(a, a, part[u % 4][:, 0:cols], ALU.add).then_inc(added, 1)


def load_nodes(nc, tag, x, x_d):
    with Box(nc, tag) as box:
        cleared, loaded = box.sem("cleared"), box.sem("loaded")
        with nc.Block() as block:

            @block.vector
            def _(dve):
                nc.vector.memset(x[:, NB - 1, :], 0.0)
                dve.drain().then_inc(cleared, 1)

            @block.sync
            def _(sp):
                sp.wait_ge(cleared, 1)
                sp.dma_start(x[:, 0:NB - 1, :], x_d[0:(NB - 1) * P, :].rearrange("(b p) d -> p b d", p=P)).then_inc(loaded, 16)
                sp.dma_start(x[0:LAST, NB - 1, :], x_d[(NB - 1) * P:N, :]).then_inc(loaded, 16)
                sp.wait_ge(loaded, 32)


def store_nodes(nc, tag, src, dst_d, rows=NPAD):
    with Box(nc, tag) as box:
        stored = box.sem("stored")
        full = NB if rows == NPAD else NB - 1
        with nc.Block() as block:

            @block.sync
            def _(sp):
                sp.dma_start(dst_d[0:full * P, :].rearrange("(b p) d -> p b d", p=P), src[:, 0:full, :]).then_inc(stored, 16)
                if full < NB:
                    sp.dma_start(dst_d[full * P:N, :], src[0:LAST, full, :]).then_inc(stored, 16)
                sp.wait_ge(stored, 16 * (1 + (full < NB)))


def sage(nc, tag, c, x, h, acc, own_d, wl_d, wr_d, b_d, residual):
    with Box(nc, tag) as box:
        wlT = box.sb("wlT", [P, 2, D])
        wrT = box.sb("wrT", [P, 2, D])
        bias = box.sb("bias", [P, D])
        transpose_weights(nc, tag + "w", c, [(wl_d, wlT), (wr_d, wrT)])

        def before(dve):
            if c.rdeg_made:
                return
            nc.vector.tensor_scalar(c.rdeg[:, :], acc[:, :, D], 1.0, None, ALU.max)
            dve.drain()
            nc.vector.reciprocal(c.rdeg[:, :], c.rdeg[:, :])
            c.rdeg_made = True

        def finish(dve, b, ps):
            if not residual:
                out = flat(h[:, bass.ds(b, 1), :])
                nc.vector.tensor_tensor(out, ps, bias[:, :], ALU.add)
                dve.drain()
                return nc.vector.tensor_scalar(out, out, 0.0, None, ALU.max)
            out = flat(x[:, bass.ds(b, 1), :])
            nc.vector.tensor_tensor(out, out, ps, ALU.add)
            dve.drain()
            return nc.vector.tensor_tensor(out, out, bias[:, :], ALU.add)

        project(nc, tag + "p", c, [(acc, 2, c.rdeg), (h, 2, None)],
                [wlT[:, 0, :], wlT[:, 1, :], wrT[:, 0, :], wrT[:, 1, :]], D, finish, before=before,
                load=[(bias[:, :], b_d.rearrange("(o d) -> o d", o=1).broadcast_to([P, D])),
                      (h[:, :, :], own_d.rearrange("(b p) d -> p b d", p=P))])


def fold_attention(nc, tag, c, lhs, attn_ds, heads, width, dst):
    blocks, rels = heads * width // P, len(lhs[0])
    with Box(nc, tag) as box:
        offset = box.sb("offset", [P, blocks, heads])
        inside = box.sb("inside", [P, blocks, heads])
        attn = box.sb("attn", [P, 2, blocks])
        spread = box.sb("spread", [P, blocks, 2, heads])
        folded = [box.ps(f"folded{k}", [P, 512]) for k in range(len(lhs))]
        made, loaded, ready, done = (box.sem(n) for n in ("made", "loaded", "ready", "done"))
        with nc.Block() as block:

            @block.gpsimd
            def _(pool):
                pool.iota(offset[:, :, :], pattern=[[P, blocks], [-width, heads]], base=0, channel_multiplier=1,
                          allow_small_or_imprecise_dtypes=True).then_inc(made, 1)

            @block.sync
            def _(sp):
                for s, d in enumerate(attn_ds):
                    flat_d = d.rearrange("h d -> (h d)")
                    for k in range(blocks):
                        sp.dma_start(attn[:, s, k:k + 1],
                                     flat_d[k * P:(k + 1) * P].rearrange("(p c) -> p c", c=1)).then_inc(loaded, 16)

            @block.vector
            def _(dve):
                dve.wait_ge(made, 1)
                dve.wait_ge(loaded, 32 * blocks)
                nc.vector.tensor_scalar(inside[:, :, :], offset[:, :, :], 0.0, None, ALU.is_ge)
                dve.drain()
                nc.vector.scalar_tensor_tensor(out=inside[:, :, :], in0=offset[:, :, :], scalar=float(width),
                                               in1=inside[:, :, :], op0=ALU.is_lt, op1=ALU.mult)
                dve.drain()
                for s in range(2):
                    for k in range(blocks):
                        nc.vector.tensor_scalar(spread[:, k, s, :], inside[:, k, :], attn[:, s, k:k + 1], None, ALU.mult)
                dve.drain().then_inc(ready, 1)
                dve.wait_ge(done, 1)
                n = rels * 2 * heads
                for fc in range(len(lhs)):
                    for s in range(2):
                        nc.vector.tensor_copy(
                            dst[:, fc, s, :, :],
                            folded[fc][:, 0:n].rearrange("p (r s h) -> p r s h", r=rels, s=2)[:, :, s, :])

            @block.tensor
            def _(pe):
                pe.wait_ge(ready, 1)
                for fc in range(len(lhs)):
                    for r in range(rels):
                        at = r * 2 * heads
                        for k in range(blocks):
                            last = nc.tensor.matmul(folded[fc][:, at:at + 2 * heads], lhs[fc][r][k],
                                                    spread[:, k, :, :].rearrange("p s h -> p (s h)"),
                                                    start=(k == 0), stop=(k == blocks - 1))
                last.then_inc(done, 1)


def relation_tables(nc, tag, c, h, wT, scoreT, rows_d, src_scores, dst_scores):
    RH = R8 * H1
    with Box(nc, tag) as box:
        stage = box.sb("stage", [P, 4, D])
        turned_sb = box.sb("turned_sb", [P, 4, D])
        out = box.sb("out", [P, 2, R8 * D])
        turned = [box.ps(f"turned{k}", [P, 512]) for k in range(2)]
        result = [box.ps(f"result{k}", [P, 512]) for k in range(5)]
        ready, staged, turns, copied, made_a, made_v, product = (
            box.sem(n) for n in ("ready", "staged", "turned", "copied", "made_a", "made_v", "product"))
        stored, slots_free = box.sem("stored"), box.sem("slots_free")
        with nc.Block() as block:

            @block.sync
            def _(sp):
                with nc.sync.Fori(0, NI) as i:
                    for u in range(U):
                        b = i * U + u
                        sp.wait_ge(made_a, b * 2 + 4)
                        sp.wait_ge(made_v, b * 3 + 5 + 3)
                        sp.dma_start(rows_d[bass.ds(b * P, P), :], out[:, u % 2, :]).then_inc(stored, 16)
                        sp.wait_ge(stored, b * 16 + 16)
                        sp.sem_inc(slots_free, 1)

            @block.scalar
            def _(act):
                act.wait_ge(ready, 1)

                def stage_block(b, u):
                    act.wait_ge(copied, b + (U - 2))
                    nc.scalar.copy(stage[:, u % 4, :], flat(h[:, bass.ds(b, 1), 0:D])).then_inc(staged, 1)

                with nc.scalar.Fori(0, NI) as i:
                    stage_block(i * U, 0)
                    for u in range(U):
                        b = i * U + u
                        if u + 1 < U:
                            stage_block(b + 1, u + 1)
                        act.wait_ge(slots_free, b + (2 if u == 0 else 1))
                        for j in range(2):
                            act.wait_ge(product, b * 5 + (j + 1))
                            nc.scalar.copy(out[:, u % 2, j * 512:(j + 1) * 512], result[j][:, :]).then_inc(made_a, 1)

            @block.tensor
            def _(pe):
                def turn(b, u):
                    pe.wait_ge(staged, b + 1)
                    pe.wait_ge(copied, b + (U if u == 0 else U - 1))
                    for k in range(2):
                        last = nc.tensor.transpose(turned[u % 2][:, k * P:(k + 1) * P],
                                                   stage[:, u % 4, k * P:(k + 1) * P], c.ident[:, :])
                    last.then_inc(turns, 1)

                pe.wait_ge(ready, 1)
                with nc.tensor.Fori(0, NI) as i:
                    turn(i * U, 0)
                    for u in range(U):
                        b = i * U + u
                        if u + 1 < U:
                            turn(b + 1, u + 1)
                        pe.wait_ge(copied, b + U + 1)
                        for j in range(5):
                            if j < 2:
                                pe.wait_ge(made_a, b * 2 + 2)
                            else:
                                pe.wait_ge(made_v, b * 3 + 5)
                            w = wT[:, :, j * 512:(j + 1) * 512] if j < 4 else scoreT
                            n = 512 if j < 4 else 2 * RH
                            for k in range(2):
                                last = nc.tensor.matmul(result[j][:, 0:n], turned_sb[:, u % 4, k * P:(k + 1) * P],
                                                        w[:, k, :], start=(k == 0), stop=(k == 1))
                            last.then_inc(product, 1)

            @block.vector
            def _(dve):
                dve.sem_inc(copied, U)
                dve.sem_inc(made_v, 5)
                dve.sem_inc(made_a, 2)
                dve.sem_inc(slots_free, 2)
                dve.drain().then_inc(ready, 1)

                def copy_turned(b, u):
                    dve.wait_ge(turns, b + 1)
                    nc.vector.tensor_copy(turned_sb[:, u % 4, :], turned[u % 2][:, 0:D]).then_inc(copied, 1)

                with nc.vector.Fori(0, NI) as i:
                    copy_turned(i * U, 0)
                    for u in range(U):
                        b = i * U + u
                        if u + 1 < U:
                            copy_turned(b + 1, u + 1)
                        dve.wait_ge(slots_free, b + (2 if u == 0 else 1))
                        for j in range(2, 4):
                            dve.wait_ge(product, b * 5 + (j + 1))
                            nc.vector.tensor_copy(out[:, u % 2, j * 512:(j + 1) * 512], result[j][:, :]).then_inc(made_v, 1)
                        dve.wait_ge(product, b * 5 + 5)
                        nc.vector.tensor_scalar(flat(src_scores[:, bass.ds(b, 1), :]), result[4][:, 0:RH], 1.0, None, ALU.mult)
                        nc.vector.tensor_scalar(flat(dst_scores[:, bass.ds(b, 1), :]), result[4][:, RH:2 * RH], 1.0,
                                                None, ALU.mult)
                        dve.drain().then_inc(made_v, 1)


def on_vector(nc, tag, loads, body):
    with Box(nc, tag) as box:
        loaded = box.sem("loaded")
        with nc.Block() as block:

            @block.sync
            def _(sp):
                for dst, src in loads:
                    sp.dma_start(dst, src).then_inc(loaded, 16)

            @block.vector
            def _(dve):
                if loads:
                    dve.wait_ge(loaded, 16 * len(loads))
                body(dve)


def row_bias(d, n):
    return d.rearrange("(o d) -> o d", o=1).broadcast_to([P, n])


def over_nodes(ap, n):
    return ap.rearrange("p (o d) -> p o d", o=1).broadcast_to([P, NB, n])


def layer1(nc, c, a, x, acc, order):
    rows_d = nc.dram_tensor("l1_rows", [NPAD, R8 * D], F32).ap()
    src_d = nc.dram_tensor("l1_src", [NPAD, R8 * H1], F32).ap()
    with Box(nc, "l1") as box:
        dst_scores = box.sb("dst_scores", [P, NB, R8 * H1])
        with Box(nc, "l1t") as b:
            wT = b.sb("wT", [P, 2, R8 * D])
            scoreT = b.sb("scoreT", [P, 2, 2 * R8 * H1])
            src_scores = b.sb("src_scores", [P, NB, R8 * H1])
            raw = acc[:, 0:2 * R8, 0:D]
            transpose_weights(nc, "l1x", c, [(a["L1_gnn_W"].rearrange("r o f -> (r o) f"), wT)], [raw])
            fold_attention(nc, "l1f", c,
                           [[[raw[:, 2 * r + k, fc * P:(fc + 1) * P] for k in range(2)] for r in range(R8)] for fc in range(2)],
                           (a["L1_gnn_attn_src"], a["L1_gnn_attn_dst"]), H1, D1,
                           scoreT[:, :, :].rearrange("p k (s r h) -> p k s r h", s=2, r=R8))
            normalize(nc, "n1", c, x, acc, None)
            relation_tables(nc, "l1p", c, acc, wT, scoreT, rows_d, src_scores, dst_scores)
            store_nodes(nc, "l1s", src_scores, src_d)
        score = box.sb("score", [P, T + G, H1])
        top = box.sb("top", [P, NB, H1])
        on_vector(nc, "l1z", [], lambda dve: nc.vector.memset(top[:, :, :], 0.0))
        attention_max(nc, "l1m", c, order, order.rel_other, src_d.rearrange("n (r h) -> (n r) h", r=R8), H1, R8,
                      dst_scores, score, top)
        attention_sum(nc, "l1a", c, order, order.rel_other, rows_d.rearrange("n (r d) -> (n r) d", r=R8), D, H1,
                      score, top, acc)
        rden = box.sb("rden", [P, NB, H1])

        def divide(dve):
            nc.vector.tensor_scalar(rden[:, :, :], acc[:, :, D:D + H1], 1e-12, None, ALU.add)
            dve.drain()
            nc.vector.reciprocal(rden[:, :, :], rden[:, :, :])
            dve.drain()
            m = acc[:, :, 0:D].rearrange("p b (h d) -> p b h d", h=H1)
            r = rden[:, :, :].rearrange("p b (h o) -> p b h o", o=1).broadcast_to([P, NB, H1, D1])
            nc.vector.tensor_tensor(m, m, r, ALU.mult)
            dve.drain()
            nc.vector.tensor_tensor(x[:, :, :], x[:, :, :], acc[:, :, 0:D], ALU.add)

        on_vector(nc, "l1d", [], divide)


def layer2(nc, c, a, x, acc, by_dst, by_src):
    support_d = nc.dram_tensor("support", [NPAD, D], F32).ap()
    with Box(nc, "l2") as box:
        w = box.sb("w", [P, 2, D])
        bias = box.sb("bias", [P, D])
        normalize(nc, "n2", c, x, acc, None)
        project(nc, "l2p", c, [(acc, 2, None)], [w[:, 0, :], w[:, 1, :]], D,
                lambda dve, b, ps: nc.vector.tensor_scalar(flat(acc[:, bass.ds(b, 1), 0:D]), ps, 1.0, None, ALU.mult),
                load=[(w[:, :, :], a["L2_gnn_weight"].rearrange("(c p) o -> p c o", p=P)),
                      (bias[:, :], row_bias(a["L2_gnn_bias"], D))])
        store_nodes(nc, "l2s", acc[:, :, 0:D], support_d)
        gather_sum(nc, "l2d", c, by_dst, by_dst.other, support_d, acc, D, weighted=True)
        gather_sum(nc, "l2r", c, by_src, by_src.other, support_d, acc, D, weighted=True, clear=False)

        def add(dve):
            nc.vector.tensor_tensor(acc[:, :, 0:D], acc[:, :, 0:D], over_nodes(bias[:, :], D), ALU.add)
            dve.drain()
            nc.vector.tensor_tensor(x[:, :, :], x[:, :, :], acc[:, :, 0:D], ALU.add)

        on_vector(nc, "l2a", [], add)


def layer3(nc, c, a, x, acc, order):
    rows_d = nc.dram_tensor("l3_rows", [NPAD, F3], F32).ap()
    src_d = nc.dram_tensor("l3_src", [NPAD, H3], F32).ap()
    with Box(nc, "l3") as box:
        w = box.sb("w", [P, 2, F3 + 2 * H3])
        wT = box.sb("wT", [P, 1, D])
        folded = box.sb("folded", [P, 2, 2, 1, H3])
        dst_scores = box.sb("dst_scores", [P, NB, H3])
        score = box.sb("score", [P, T + G, H3])
        top = box.sb("top", [P, NB, H3])
        rden = box.sb("rden", [P, NB, H3])
        lin = box.sb("lin", [P, D])
        lin_b = box.sb("lin_b", [P, D])
        gat_b = box.sb("gat_b", [P, F3])
        w_d = a["L3_gnn_W"]
        transpose_weights(nc, "l3x", c, [(w_d, wT)])
        fold_attention(nc, "l3f", c, [[[wT[:, 0, fc * P:(fc + 1) * P]]] for fc in range(2)],
                       (a["L3_gnn_attn_l"], a["L3_gnn_attn_r"]), H3, D3, folded)

        def prepare(dve):
            nc.vector.tensor_copy(w[:, :, F3:], folded[:, :, :, :, :].rearrange("p k s r h -> p k (s r h)"))
            nc.vector.memset(top[:, :, :], -NEG)

        on_vector(nc, "l3w", [(w[:, :, 0:F3], w_d.rearrange("(c p) o -> p c o", p=P)),
                              (lin[:, :], a["L3_gnn_lin_W"]), (lin_b[:, :], row_bias(a["L3_gnn_lin_b"], D)),
                              (gat_b[:, :], row_bias(a["L3_gnn_gat_bias"], F3))], prepare)
        normalize(nc, "n3", c, x, acc, None)
        cols = F3 + 2 * H3
        project(nc, "l3p", c, [(acc, 2, None)], [w[:, 0, :], w[:, 1, :]], cols,
                lambda dve, b, ps: nc.vector.tensor_scalar(flat(acc[:, bass.ds(b, 1), 0:cols]), ps, 1.0, None, ALU.mult))
        store_nodes(nc, "l3s", acc[:, :, 0:F3], rows_d)
        store_nodes(nc, "l3t", acc[:, :, F3:F3 + H3], src_d)
        on_vector(nc, "l3c", [], lambda dve: nc.vector.tensor_copy(dst_scores[:, :, :], acc[:, :, F3 + H3:cols]))
        attention_max(nc, "l3m", c, order, order.other, src_d, H3, 1, dst_scores, score, top)
        attention_sum(nc, "l3a", c, order, order.other, rows_d, F3, H3, score, top, acc)

        def divide(dve):
            nc.vector.tensor_scalar(rden[:, :, :], acc[:, :, F3:F3 + H3], 1e-30, None, ALU.max)
            dve.drain()
            nc.vector.reciprocal(rden[:, :, :], rden[:, :, :])
            dve.drain()
            m = acc[:, :, 0:F3].rearrange("p b (h d) -> p b h d", h=H3)
            r = rden[:, :, :].rearrange("p b (h o) -> p b h o", o=1).broadcast_to([P, NB, H3, D3])
            nc.vector.tensor_tensor(m, m, r, ALU.mult)
            dve.drain()
            nc.vector.tensor_tensor(acc[:, :, 0:F3], acc[:, :, 0:F3], over_nodes(gat_b[:, :], F3), ALU.add)
            dve.drain()
            nc.vector.tensor_scalar(acc[:, :, 0:F3], acc[:, :, 0:F3], 0.0, None, ALU.max)

        on_vector(nc, "l3d", [], divide)
        relu = box.sb("relu", [P, 2, D])

        def finish(dve, b, ps):
            r = relu[:, 0, :]
            nc.vector.tensor_tensor(r, ps, lin_b[:, :], ALU.add)
            dve.drain()
            out = flat(x[:, bass.ds(b, 1), :])
            nc.vector.scalar_tensor_tensor(out=out, in0=r, scalar=0.0, in1=out, op0=ALU.max, op1=ALU.add)
            return dve.drain()

        project(nc, "l3o", c, [(acc, 1, None)], [lin[:, :]], D, finish)


def build(nc, a, out_d, layers=4):
    c = Consts()
    with Box(nc, "k") as top:
        setup_constants(nc, top, c)
        by_dst, by_src = Order(), Order()
        for name, o in (("dst", by_dst), ("src", by_src)):
            o.tile_bucket = top.sb(f"bucket_{name}", [1, T + RING], I32)
            o.local = top.sb(f"local_{name}", [P, T + G])
            o.weight = top.sb(f"weight_{name}", [P, T + G])
            o.other = top.sb(f"other_{name}", [P, T + RING], I32)
            o.rel_other = o.type8 = None
        by_dst.rel_other = top.sb("rel_other", [P, T + RING], I32)
        by_dst.type8 = top.sb("type8", [P, T + G])
        c.rdeg = top.sb("rdeg", [P, NB])
        c.rdeg_made = False
        for name, key, other, o in (("sd", "dst", "src", by_dst), ("ss", "src", "dst", by_src)):
            rec_d = nc.dram_tensor(f"rec_{name}", [P * T, 4], I32).ap()
            sort_edges(nc, name, c, a[key], a[other], a["edge_type_8"], a["edge_type_11"], a["L2_gnn_alpha"], rec_d, o)
        x = top.sb("x", [P, NB, D])
        acc = top.sb("acc", [P, NB, ACCW])
        load_nodes(nc, "ld", x, a["x"])
        h0_d = nc.dram_tensor("h0", [NPAD, D], F32).ap()
        h1_d = nc.dram_tensor("h1", [NPAD, D], F32).ap()
        with Box(nc, "b0") as b:
            h = b.sb("h", [P, NB, D])
            normalize(nc, "n0", c, x, h, h0_d)
        gather_sum(nc, "g0", c, by_dst, by_dst.other, h0_d, acc, D, count=True)
        with Box(nc, "b1") as b:
            h = b.sb("h", [P, NB, D])
            sage(nc, "s0", c, x, h, acc, h0_d, a["L0_gnn_w1_l"], a["L0_gnn_w1_r"], a["L0_gnn_b1"], False)
            store_nodes(nc, "st0", h, h1_d)
        gather_sum(nc, "g1", c, by_dst, by_dst.other, h1_d, acc, D)
        with Box(nc, "b2") as b:
            h = b.sb("h", [P, NB, D])
            sage(nc, "s1", c, x, h, acc, h1_d, a["L0_gnn_w2_l"], a["L0_gnn_w2_r"], a["L0_gnn_b2"], True)
        if layers > 1:
            layer1(nc, c, a, x, acc, by_dst)
        if layers > 2:
            layer2(nc, c, a, x, acc, by_dst, by_src)
        if layers > 3:
            layer3(nc, c, a, x, acc, by_dst)
        store_nodes(nc, "out", x, out_d, rows=N)


_INS = ['x', 'src', 'dst', 'edge_type_11', 'edge_type_8', 'L0_gnn_w1_l', 'L0_gnn_w1_r', 'L0_gnn_b1', 'L0_gnn_w2_l',
        'L0_gnn_w2_r', 'L0_gnn_b2', 'L1_gnn_W', 'L1_gnn_attn_src', 'L1_gnn_attn_dst', 'L2_gnn_weight', 'L2_gnn_bias',
        'L2_gnn_alpha', 'L3_gnn_W', 'L3_gnn_attn_l', 'L3_gnn_attn_r', 'L3_gnn_gat_bias', 'L3_gnn_lin_W', 'L3_gnn_lin_b']
_OUTS = [((N, D), 'float32')]
LAYERS = 4


def kernel(**inputs):
    import numpy as _np
    import concourse.bacc as _bacc
    from concourse import mybir as _mybir
    from concourse.bass_utils import run_bass_kernel_spmd as _run

    nc = _bacc.Bacc("TRN2", target_bir_lowering=False, num_devices=1)
    arrays, args = {}, {}
    for name in _INS:
        a = _np.ascontiguousarray(inputs[name])
        arrays[f"in_{name}_dram"] = a
        args[name] = nc.dram_tensor(f"in_{name}_dram", a.shape, _mybir.dt.from_np(a.dtype), kind="ExternalInput").ap()
    out = nc.dram_tensor("out_0_dram", _OUTS[0][0], _mybir.dt.from_np(_np.dtype(_OUTS[0][1])), kind="ExternalOutput").ap()
    build(nc, args, out, LAYERS)
    r = _run(nc, [arrays], core_ids=[0])
    return r.results[0]["out_0_dram"]
```

```python
import math
from contextlib import ExitStack, contextmanager

import concourse.bass as bass
from concourse import mybir

F32 = mybir.dt.float32
BF16 = mybir.dt.bfloat16
I32 = mybir.dt.int32
ALU = mybir.AluOpType
ACT = mybir.ActivationFunctionType
AX_X = mybir.AxisListType.X

P = 128
N, D, E = 6250, 256, 100000
NB = -(-N // P)
NPAD = NB * P
LAST = N - (NB - 1) * P
EC = E // P
EREST = E - EC * P
CE = EC + 1
G = 8
RING = 2 * G
T = -(-(E // P + NB) // RING) * RING
NIT = T // RING
NH = T // G
U = 7
NI = NB // U
R8, H1, D1 = 8, 8, 32
R11 = 11
H3, D3 = 2, 64
F3 = H3 * D3
ACCW = D + H1
NEG = 1e30
EPS = 1e-5
SCAT_HALVES = ((0, 6), (6, 11))
SG = 11
NSG = EC // SG


class Box:

    def __init__(self, nc, tag):
        self.nc, self.tag, self.stack, self.sems = nc, tag, ExitStack(), []

    def __enter__(self):
        return self

    def __exit__(self, *a):
        if self.sems and a[0] is None:
            self.nc.clear_and_free_semaphores(self.sems)
            self.nc.all_engine_barrier()
        return self.stack.__exit__(*a)

    def sb(self, name, shape, dt=F32):
        return self.stack.enter_context(self.nc.sbuf_tensor(f"{self.tag}_{name}", shape, dt))

    def ps(self, name, shape, dt=F32):
        return self.stack.enter_context(self.nc.psum_tensor(f"{self.tag}_{name}", shape, dt))

    def sem(self, name):
        self.sems.append(self.nc.alloc_semaphore(f"{self.tag}_{name}"))
        return self.sems[-1]


def setup_constants(nc, box, c):
    c.iota = box.sb("iota", [P, P])
    c.ident = box.sb("ident", [P, P])
    c.identb = box.sb("identb", [P, P], BF16)
    c.below = box.sb("below", [P, P])
    c.upto = box.sb("upto", [P, P])
    c.ones = box.sb("ones", [P, P])
    diff = box.sb("diff", [P, P])
    made = box.sem("indices_made")
    with nc.Block() as block:

        @block.gpsimd
        def _(pool):
            pool.iota(c.iota[:, :], pattern=[[1, P]], base=0, channel_multiplier=0,
                      allow_small_or_imprecise_dtypes=True).then_inc(made, 1)
            pool.iota(diff[:, :], pattern=[[1, P]], base=0, channel_multiplier=-1,
                      allow_small_or_imprecise_dtypes=True).then_inc(made, 1)

        @block.vector
        def _(dve):
            nc.vector.memset(c.ones[:, :], 1.0)
            dve.wait_ge(made, 2)
            nc.vector.tensor_scalar(c.ident[:, :], diff[:, :], 0.0, None, ALU.is_equal)
            nc.vector.tensor_scalar(c.identb[:, :], diff[:, :], 0.0, None, ALU.is_equal)
            nc.vector.tensor_scalar(c.below[:, :], diff[:, :], 0.0, None, ALU.is_gt)
            nc.vector.tensor_scalar(c.upto[:, :], diff[:, :], 0.0, None, ALU.is_ge)


def sort_edges(nc, c, ends, t8_d, t11_d, alpha_d, rec_d, pads_d, todo_d, by_dst, by_src):
    with Box(nc, "so") as box:
        raw = [box.sb(f"end{k}", [P, CE], I32) for k in range(2)]
        t8 = box.sb("t8", [P, CE], I32)
        t11 = box.sb("t11", [P, CE], I32)
        bucket_i = box.sb("bucket_i", [P, CE], I32)
        bucket = box.sb("bucket", [P, CE])
        rec = box.sb("rec", [P, CE, 4], I32)
        todo = box.sb("todo", [P, T, 5], I32)
        spare = box.sb("spare", [P, T], I32)
        pads = box.sb("pads", [P, T, 4], I32)
        onesw = box.sb("onesw", [P, CE], BF16)
        match = box.sb("match", [P, CE])
        run = box.sb("run", [P, CE])
        pos = box.sb("pos", [P, CE])
        posi = box.sb("posi", [P, CE], I32)
        slot_t = box.sb("slot_t", [P, CE], I32)
        addr = box.sb("addr", [P, CE], I32)
        cnt = box.sb("cnt", [P, NB])
        tot_i = box.sb("tot_i", [P, NB], I32)
        tiles = box.sb("tiles", [P, NB])
        bucket_end = box.sb("bucket_end", [P, NB])
        start = box.sb("start", [P, NB])
        nT_i = box.sb("nT_i", [NB, 1], I32)
        nT = box.sb("nT", [NB, 1])
        endT = box.sb("endT", [NB, 1])
        tile_no = box.sb("tile_no", [NB, T])
        after = box.sb("after", [NB, T])
        alpha = box.sb("alpha", [P, R11])
        scratch = box.sb("scratch", [P, T])
        rec_ring = box.sb("rec_ring", [P, SG, 4], I32)
        addr_ring = box.sb("addr_ring", [P, SG], I32)
        ps_tot = box.ps("ps_tot", [P, 512])[:, 0:NB]
        ps_low = box.ps("ps_low", [P, 512])[:, 0:NB]
        ps_nT = box.ps("ps_nT", [P, 512])[0:NB, 0:1]
        ps_end = box.ps("ps_end", [P, 512])[0:NB, 0:1]
        ps_bk = box.ps("ps_bk", [P, 512])[0:1, 0:T // 2]
        ps_bk2 = box.ps("ps_bk2", [P, 512])[0:1, 0:T // 2]
        filled, loaded, padded, counted, summed, nt_ready, end_summed, after_ready, bk_summed, iota_made = (
            box.sem(x) for x in ("filled", "loaded", "padded", "counted", "summed", "nt_ready",
                                 "end_summed", "after_ready", "bk_summed", "iota_made"))
        placed, ring_full, reloaded = box.sem("placed"), box.sem("ring_full"), box.sem("reloaded")
        scattered = [box.sem(f"scattered{h}") for h in range(2)]
        last_out, held, todo_ready, todo_stored = (box.sem(x) for x in ("last_out", "held", "todo_ready", "todo_stored"))
        with nc.Block() as block:

            @block.sync
            def _(sp):
                sp.wait_ge(filled, 1)
                sources = ((ends[0], raw[0]), (ends[1], raw[1]), (t8_d, t8), (t11_d, t11))
                for d, s in sources:
                    sp.dma_start(s[:, 0:EC], d[0:EC * P].rearrange("(p c) -> p c", p=P)).then_inc(loaded, 16)
                    sp.dma_start(s[0:EREST, EC:CE], d[EC * P:E].rearrange("(p c) -> p c", c=1)).then_inc(loaded, 16)
                sp.dma_start(alpha[:, :], alpha_d.rearrange("r o -> o r").broadcast_to([P, R11])).then_inc(loaded, 16)
                for d in (rec_d, pads_d):
                    sp.dma_start(d.rearrange("(p t) f -> p t f", p=P), pads[:, :, :]).then_inc(padded, 16)
                sp.wait_ge(todo_ready, 1)
                sp.dma_start(todo_d, todo[:, :, :]).then_inc(todo_stored, 16)
                for h, (a, b) in enumerate(SCAT_HALVES):
                    sp.wait_ge(scattered[h], 16 * (b - a) * NSG)
                sp.wait_ge(last_out, 16)
                sp.dma_start(pads[:, :, :], rec_d.rearrange("(p t) f -> p t f", p=P)).then_inc(reloaded, 16)
                sp.wait_ge(todo_stored, 16)

            @block.gpsimd
            def _(pool):
                pool.iota(tile_no[:, :], pattern=[[1, T]], base=0, channel_multiplier=0,
                          allow_small_or_imprecise_dtypes=True).then_inc(iota_made, 1)
                pool.iota(spare[:, :], pattern=[[P, T]], base=P * T - EC * P, channel_multiplier=1).then_inc(iota_made, 1)
                pool.wait_ge(padded, 32)
                with nc.gpsimd.Fori(0, NSG) as g:
                    for h, (a, b) in enumerate(SCAT_HALVES):
                        hold(pool, ring_full, g * 2 + (h + 1), held)
                        for u in range(a, b):
                            pool.indirect_dma_start(
                                out=rec_d, out_offset=bass.IndirectOffsetOnAxis(ap=addr_ring[:, u:u + 1], axis=0),
                                in_=rec_ring[:, u, :], in_offset=None).then_inc(scattered[h], 16)
                pool.indirect_dma_start(
                    out=rec_d, out_offset=bass.IndirectOffsetOnAxis(ap=addr[0:EREST, EC:CE], axis=0),
                    in_=rec[0:EREST, EC, :], in_offset=None).then_inc(last_out, 16)

            @block.scalar
            def _(act):
                act.wait_ge(placed, 1)

                def stage(g, a, b):
                    nc.scalar.copy(rec_ring[:, a:b, :].rearrange("p c f -> p (c f)"),
                                   rec[:, :, :].rearrange("p c f -> p (c f)")[:, bass.ds((g * SG + a) * 4, (b - a) * 4)])
                    nc.scalar.copy(addr_ring[:, a:b], addr[:, bass.ds(g * SG + a, b - a)])
                    act.drain().then_inc(ring_full, 1)

                for a, b in SCAT_HALVES:
                    stage(0, a, b)
                with nc.scalar.Fori(0, NSG - 1) as g:
                    for h, (a, b) in enumerate(SCAT_HALVES):
                        act.wait_ge(scattered[h], g * (16 * (b - a)) + 16 * (b - a))
                        stage(g + 1, a, b)

            @block.tensor
            def _(pe):
                for k in range(2):
                    pe.wait_ge(counted, k + 1)
                    nc.tensor.matmul(ps_tot[:, :], c.ones[:, :], cnt[:, :], start=True, stop=True)
                    nc.tensor.matmul(ps_low[:, :], c.below[:, :], cnt[:, :], start=True, stop=True)
                    nc.tensor.matmul(ps_nT[:, :], cnt[:, :], c.ones[:, 0:1], start=True, stop=True).then_inc(summed, 1)
                    pe.wait_ge(nt_ready, k + 1)
                    nc.tensor.matmul(ps_end[:, :], c.upto[0:NB, 0:NB], nT[:, :], start=True, stop=True).then_inc(end_summed, 1)
                    pe.wait_ge(after_ready, k + 1)
                    nc.tensor.matmul(ps_bk[:, :], c.ones[0:NB, 0:1], after[:, 0:T // 2], start=True, stop=True)
                    nc.tensor.matmul(ps_bk2[:, :], c.ones[0:NB, 0:1], after[:, T // 2:T], start=True, stop=True).then_inc(bk_summed, 1)

            @block.vector
            def _(dve):
                for k in range(2):
                    nc.vector.memset(raw[k][:, EC:CE], P * (P - 1))
                nc.vector.memset(t8[:, EC:CE], 0)
                nc.vector.memset(t11[:, EC:CE], 0)
                nc.vector.memset(pads[:, :, :], 0)
                dve.drain()
                nc.vector.memset(pads[:, :, 1:2], -1)
                nc.vector.memset(onesw[:, :], 1.0)
                nc.vector.memset(pos[:, :], 0.0)
                dve.drain().then_inc(filled, 1)
                nc.vector.memset(todo[:, :, :], 0)
                dve.wait_ge(iota_made, 2)
                dve.drain()
                nc.vector.tensor_copy(todo[:, :, 4], spare[:, :])
                dve.wait_ge(loaded, 16 * 9)

                def place(k, records, order):
                    nc.vector.tensor_scalar(bucket_i[:, :], raw[k][:, :], 7, None, ALU.arith_shift_right)
                    nc.vector.tensor_copy(records[:, :, 0], raw[1 - k][:, :])
                    nc.vector.tensor_scalar(records[:, :, 1], raw[k][:, :], P - 1, None, ALU.bitwise_and)
                    nc.vector.tensor_copy(records[:, :, 2], t8[:, :])
                    nc.vector.tensor_copy(records[:, :, 3], t11[:, :])
                    dve.drain()
                    nc.vector.tensor_copy(bucket[:, :], bucket_i[:, :])
                    dve.drain()
                    with nc.vector.Fori(0, NB) as b:
                        nc.vector.tensor_scalar(match[:, :], bucket[:, :], c.iota[:, bass.ds(b, 1)], 0.0,
                                                ALU.is_equal, ALU.add, accum_out=cnt[:, bass.ds(b, 1)])
                        dve.drain()
                    dve.drain().then_inc(counted, 1)
                    dve.wait_ge(summed, k + 1)
                    nc.vector.tensor_scalar(tot_i[:, :], ps_tot[:, :], float(P - 1), None, ALU.add)
                    nc.vector.tensor_scalar(nT_i[:, :], ps_nT[:, :], float(P - 1), None, ALU.add)
                    dve.drain()
                    nc.vector.tensor_scalar(tot_i[:, :], tot_i[:, :], 7, None, ALU.arith_shift_right)
                    nc.vector.tensor_scalar(nT_i[:, :], nT_i[:, :], 7, None, ALU.arith_shift_right)
                    dve.drain()
                    nc.vector.tensor_copy(tiles[:, :], tot_i[:, :])
                    nc.vector.tensor_copy(nT[:, :], nT_i[:, :])
                    dve.drain().then_inc(nt_ready, 1)
                    nc.vector.tensor_tensor_scan(bucket_end[:, :], onesw[:, 0:NB], tiles[:, :], 0.0, ALU.mult, ALU.add)
                    dve.drain()
                    nc.vector.tensor_tensor(start[:, :], bucket_end[:, :], tiles[:, :], ALU.subtract)
                    dve.drain()
                    nc.vector.tensor_scalar(start[:, :], start[:, :], float(P), -1.0, ALU.mult, ALU.add)
                    dve.drain()
                    nc.vector.tensor_tensor(start[:, :], start[:, :], ps_low[:, :], ALU.add)
                    dve.drain()
                    with nc.vector.Fori(0, NB) as b:
                        nc.vector.tensor_scalar(match[:, :], bucket[:, :], c.iota[:, bass.ds(b, 1)], None, ALU.is_equal)
                        dve.drain()
                        nc.vector.tensor_tensor_scan(run[:, :], onesw[:, :], match[:, :], start[:, bass.ds(b, 1)],
                                                     ALU.mult, ALU.add)
                        dve.drain()
                        nc.vector.copy_predicated(pos[:, :], match[:, :].bitcast(I32), run[:, :])
                        dve.drain()
                    nc.vector.tensor_copy(posi[:, :], pos[:, :])
                    dve.drain()
                    nc.vector.tensor_scalar(slot_t[:, :], posi[:, :], 7, None, ALU.arith_shift_right)
                    nc.vector.tensor_scalar(posi[:, :], posi[:, :], P - 1, None, ALU.bitwise_and)
                    dve.drain()

                def row(out, lanes, a, b):
                    nc.vector.scalar_tensor_tensor(out=out, in0=posi[0:lanes, a:b], scalar=float(T),
                                                   in1=slot_t[0:lanes, a:b], op0=ALU.mult, op1=ALU.add)

                def tile_buckets(k, order):
                    dve.wait_ge(end_summed, k + 1)
                    nc.vector.tensor_copy(endT[:, :], ps_end[:, :])
                    dve.drain()
                    nc.vector.tensor_scalar(after[:, :], tile_no[:, :], endT[:, :], None, ALU.is_ge)
                    nc.vector.memset(order.tile_bucket[:, :], 0)
                    dve.drain().then_inc(after_ready, 1)
                    dve.wait_ge(bk_summed, k + 1)
                    nc.vector.tensor_scalar(order.tile_bucket[:, 0:T // 2], ps_bk[:, :], float(NB - 1), None, ALU.min)
                    nc.vector.tensor_scalar(order.tile_bucket[:, T // 2:T], ps_bk2[:, :], float(NB - 1), None, ALU.min)

                place(0, rec, by_dst)
                row(addr[:, :], P, 0, CE)
                dve.drain().then_inc(placed, 1)
                tile_buckets(0, by_dst)
                place(1, todo[:, 0:CE, :], by_src)
                row(todo[:, 0:EC, 4], P, 0, EC)
                row(todo[0:EREST, EC:CE, 4], EREST, EC, CE)
                dve.drain().then_inc(todo_ready, 1)
                tile_buckets(1, by_src)
                dve.wait_ge(reloaded, 16)
                unpack(nc, dve, pads, alpha, scratch, by_dst)


def unpack(nc, dve, records, alpha, scratch, out):
    nc.vector.memset(out.local[:, T:T + G], -1.0)
    nc.vector.memset(out.other[:, T:], 0)
    nc.vector.tensor_copy(out.other[:, 0:T], records[:, :, 0])
    nc.vector.tensor_copy(out.local[:, 0:T], records[:, :, 1])
    nc.vector.memset(out.weight[:, :], 0.0)
    if out.rel_other is not None:
        nc.vector.scalar_tensor_tensor(out=out.rel_other[:, 0:T], in0=records[:, :, 0], scalar=float(R8),
                                       in1=records[:, :, 2], op0=ALU.mult, op1=ALU.add)
        nc.vector.memset(out.rel_other[:, T:], 0)
        nc.vector.memset(out.type8[:, T:T + G], 0.0)
        nc.vector.tensor_copy(out.type8[:, 0:T], records[:, :, 2])
    dve.drain()
    for r in range(R11):
        nc.vector.tensor_scalar(scratch[:, :], records[:, :, 3], float(r), alpha[:, r:r + 1], ALU.is_equal, ALU.mult)
        dve.drain()
        nc.vector.tensor_tensor(out.weight[:, 0:T], out.weight[:, 0:T], scratch[:, :], ALU.add)
        dve.drain()


def wait_past(eng, sem, count):
    if not isinstance(count, int) or count > 0:
        eng.wait_ge(sem, count)


def hold(pool, sem, count, held):
    pool.wait_ge(sem, count)
    pool.sem_inc(held, 1)


class Order:
    pass


class Consts:
    pass


def gather_sum(nc, tag, c, order, index, table, acc, width, weighted=False, count=False, clear=True):
    cols = width + (1 if count else 0)
    with Box(nc, tag) as box:
        rows = box.sb("rows", [P, RING, ACCW])
        hot = box.sb("hot", [P, RING, P])
        idx = box.sb("idx", [P, RING], I32)
        part = [box.ps(f"part{k}", [P, 512]) for k in range(4)]
        ready = box.sem("ready")
        staged = box.sem("indices_staged")
        held = box.sem("held")
        landed = [box.sem(f"rows_landed{h}") for h in range(2)]
        hot_made = box.sem("hot_made")
        summed = box.sem("tiles_summed")
        added = box.sem("parts_added")
        with nc.Block() as block:

            @block.gpsimd
            def _(pool):
                pool.wait_ge(ready, 1)
                with nc.gpsimd.Fori(0, NIT) as g:
                    for h in range(2):
                        pool.wait_ge(staged, g * 2 + (h + 1))
                        for u in range(h * G, h * G + G):
                            if u % 4 == 0:
                                hold(pool, summed, g * RING + (u + 4), held)
                            pool.indirect_dma_start(
                                out=rows[:, u, 0:width], out_offset=None, in_=table,
                                in_offset=bass.IndirectOffsetOnAxis(ap=idx[:, u:u + 1], axis=0)).then_inc(landed[h], 16)

            @block.scalar
            def _(act):
                with nc.scalar.Fori(0, NIT) as g:
                    for h in range(2):
                        act.wait_ge(summed, g * RING + (h + 1) * G)
                        nc.scalar.copy(idx[:, h * G:h * G + G],
                                       index[:, bass.ds(g * RING + h * G, G)]).then_inc(staged, 1)

            @block.tensor
            def _(pe):
                pe.sem_inc(summed, RING)
                with nc.tensor.Fori(0, NIT) as g:
                    for u in range(RING):
                        if u % G == 0:
                            pe.wait_ge(landed[u // G], g * (16 * G) + 16 * G)
                        pe.wait_ge(hot_made, g * RING + (u + 1))
                        pe.wait_ge(added, g * RING + (u + 1))
                        nc.tensor.matmul(part[u % 4][:, 0:cols], hot[:, u, :], rows[:, u, 0:cols],
                                         start=True, stop=True).then_inc(summed, 1)

            @block.vector
            def _(dve):
                if clear:
                    nc.vector.memset(acc[:, :, :], 0.0)
                if count:
                    nc.vector.memset(rows[:, :, width:width + 1], 1.0)
                dve.drain().then_inc(ready, 1)
                dve.sem_inc(added, 4)

                def one_hots(tile0, h):
                    for u in range(h * G, h * G + G):
                        t = tile0 + (u - h * G)
                        nc.vector.tensor_scalar(hot[:, u, :], c.iota[:, :], order.local[:, bass.ds(t, 1)],
                                                order.weight[:, bass.ds(t, 1)] if weighted else None,
                                                ALU.is_equal, ALU.mult if weighted else ALU.bypass).then_inc(hot_made, 1)

                one_hots(0, 0)
                with nc.vector.Fori(0, NIT) as g:
                    for h in range(2):
                        dve.wait_ge(summed, g * RING + (h + 2) * G)
                        one_hots(g * RING + (h + 1) * G, 1 - h)
                        buckets = buckets_of(nc, mybir.EngineType.DVE, order, g * RING + h * G)
                        for u in range(h * G, h * G + G):
                            dve.wait_ge(summed, g * RING + (RING + u + 1))
                            dve.wait_ge(added, g * RING + (u + 4))
                            a = acc[:, bass.ds(buckets[u % G], 1), 0:cols].rearrange("p o c -> p (o c)")
                            nc.vector.tensor_tensor(a, a, part[u % 4][:, 0:cols], ALU.add).then_inc(added, 1)


def normalize(nc, tag, c, x, h, table_d):
    with Box(nc, tag) as box:
        stats = box.sb("stats", [P, NB, 6])
        mv = box.sb("mv", [P, NB, 2])
        rstd = box.sb("rstd", [P, NB])
        shift = box.sb("shift", [P, NB])
        var_ready, std_ready, scale_ready, made, stored = (
            box.sem(n) for n in ("var_ready", "std_ready", "scale_ready", "made", "stored"))
        with nc.Block() as block:

            @block.vector
            def _(dve):
                with nc.vector.Fori(0, NI) as i:
                    for u in range(U):
                        nc.vector.bn_stats(stats[:, bass.ds(i * U + u, 1), :].rearrange("p o s -> p (o s)"),
                                           x[:, bass.ds(i * U + u, 1), :].rearrange("p o d -> p (o d)"))
                dve.drain()
                for b in range(NB):
                    nc.vector.bn_aggr(mv[:, b, :], stats[:, b, :])
                dve.drain()
                nc.vector.tensor_scalar(rstd[:, :], mv[:, :, 1], EPS, None, ALU.add)
                dve.drain().then_inc(var_ready, 1)
                dve.wait_ge(std_ready, 1)
                nc.vector.reciprocal(rstd[:, :], rstd[:, :])
                dve.drain()
                nc.vector.scalar_tensor_tensor(out=shift[:, :], in0=mv[:, :, 0], scalar=-1.0, in1=rstd[:, :],
                                               op0=ALU.mult, op1=ALU.mult)
                dve.drain().then_inc(scale_ready, 1)

            @block.scalar
            def _(act):
                act.wait_ge(var_ready, 1)
                nc.scalar.activation(rstd[:, :], rstd[:, :], ACT.Sqrt)
                act.drain().then_inc(std_ready, 1)
                act.wait_ge(scale_ready, 1)
                with nc.scalar.Fori(0, NI) as i:
                    for u in range(U):
                        b = i * U + u
                        nc.scalar.activation(h[:, bass.ds(b, 1), 0:D].rearrange("p o d -> p (o d)"),
                                             x[:, bass.ds(b, 1), :].rearrange("p o d -> p (o d)"),
                                             ACT.Relu, bias=shift[:, bass.ds(b, 1)],
                                             scale=rstd[:, bass.ds(b, 1)]).then_inc(made, 1)

            @block.sync
            def _(sp):
                if table_d is not None:
                    table = table_d.rearrange("(b p) d -> p b d", p=P)
                    for i in range(NI):
                        sp.wait_ge(made, (i + 1) * U)
                        sp.dma_start(table[:, i * U:(i + 1) * U, :], h[:, i * U:(i + 1) * U, :]).then_inc(stored, 16)
                    sp.wait_ge(stored, 16 * NI)


def transpose_weights(nc, tag, c, pairs, raw=None):
    with Box(nc, tag) as box:
        raw = raw or [box.sb(f"raw{k}", [P, w_d.shape[0] // P, w_d.shape[1]]) for k, (w_d, _) in enumerate(pairs)]
        turned = [box.ps(f"turned{k}", [P, 512]) for k in range(2)]
        loaded, turns, copied = box.sem("loaded"), box.sem("turned"), box.sem("copied")
        blocks = [(raw[k][:, oc, fc * P:(fc + 1) * P], wT[:, fc, oc * P:(oc + 1) * P])
                  for k, (w_d, wT) in enumerate(pairs)
                  for fc in range(w_d.shape[1] // P) for oc in range(w_d.shape[0] // P)]
        with nc.Block() as block:

            @block.sync
            def _(sp):
                for k, (w_d, _) in enumerate(pairs):
                    sp.dma_start(raw[k][:, :, :], w_d.rearrange("(c p) f -> p c f", p=P)).then_inc(loaded, 16)

            @block.tensor
            def _(pe):
                pe.wait_ge(loaded, 16 * len(pairs))
                for n, (src, _) in enumerate(blocks):
                    if n >= 2:
                        pe.wait_ge(copied, n - 1)
                    nc.tensor.transpose(turned[n % 2][:, 0:P], src, c.ident[:, :]).then_inc(turns, 1)

            @block.vector
            def _(dve):
                for n, (_, dst) in enumerate(blocks):
                    dve.wait_ge(turns, n + 1)
                    nc.vector.tensor_copy(dst, turned[n % 2][:, 0:P]).then_inc(copied, 1)


def project(nc, tag, c, sources, weights, cols, finish, before=None, load=None):
    chunks = sum(n for _, n, _ in sources)
    with Box(nc, tag) as box:
        stage = box.sb("stage", [P, 4, chunks * P])
        turned_sb = box.sb("turned_sb", [P, 4, chunks * P])
        turned = [box.ps(f"turned{k}", [P, 512]) for k in range(2)]
        result = [box.ps(f"result{k}", [P, 512]) for k in range(2)]
        ready, staged, turns, copied, product, finished, got = (
            box.sem(n) for n in ("ready", "staged", "turned", "copied", "product", "finished", "got"))
        with nc.Block() as block:

            @block.sync
            def _(sp):
                for dst, src in load or []:
                    sp.dma_start(dst, src).then_inc(got, 16)

            @block.scalar
            def _(act):
                act.wait_ge(ready, 1)
                with nc.scalar.Fori(0, NI) as i:
                    for u in range(U):
                        b = i * U + u
                        act.wait_ge(copied, b + (U - 2))
                        at = 0
                        for k, (src, n, scale) in enumerate(sources):
                            a = src[:, bass.ds(b, 1), 0:n * P].rearrange("p o d -> p (o d)")
                            last = nc.scalar.activation(stage[:, u % 4, at:at + n * P], a, ACT.Copy,
                                                        scale=1.0 if scale is None else scale[:, bass.ds(b, 1)])
                            last.then_inc(staged, 1)
                            at += n * P

            @block.tensor
            def _(pe):
                def turn(b, u):
                    pe.wait_ge(staged, b * len(sources) + len(sources))
                    pe.wait_ge(copied, b + (U if u == 0 else U - 1))
                    for k in range(chunks):
                        last = nc.tensor.transpose(turned[u % 2][:, k * P:(k + 1) * P],
                                                   stage[:, u % 4, k * P:(k + 1) * P], c.ident[:, :])
                    last.then_inc(turns, 1)

                pe.wait_ge(ready, 1)
                with nc.tensor.Fori(0, NI) as i:
                    turn(i * U, 0)
                    for u in range(U):
                        b = i * U + u
                        if u + 1 < U:
                            turn(b + 1, u + 1)
                        pe.wait_ge(copied, b + U + 1)
                        pe.wait_ge(finished, b + (2 if u == 0 else 1))
                        for k in range(chunks):
                            last = nc.tensor.matmul(result[u % 2][:, 0:cols], turned_sb[:, u % 4, k * P:(k + 1) * P],
                                                    weights[k], start=(k == 0), stop=(k == chunks - 1))
                        last.then_inc(product, 1)

            @block.vector
            def _(dve):
                if load:
                    dve.wait_ge(got, 16 * len(load))
                if before:
                    before(dve)
                dve.sem_inc(copied, U)
                dve.sem_inc(finished, 2)
                dve.drain().then_inc(ready, 1)

                def copy_turned(b, u):
                    dve.wait_ge(turns, b + 1)
                    nc.vector.tensor_copy(turned_sb[:, u % 4, :], turned[u % 2][:, 0:chunks * P]).then_inc(copied, 1)

                with nc.vector.Fori(0, NI) as i:
                    copy_turned(i * U, 0)
                    for u in range(U):
                        b = i * U + u
                        if u + 1 < U:
                            copy_turned(b + 1, u + 1)
                        dve.wait_ge(product, b + 1)
                        finish(dve, b, result[u % 2][:, 0:cols]).then_inc(finished, 1)


def flat(ap):
    return ap.rearrange("p o d -> p (o d)")


def buckets_of(nc, engine, order, tile, n=G):
    _, values = nc.values_load_multi_w_load_instructions(
        order.tile_bucket[0:1, bass.ds(tile, n)], engines=[engine], min_val=0, max_val=NB - 1,
        skip_runtime_bounds_check_because="a count of buckets, clipped to NB - 1 where it is made")
    return values


def there(k):
    return not isinstance(k, int) or k < NH


def each_half(engine, step):
    with engine.Fori(0, NH // 4 - 1) as g:
        for hh in range(4):
            step(g, hh)
    for hh in range(4):
        step(NH // 4 - 1, hh)


def attention_max(nc, tag, c, order, index, table, H, R, dst_scores, score, top, x, x_d, later=None):
    with Box(nc, tag) as box:
        src = box.sb("src", [P, 2, G, H])
        hot = box.sb("hot", [P, 2, G, P], BF16)
        hotT = box.sb("hotT", [P, G, P])
        other = box.sb("other", [P, 4, G, P], BF16)
        typed = box.sb("typed", [P, G, R])
        picked = box.sb("picked", [P, G, R, H])
        s = box.sb("s", [P, G, H])
        rest = box.sb("rest", [P, G, H])
        parts = box.sb("parts", [P, G, 3, H], BF16)
        partsT = box.sb("partsT", [3 * H, G * P], BF16)
        sel = box.sb("sel", [3 * H, H, P], BF16)
        sel_v = hotT[0:3 * H, 0:H, :]
        sel_a = other[0:3 * H, 0, 0:H, :]
        tile_top = box.sb("tile_top", [P, G, H])
        idx = box.sb("idx", [P, 2, G], I32)
        todo = box.sb("todo", [P, 2, G, 5], I32)
        ps_hot = box.ps("ps_hot", [P, G, P], BF16)
        ps_dst = box.ps("ps_dst", [P, 512])
        ps_parts = box.ps("ps_parts", [P, G * P], BF16)[0:3 * H, :]
        big = [box.ps(f"big{k}", [P, H * P]) for k in range(2)]
        names = ("ready", "held", "staged", "hot_made", "hot_turned", "hot_copied", "dst_spread", "scored",
                 "parts_turned", "parts_copied", "masked", "reduced", "topped", "sel_index", "x_stored")
        (ready, held, staged, hot_made, hot_turned, hot_copied, dst_spread, scored, parts_turned, parts_copied,
         masked, reduced, topped, sel_index, x_stored) = (box.sem(n) for n in names)
        landed = [box.sem(f"landed{h}") for h in range(2)]
        fed = [box.sem(f"fed{h}") for h in range(2)]
        scattered = [box.sem(f"scattered{h}") for h in range(2)]
        with nc.Block() as block:

            @block.sync
            def _(sp):
                sp.dma_start(x_d.rearrange("(b p) d -> p b d", p=P), x[:, :, :]).then_inc(x_stored, 16)

                def feed(k, h):
                    sp.dma_start(todo[:, h, :, :], later[0][:, bass.ds(k * G, G), :]).then_inc(fed[h], 16)

                def feed_ahead(g, hh):
                    k = g * 4 + hh
                    if there(k + 2):
                        sp.wait_ge(scattered[hh % 2], g * (32 * G) + 16 * G * (hh // 2 + 1))
                        feed(k + 2, hh % 2)

                if later:
                    feed(0, 0)
                    feed(1, 1)
                    each_half(nc.sync, feed_ahead)
                    for h in range(2):
                        sp.wait_ge(scattered[h], 16 * G * (NH // 2))
                sp.wait_ge(x_stored, 16)

            @block.gpsimd
            def _(pool):
                pool.iota(sel_v, pattern=[[-1, H], [0, P]], base=0,
                          channel_multiplier=1, allow_small_or_imprecise_dtypes=True).then_inc(sel_index, 1)
                pool.wait_ge(ready, 1)

                def gather(g, hh):
                    k, h = g * 4 + hh, hh % 2
                    pool.wait_ge(staged, k + 1)
                    hold(pool, scored, k + 1, held)
                    for u in range(G):
                        pool.indirect_dma_start(
                            out=src[:, h, u, :], out_offset=None, in_=table,
                            in_offset=bass.IndirectOffsetOnAxis(ap=idx[:, h, u:u + 1], axis=0)).then_inc(landed[h], 16)
                    if later:
                        hold(pool, fed[h], (g * 2 + hh // 2) * 16 + 16, held)
                        for u in range(G):
                            pool.indirect_dma_start(
                                out=later[1], out_offset=bass.IndirectOffsetOnAxis(ap=todo[:, h, u, 4:5], axis=0),
                                in_=todo[:, h, u, 0:4], in_offset=None).then_inc(scattered[h], 16)

                each_half(nc.gpsimd, gather)

            @block.scalar
            def _(act):
                act.wait_ge(ready, 1)

                def stage_indices(k, h):
                    nc.scalar.copy(idx[:, h, :], index[:, bass.ds(k * G, G)]).then_inc(staged, 1)

                def copy_hots(k, slot):
                    act.wait_ge(hot_turned, k + 1)
                    wait_past(act, dst_spread, k)
                    nc.scalar.copy(hotT[:, :, :], ps_hot[:, :, :])
                    act.wait_ge(masked, k * G + G)
                    nc.scalar.activation(other[:, slot, :, :], ps_hot[:, :, :], ACT.Copy, scale=NEG, bias=-NEG)
                    act.drain().then_inc(hot_copied, 1)

                def copy_parts(k):
                    act.wait_ge(parts_turned, k + 1)
                    act.wait_ge(masked, k * G + 4 * G)
                    nc.scalar.copy(partsT[:, :], ps_parts[:, :]).then_inc(parts_copied, 1)

                stage_indices(0, 0)
                stage_indices(1, 1)
                copy_hots(0, 0)
                copy_hots(1, 1)
                act.wait_ge(scored, 3)
                stage_indices(2, 0)
                copy_parts(0)

                def step(g, hh):
                    k = g * 4 + hh
                    if there(k + 3):
                        act.wait_ge(scored, k + 4)
                        stage_indices(k + 3, (hh + 3) % 2)
                    if there(k + 2):
                        copy_hots(k + 2, (hh + 2) % 4)
                    if there(k + 1):
                        copy_parts(k + 1)

                each_half(nc.scalar, step)

            @block.tensor
            def _(pe):
                pe.wait_ge(ready, 1)
                pe.sem_inc(masked, 4 * G)

                def turn_hots(k, h):
                    pe.wait_ge(hot_made, k + 1)
                    wait_past(pe, hot_copied, k)
                    for u in range(G):
                        last = nc.tensor.transpose(ps_hot[:, u, :], hot[:, h, u, :], c.identb[:, :])
                    last.then_inc(hot_turned, 1)

                def spread(k):
                    buckets = buckets_of(nc, mybir.EngineType.PE, order, k * G)
                    pe.wait_ge(hot_copied, k + 1)
                    pe.wait_ge(scored, k + 2)
                    for u in range(G):
                        last = nc.tensor.matmul(ps_dst[:, u * R * H:(u + 1) * R * H], hotT[:, u, :],
                                                flat(dst_scores[:, bass.ds(buckets[u], 1), :]), start=True, stop=True)
                    last.then_inc(dst_spread, 1)

                def turn_parts(k):
                    pe.wait_ge(scored, k + 3)
                    wait_past(pe, parts_copied, k)
                    for u in range(G):
                        last = nc.tensor.transpose(ps_parts[:, u * P:(u + 1) * P],
                                                   parts[:, u, :, :].rearrange("p a h -> p (a h)"), c.identb[:, :])
                    last.then_inc(parts_turned, 1)

                def mask(k, slot):
                    pe.wait_ge(parts_copied, k + 1)
                    for u in range(G):
                        pe.wait_ge(reduced, k * G + (u + 1))
                        for hd in range(H):
                            at = big[u % 2][:, hd * P:(hd + 1) * P]
                            nc.tensor.matmul(at, c.identb[:, :], other[:, slot, u, :], start=True, stop=False)
                            last = nc.tensor.matmul(at, sel[:, hd, :], partsT[:, u * P:(u + 1) * P],
                                                    start=False, stop=True)
                        last.then_inc(masked, 1)

                for k in range(2):
                    turn_hots(k, k)
                    spread(k)
                turn_parts(0)

                def step(g, hh):
                    k = g * 4 + hh
                    if there(k + 2):
                        turn_hots(k + 2, hh % 2)
                    mask(k, hh)
                    if there(k + 2):
                        spread(k + 2)
                    if there(k + 1):
                        turn_parts(k + 1)

                each_half(nc.tensor, step)

            @block.vector
            def _(dve):
                dve.wait_ge(sel_index, 1)
                nc.vector.tensor_scalar(sel_a, sel_v, 0.0, None, ALU.is_equal)
                dve.drain()
                nc.vector.scalar_tensor_tensor(out=sel_a, in0=sel_v, scalar=float(H), in1=sel_a,
                                               op0=ALU.is_equal, op1=ALU.add)
                dve.drain()
                nc.vector.scalar_tensor_tensor(out=sel[:, :, :], in0=sel_v, scalar=float(2 * H),
                                               in1=sel_a, op0=ALU.is_equal, op1=ALU.add)
                dve.sem_inc(scored, 2)
                dve.sem_inc(reduced, 2)
                dve.sem_inc(topped, 1)
                dve.drain().then_inc(ready, 1)

                def one_hots(k, h):
                    for u in range(G):
                        last = nc.vector.tensor_scalar(hot[:, h, u, :], c.iota[:, :],
                                                       order.local[:, bass.ds(k * G + u, 1)], None, ALU.is_equal)
                    last.then_inc(hot_made, 1)

                def score_half(k, h, landed_at):
                    if R > 1:
                        nc.vector.tensor_tensor(
                            typed[:, :, :], order.type8[:, bass.ds(k * G, G)].rearrange("p (u o) -> p u o", o=1).broadcast_to([P, G, R]),
                            c.iota[:, 0:R].rearrange("p (o r) -> p o r", o=1).broadcast_to([P, G, R]), ALU.is_equal)
                        dve.drain()
                    dve.wait_ge(dst_spread, k + 1)
                    if R > 1:
                        nc.vector.tensor_tensor(
                            picked[:, :, :, :], ps_dst[:, 0:G * R * H].rearrange("p (u r h) -> p u r h", u=G, r=R),
                            typed[:, :, :].rearrange("p u (r o) -> p u r o", o=1).broadcast_to([P, G, R, H]), ALU.mult)
                        dve.drain()
                        nc.vector.reduce_sum(s[:, :, :], picked[:, :, :, :].rearrange("p u r h -> p u h r"), AX_X)
                        dve.drain()
                    dve.wait_ge(landed[h], landed_at)
                    near = s[:, :, :] if R > 1 else ps_dst[:, 0:G * H].rearrange("p (u h) -> p u h", u=G)
                    nc.vector.tensor_tensor(s[:, :, :], near, src[:, h, :, :], ALU.add)
                    dve.drain()
                    out = score[:, bass.ds(k * G, G), :]
                    nc.vector.scalar_tensor_tensor(out=out, in0=s[:, :, :], scalar=0.2, in1=s[:, :, :],
                                                   op0=ALU.mult, op1=ALU.max)
                    dve.drain()
                    wait_past(dve, parts_turned, k)
                    nc.vector.tensor_scalar(parts[:, :, 0, :], out, 1.0, None, ALU.mult)
                    dve.drain()
                    nc.vector.tensor_tensor(rest[:, :, :], out, parts[:, :, 0, :], ALU.subtract)
                    dve.drain()
                    nc.vector.tensor_copy(parts[:, :, 1, :], rest[:, :, :])
                    dve.drain()
                    nc.vector.tensor_tensor(parts[:, :, 2, :], rest[:, :, :], parts[:, :, 1, :], ALU.subtract)
                    dve.drain().then_inc(scored, 1)

                one_hots(0, 0)
                one_hots(1, 1)
                score_half(0, 0, 16 * G)
                one_hots(2, 0)
                score_half(1, 1, 16 * G)

                def step(g, hh):
                    k = g * 4 + hh
                    for u in range(G):
                        dve.wait_ge(masked, k * G + (4 * G + u + 1))
                        nc.vector.reduce_max(tile_top[:, u, :], big[u % 2][:, :].rearrange("p (h e) -> p h e", h=H),
                                             AX_X).then_inc(reduced, 1)
                    if there(k + 3):
                        one_hots(k + 3, (hh + 3) % 2)
                    buckets = buckets_of(nc, mybir.EngineType.DVE, order, k * G)
                    dve.wait_ge(reduced, k * G + (G + 2))
                    for u in range(G):
                        dve.wait_ge(topped, k * G + (u + 1))
                        a = flat(top[:, bass.ds(buckets[u], 1), :])
                        nc.vector.tensor_tensor(a, a, tile_top[:, u, :], ALU.max).then_inc(topped, 1)
                    if there(k + 2):
                        score_half(k + 2, hh % 2, g * (32 * G) + ((hh + 2) // 2 + 1) * 16 * G)

                each_half(nc.vector, step)


def attention_sum(nc, tag, c, order, index, table, width, H, score, top, acc, x):
    cols = width + H
    with Box(nc, tag) as box:
        room = x[:, :, :].rearrange("p b d -> p (b d)")
        rows = room[:, 0:4 * G * ACCW].rearrange("p (u c) -> p u c", c=ACCW)
        hot = room[:, 4 * G * ACCW:4 * G * (ACCW + P)].rearrange("p (u n) -> p u n", n=P)
        hotT = box.sb("hotT", [P, G, P], BF16)
        near = box.sb("near", [P, G, H])
        below = box.sb("below", [P, 2, G, H])
        idx = box.sb("idx", [P, 4, G], I32)
        ps_hot = box.ps("ps_hot", [P, G, P])
        ps_top = box.ps("ps_top", [P, 512])
        part = [box.ps(f"part{k}", [P, 512]) for k in range(4)]
        names = ("ready", "held", "staged", "hot_made", "hot_turned", "hot_copied", "top_spread", "lowered", "weighed",
                 "messages", "summed", "added")
        (ready, held, staged, hot_made, hot_turned, hot_copied, top_spread, lowered, weighed, messages, summed,
         added) = (box.sem(n) for n in names)
        landed = [box.sem(f"landed{h}") for h in range(4)]
        with nc.Block() as block:

            @block.gpsimd
            def _(pool):
                pool.wait_ge(ready, 1)

                def gather(g, hh):
                    k = g * 4 + hh
                    pool.wait_ge(staged, k + 1)
                    for u in range(G):
                        if u % 4 == 0:
                            hold(pool, summed, k * G + (u + 4), held)
                        pool.indirect_dma_start(
                            out=rows[:, hh * G + u, 0:width], out_offset=None, in_=table,
                            in_offset=bass.IndirectOffsetOnAxis(ap=idx[:, hh, u:u + 1], axis=0)).then_inc(landed[hh], 16)

                each_half(nc.gpsimd, gather)

            @block.scalar
            def _(act):
                act.wait_ge(ready, 1)

                def stage_indices(k, slot):
                    nc.scalar.copy(idx[:, slot, :], index[:, bass.ds(k * G, G)]).then_inc(staged, 1)

                def weigh(k, slot):
                    act.wait_ge(hot_turned, k + 1)
                    wait_past(act, top_spread, k)
                    nc.scalar.copy(hotT[:, :, :], ps_hot[:, :, :]).then_inc(hot_copied, 1)
                    act.wait_ge(lowered, k + 1)
                    act.wait_ge(summed, k * G + G)
                    nc.scalar.activation(rows[:, slot * G:slot * G + G, width:cols], below[:, slot % 2, :, :],
                                         ACT.Exp).then_inc(weighed, 1)

                for k in range(3):
                    stage_indices(k, k)
                weigh(0, 0)
                weigh(1, 1)

                def step(g, hh):
                    k = g * 4 + hh
                    if there(k + 3):
                        wait_past(act, messages, k * 2)
                        stage_indices(k + 3, (hh + 3) % 4)
                    if there(k + 2):
                        weigh(k + 2, (hh + 2) % 4)

                each_half(nc.scalar, step)

            @block.tensor
            def _(pe):
                pe.wait_ge(ready, 1)
                pe.sem_inc(summed, 4 * G)

                def turn_hots(k, slot):
                    pe.wait_ge(hot_made, k + 1)
                    wait_past(pe, hot_copied, k)
                    for u in range(G):
                        last = nc.tensor.transpose(ps_hot[:, u, :], hot[:, slot * G + u, :], c.ident[:, :])
                    last.then_inc(hot_turned, 1)

                def spread(k):
                    buckets = buckets_of(nc, mybir.EngineType.PE, order, k * G)
                    pe.wait_ge(hot_copied, k + 1)
                    wait_past(pe, lowered, k)
                    for u in range(G):
                        last = nc.tensor.matmul(ps_top[:, u * 3 * H:(u + 1) * 3 * H], hotT[:, u, :],
                                                flat(top[:, bass.ds(buckets[u], 1), :]), start=True, stop=True)
                    last.then_inc(top_spread, 1)

                for k in range(2):
                    turn_hots(k, k)
                    spread(k)

                def step(g, hh):
                    k = g * 4 + hh
                    if there(k + 2):
                        turn_hots(k + 2, (hh + 2) % 4)
                    for u in range(G):
                        if u % 4 == 0:
                            pe.wait_ge(messages, k * 2 + (u // 4 + 1))
                        pe.wait_ge(added, k * G + (u + 1))
                        nc.tensor.matmul(part[u % 4][:, 0:cols], hot[:, hh * G + u, :], rows[:, hh * G + u, 0:cols],
                                         start=True, stop=True).then_inc(summed, 1)
                    if there(k + 2):
                        spread(k + 2)

                each_half(nc.tensor, step)

            @block.vector
            def _(dve):
                nc.vector.memset(acc[:, :, :], 0.0)
                dve.sem_inc(added, 4)
                dve.drain().then_inc(ready, 1)

                def one_hots(k, slot):
                    for u in range(G):
                        last = nc.vector.tensor_scalar(hot[:, slot * G + u, :], c.iota[:, :],
                                                       order.local[:, bass.ds(k * G + u, 1)], None, ALU.is_equal)
                    last.then_inc(hot_made, 1)

                def lower(k, h):
                    dve.wait_ge(top_spread, k + 1)
                    nc.vector.reduce_sum(near[:, :, :], ps_top[:, 0:G * 3 * H].rearrange("p (u a h) -> p u h a", u=G, a=3), AX_X)
                    dve.drain()
                    nc.vector.tensor_tensor(below[:, h, :, :], score[:, bass.ds(k * G, G), :], near[:, :, :], ALU.subtract)
                    dve.drain()
                    nc.vector.tensor_scalar(below[:, h, :, :], below[:, h, :, :], 0.0, None, ALU.min).then_inc(lowered, 1)

                def weigh_rows(k, slot, landed_at):
                    dve.wait_ge(landed[slot], landed_at)
                    dve.wait_ge(weighed, k + 1)
                    for u in range(slot * G, slot * G + G, 4):
                        m = rows[:, u:u + 4, 0:width].rearrange("p u (h d) -> p u h d", h=H)
                        w = rows[:, u:u + 4, width:cols].rearrange("p u (h o) -> p u h o", o=1)
                        nc.vector.tensor_tensor(m, m, w.broadcast_to([P, 4, H, width // H]), ALU.mult).then_inc(messages, 1)

                for k in range(3):
                    one_hots(k, k)
                lower(0, 0)
                lower(1, 1)
                weigh_rows(0, 0, 16 * G)

                def step(g, hh):
                    k = g * 4 + hh
                    if there(k + 1):
                        weigh_rows(k + 1, (hh + 1) % 4, g * (16 * G) + 16 * G * ((hh + 1) // 4 + 1))
                    buckets = buckets_of(nc, mybir.EngineType.DVE, order, k * G)
                    for u in range(G):
                        dve.wait_ge(summed, k * G + (4 * G + u + 1))
                        dve.wait_ge(added, k * G + (u + 4))
                        a = acc[:, bass.ds(buckets[u], 1), 0:cols].rearrange("p o c -> p (o c)")
                        nc.vector.tensor_tensor(a, a, part[u % 4][:, 0:cols], ALU.add).then_inc(added, 1)
                    if there(k + 3):
                        one_hots(k + 3, (hh + 3) % 4)
                    if there(k + 2):
                        lower(k + 2, hh % 2)

                each_half(nc.vector, step)


def split_top(nc, tag, top, parts, rest):
    def body(dve):
        nc.vector.tensor_copy(parts[:, :, 0, :], top[:, :, :])
        dve.drain()
        nc.vector.tensor_tensor(rest[:, :, :], top[:, :, :], parts[:, :, 0, :], ALU.subtract)
        dve.drain()
        nc.vector.tensor_copy(parts[:, :, 1, :], rest[:, :, :])
        dve.drain()
        nc.vector.tensor_tensor(parts[:, :, 2, :], rest[:, :, :], parts[:, :, 1, :], ALU.subtract)

    on_vector(nc, tag, [], body)


def load_nodes(nc, tag, x, x_d):
    with Box(nc, tag) as box:
        cleared, loaded = box.sem("cleared"), box.sem("loaded")
        with nc.Block() as block:

            @block.vector
            def _(dve):
                nc.vector.memset(x[:, NB - 1, :], 0.0)
                dve.drain().then_inc(cleared, 1)

            @block.sync
            def _(sp):
                sp.wait_ge(cleared, 1)
                sp.dma_start(x[:, 0:NB - 1, :], x_d[0:(NB - 1) * P, :].rearrange("(b p) d -> p b d", p=P)).then_inc(loaded, 16)
                sp.dma_start(x[0:LAST, NB - 1, :], x_d[(NB - 1) * P:N, :]).then_inc(loaded, 16)
                sp.wait_ge(loaded, 32)


def store_nodes(nc, tag, src, dst_d, rows=NPAD):
    with Box(nc, tag) as box:
        stored = box.sem("stored")
        full = NB if rows == NPAD else NB - 1
        with nc.Block() as block:

            @block.sync
            def _(sp):
                sp.dma_start(dst_d[0:full * P, :].rearrange("(b p) d -> p b d", p=P), src[:, 0:full, :]).then_inc(stored, 16)
                if full < NB:
                    sp.dma_start(dst_d[full * P:N, :], src[0:LAST, full, :]).then_inc(stored, 16)
                sp.wait_ge(stored, 16 * (1 + (full < NB)))


def sage(nc, tag, c, x, h, acc, own_d, wl_d, wr_d, b_d, residual):
    with Box(nc, tag) as box:
        wlT = box.sb("wlT", [P, 2, D])
        wrT = box.sb("wrT", [P, 2, D])
        bias = box.sb("bias", [P, D])
        transpose_weights(nc, tag + "w", c, [(wl_d, wlT), (wr_d, wrT)])

        def before(dve):
            if c.rdeg_made:
                return
            nc.vector.tensor_scalar(c.rdeg[:, :], acc[:, :, D], 1.0, None, ALU.max)
            dve.drain()
            nc.vector.reciprocal(c.rdeg[:, :], c.rdeg[:, :])
            c.rdeg_made = True

        def finish(dve, b, ps):
            if not residual:
                out = flat(h[:, bass.ds(b, 1), :])
                nc.vector.tensor_tensor(out, ps, bias[:, :], ALU.add)
                dve.drain()
                return nc.vector.tensor_scalar(out, out, 0.0, None, ALU.max)
            out = flat(x[:, bass.ds(b, 1), :])
            nc.vector.tensor_tensor(out, out, ps, ALU.add)
            dve.drain()
            return nc.vector.tensor_tensor(out, out, bias[:, :], ALU.add)

        project(nc, tag + "p", c, [(acc, 2, c.rdeg), (h, 2, None)],
                [wlT[:, 0, :], wlT[:, 1, :], wrT[:, 0, :], wrT[:, 1, :]], D, finish, before=before,
                load=[(bias[:, :], b_d.rearrange("(o d) -> o d", o=1).broadcast_to([P, D])),
                      (h[:, :, :], own_d.rearrange("(b p) d -> p b d", p=P))])


def fold_attention(nc, tag, c, lhs, attn_ds, heads, width, dst):
    blocks, rels = heads * width // P, len(lhs[0])
    with Box(nc, tag) as box:
        offset = box.sb("offset", [P, blocks, heads])
        inside = box.sb("inside", [P, blocks, heads])
        attn = box.sb("attn", [P, 2, blocks])
        spread = box.sb("spread", [P, blocks, 2, heads])
        folded = [box.ps(f"folded{k}", [P, 512]) for k in range(len(lhs))]
        made, loaded, ready, done = (box.sem(n) for n in ("made", "loaded", "ready", "done"))
        with nc.Block() as block:

            @block.gpsimd
            def _(pool):
                pool.iota(offset[:, :, :], pattern=[[P, blocks], [-width, heads]], base=0, channel_multiplier=1,
                          allow_small_or_imprecise_dtypes=True).then_inc(made, 1)

            @block.sync
            def _(sp):
                for s, d in enumerate(attn_ds):
                    flat_d = d.rearrange("h d -> (h d)")
                    for k in range(blocks):
                        sp.dma_start(attn[:, s, k:k + 1],
                                     flat_d[k * P:(k + 1) * P].rearrange("(p c) -> p c", c=1)).then_inc(loaded, 16)

            @block.vector
            def _(dve):
                dve.wait_ge(made, 1)
                dve.wait_ge(loaded, 32 * blocks)
                nc.vector.tensor_scalar(inside[:, :, :], offset[:, :, :], 0.0, None, ALU.is_ge)
                dve.drain()
                nc.vector.scalar_tensor_tensor(out=inside[:, :, :], in0=offset[:, :, :], scalar=float(width),
                                               in1=inside[:, :, :], op0=ALU.is_lt, op1=ALU.mult)
                dve.drain()
                for s in range(2):
                    for k in range(blocks):
                        nc.vector.tensor_scalar(spread[:, k, s, :], inside[:, k, :], attn[:, s, k:k + 1], None, ALU.mult)
                dve.drain().then_inc(ready, 1)
                dve.wait_ge(done, 1)
                n = rels * 2 * heads
                for fc in range(len(lhs)):
                    for s in range(2):
                        nc.vector.tensor_copy(
                            dst[:, fc, s, :, :],
                            folded[fc][:, 0:n].rearrange("p (r s h) -> p r s h", r=rels, s=2)[:, :, s, :])

            @block.tensor
            def _(pe):
                pe.wait_ge(ready, 1)
                for fc in range(len(lhs)):
                    for r in range(rels):
                        at = r * 2 * heads
                        for k in range(blocks):
                            last = nc.tensor.matmul(folded[fc][:, at:at + 2 * heads], lhs[fc][r][k],
                                                    spread[:, k, :, :].rearrange("p s h -> p (s h)"),
                                                    start=(k == 0), stop=(k == blocks - 1))
                last.then_inc(done, 1)


def relation_tables(nc, tag, c, h, wT, scoreT, rows_d, src_scores, dst_scores):
    RH = R8 * H1
    with Box(nc, tag) as box:
        stage = box.sb("stage", [P, 4, D])
        turned_sb = box.sb("turned_sb", [P, 4, D])
        out = box.sb("out", [P, 2, R8 * D])
        turned = [box.ps(f"turned{k}", [P, 512]) for k in range(2)]
        result = [box.ps(f"result{k}", [P, 512]) for k in range(5)]
        ready, staged, turns, copied, made_a, made_v, product = (
            box.sem(n) for n in ("ready", "staged", "turned", "copied", "made_a", "made_v", "product"))
        stored, slots_free = box.sem("stored"), box.sem("slots_free")
        with nc.Block() as block:

            @block.sync
            def _(sp):
                with nc.sync.Fori(0, NI) as i:
                    for u in range(U):
                        b = i * U + u
                        sp.wait_ge(made_a, b * 2 + 4)
                        sp.wait_ge(made_v, b * 3 + 5 + 3)
                        sp.dma_start(rows_d[bass.ds(b * P, P), :], out[:, u % 2, :]).then_inc(stored, 16)
                        sp.wait_ge(stored, b * 16 + 16)
                        sp.sem_inc(slots_free, 1)

            @block.scalar
            def _(act):
                act.wait_ge(ready, 1)

                def stage_block(b, u):
                    act.wait_ge(copied, b + (U - 2))
                    nc.scalar.copy(stage[:, u % 4, :], flat(h[:, bass.ds(b, 1), 0:D])).then_inc(staged, 1)

                with nc.scalar.Fori(0, NI) as i:
                    stage_block(i * U, 0)
                    for u in range(U):
                        b = i * U + u
                        if u + 1 < U:
                            stage_block(b + 1, u + 1)
                        act.wait_ge(slots_free, b + (2 if u == 0 else 1))
                        for j in range(2):
                            act.wait_ge(product, b * 5 + (j + 1))
                            nc.scalar.copy(out[:, u % 2, j * 512:(j + 1) * 512], result[j][:, :]).then_inc(made_a, 1)

            @block.tensor
            def _(pe):
                def turn(b, u):
                    pe.wait_ge(staged, b + 1)
                    pe.wait_ge(copied, b + (U if u == 0 else U - 1))
                    for k in range(2):
                        last = nc.tensor.transpose(turned[u % 2][:, k * P:(k + 1) * P],
                                                   stage[:, u % 4, k * P:(k + 1) * P], c.ident[:, :])
                    last.then_inc(turns, 1)

                pe.wait_ge(ready, 1)
                with nc.tensor.Fori(0, NI) as i:
                    turn(i * U, 0)
                    for u in range(U):
                        b = i * U + u
                        if u + 1 < U:
                            turn(b + 1, u + 1)
                        pe.wait_ge(copied, b + U + 1)
                        for j in range(5):
                            if j < 2:
                                pe.wait_ge(made_a, b * 2 + 2)
                            else:
                                pe.wait_ge(made_v, b * 3 + 5)
                            w = wT[:, :, j * 512:(j + 1) * 512] if j < 4 else scoreT
                            n = 512 if j < 4 else 2 * RH
                            for k in range(2):
                                last = nc.tensor.matmul(result[j][:, 0:n], turned_sb[:, u % 4, k * P:(k + 1) * P],
                                                        w[:, k, :], start=(k == 0), stop=(k == 1))
                            last.then_inc(product, 1)

            @block.vector
            def _(dve):
                dve.sem_inc(copied, U)
                dve.sem_inc(made_v, 5)
                dve.sem_inc(made_a, 2)
                dve.sem_inc(slots_free, 2)
                dve.drain().then_inc(ready, 1)

                def copy_turned(b, u):
                    dve.wait_ge(turns, b + 1)
                    nc.vector.tensor_copy(turned_sb[:, u % 4, :], turned[u % 2][:, 0:D]).then_inc(copied, 1)

                with nc.vector.Fori(0, NI) as i:
                    copy_turned(i * U, 0)
                    for u in range(U):
                        b = i * U + u
                        if u + 1 < U:
                            copy_turned(b + 1, u + 1)
                        dve.wait_ge(slots_free, b + (2 if u == 0 else 1))
                        for j in range(2, 4):
                            dve.wait_ge(product, b * 5 + (j + 1))
                            nc.vector.tensor_copy(out[:, u % 2, j * 512:(j + 1) * 512], result[j][:, :]).then_inc(made_v, 1)
                        dve.wait_ge(product, b * 5 + 5)
                        nc.vector.tensor_scalar(flat(src_scores[:, bass.ds(b, 1), :]), result[4][:, 0:RH], 1.0, None, ALU.mult)
                        nc.vector.tensor_scalar(flat(dst_scores[:, bass.ds(b, 1), :]), result[4][:, RH:2 * RH], 1.0,
                                                None, ALU.mult)
                        dve.drain().then_inc(made_v, 1)


def on_vector(nc, tag, loads, body):
    with Box(nc, tag) as box:
        loaded = box.sem("loaded")
        with nc.Block() as block:

            @block.sync
            def _(sp):
                for dst, src in loads:
                    sp.dma_start(dst, src).then_inc(loaded, 16)

            @block.vector
            def _(dve):
                if loads:
                    dve.wait_ge(loaded, 16 * len(loads))
                body(dve)


def row_bias(d, n):
    return d.rearrange("(o d) -> o d", o=1).broadcast_to([P, n])


def over_nodes(ap, n):
    return ap.rearrange("p (o d) -> p o d", o=1).broadcast_to([P, NB, n])


def layer1(nc, c, a, x, acc, order):
    rows_d = nc.dram_tensor("l1_rows", [NPAD, R8 * D], F32).ap()
    src_d = nc.dram_tensor("l1_src", [NPAD, R8 * H1], F32).ap()
    with Box(nc, "l1") as box:
        dst_scores = box.sb("dst_scores", [P, NB, R8 * H1])
        with Box(nc, "l1t") as b:
            wT = b.sb("wT", [P, 2, R8 * D])
            scoreT = b.sb("scoreT", [P, 2, 2 * R8 * H1])
            src_scores = b.sb("src_scores", [P, NB, R8 * H1])
            raw = acc[:, 0:2 * R8, 0:D]
            transpose_weights(nc, "l1x", c, [(a["L1_gnn_W"].rearrange("r o f -> (r o) f"), wT)], [raw])
            fold_attention(nc, "l1f", c,
                           [[[raw[:, 2 * r + k, fc * P:(fc + 1) * P] for k in range(2)] for r in range(R8)] for fc in range(2)],
                           (a["L1_gnn_attn_src"], a["L1_gnn_attn_dst"]), H1, D1,
                           scoreT[:, :, :].rearrange("p k (s r h) -> p k s r h", s=2, r=R8))
            normalize(nc, "n1", c, x, acc, None)
            relation_tables(nc, "l1p", c, acc, wT, scoreT, rows_d, src_scores, dst_scores)
            store_nodes(nc, "l1s", src_scores, src_d)
        score = box.sb("score", [P, T + G, H1])
        top = box.sb("top", [P, NB, H1])
        on_vector(nc, "l1z", [], lambda dve: nc.vector.memset(top[:, :, :], 0.0))
        attention_max(nc, "l1m", c, order, order.rel_other, src_d.rearrange("n (r h) -> (n r) h", r=R8), H1, R8,
                      dst_scores, score, top, x, c.x_d, later=(c.todo_d, c.rec_src_d))
        parts, rest = box.sb("parts", [P, NB, 3 * H1], BF16), box.sb("rest", [P, NB, H1])
        split_top(nc, "l1b", top, parts[:, :, :].rearrange("p b (a h) -> p b a h", a=3), rest)
        attention_sum(nc, "l1a", c, order, order.rel_other, rows_d.rearrange("n (r d) -> (n r) d", r=R8), D, H1,
                      score, parts, acc, x)
        rden = box.sb("rden", [P, NB, H1])

        def divide(dve):
            nc.vector.tensor_scalar(rden[:, :, :], acc[:, :, D:D + H1], 1e-12, None, ALU.add)
            dve.drain()
            nc.vector.reciprocal(rden[:, :, :], rden[:, :, :])
            dve.drain()
            m = acc[:, :, 0:D].rearrange("p b (h d) -> p b h d", h=H1)
            r = rden[:, :, :].rearrange("p b (h o) -> p b h o", o=1).broadcast_to([P, NB, H1, D1])
            nc.vector.tensor_tensor(m, m, r, ALU.mult)
            dve.drain()
            nc.vector.tensor_tensor(x[:, :, :], x[:, :, :], acc[:, :, 0:D], ALU.add)

        on_vector(nc, "l1d", [(x[:, :, :], c.x_d.rearrange("(b p) d -> p b d", p=P))], divide)


def layer2(nc, c, a, x, acc, by_dst, by_src):
    support_d = nc.dram_tensor("support", [NPAD, D], F32).ap()
    with Box(nc, "l2u") as box:
        records = box.sb("records", [P, T, 4], I32)
        scratch = box.sb("scratch", [P, T])
        alpha = box.sb("alpha", [P, R11])
        on_vector(nc, "l2u", [(records[:, :, :], c.rec_src_d[0:P * T, :].rearrange("(p t) f -> p t f", p=P)),
                              (alpha[:, :], a["L2_gnn_alpha"].rearrange("r o -> o r").broadcast_to([P, R11]))],
                  lambda dve: unpack(nc, dve, records, alpha, scratch, by_src))
    with Box(nc, "l2") as box:
        w = box.sb("w", [P, 2, D])
        bias = box.sb("bias", [P, D])
        normalize(nc, "n2", c, x, acc, None)
        project(nc, "l2p", c, [(acc, 2, None)], [w[:, 0, :], w[:, 1, :]], D,
                lambda dve, b, ps: nc.vector.tensor_scalar(flat(acc[:, bass.ds(b, 1), 0:D]), ps, 1.0, None, ALU.mult),
                load=[(w[:, :, :], a["L2_gnn_weight"].rearrange("(c p) o -> p c o", p=P)),
                      (bias[:, :], row_bias(a["L2_gnn_bias"], D))])
        store_nodes(nc, "l2s", acc[:, :, 0:D], support_d)
        gather_sum(nc, "l2d", c, by_dst, by_dst.other, support_d, acc, D, weighted=True)
        gather_sum(nc, "l2r", c, by_src, by_src.other, support_d, acc, D, weighted=True, clear=False)

        def add(dve):
            nc.vector.tensor_tensor(acc[:, :, 0:D], acc[:, :, 0:D], over_nodes(bias[:, :], D), ALU.add)
            dve.drain()
            nc.vector.tensor_tensor(x[:, :, :], x[:, :, :], acc[:, :, 0:D], ALU.add)

        on_vector(nc, "l2a", [], add)


def layer3(nc, c, a, x, acc, order):
    rows_d = nc.dram_tensor("l3_rows", [NPAD, F3], F32).ap()
    src_d = nc.dram_tensor("l3_src", [NPAD, H3], F32).ap()
    with Box(nc, "l3") as box:
        w = box.sb("w", [P, 2, F3 + 2 * H3])
        wT = box.sb("wT", [P, 1, D])
        folded = box.sb("folded", [P, 2, 2, 1, H3])
        dst_scores = box.sb("dst_scores", [P, NB, H3])
        score = box.sb("score", [P, T + G, H3])
        top = box.sb("top", [P, NB, H3])
        rden = box.sb("rden", [P, NB, H3])
        lin = box.sb("lin", [P, D])
        lin_b = box.sb("lin_b", [P, D])
        gat_b = box.sb("gat_b", [P, F3])
        w_d = a["L3_gnn_W"]
        transpose_weights(nc, "l3x", c, [(w_d, wT)])
        fold_attention(nc, "l3f", c, [[[wT[:, 0, fc * P:(fc + 1) * P]]] for fc in range(2)],
                       (a["L3_gnn_attn_l"], a["L3_gnn_attn_r"]), H3, D3, folded)

        def prepare(dve):
            nc.vector.tensor_copy(w[:, :, F3:], folded[:, :, :, :, :].rearrange("p k s r h -> p k (s r h)"))
            nc.vector.memset(top[:, :, :], -NEG)

        on_vector(nc, "l3w", [(w[:, :, 0:F3], w_d.rearrange("(c p) o -> p c o", p=P)),
                              (lin[:, :], a["L3_gnn_lin_W"]), (lin_b[:, :], row_bias(a["L3_gnn_lin_b"], D)),
                              (gat_b[:, :], row_bias(a["L3_gnn_gat_bias"], F3))], prepare)
        normalize(nc, "n3", c, x, acc, None)
        cols = F3 + 2 * H3
        project(nc, "l3p", c, [(acc, 2, None)], [w[:, 0, :], w[:, 1, :]], cols,
                lambda dve, b, ps: nc.vector.tensor_scalar(flat(acc[:, bass.ds(b, 1), 0:cols]), ps, 1.0, None, ALU.mult))
        store_nodes(nc, "l3s", acc[:, :, 0:F3], rows_d)
        store_nodes(nc, "l3t", acc[:, :, F3:F3 + H3], src_d)
        on_vector(nc, "l3c", [], lambda dve: nc.vector.tensor_copy(dst_scores[:, :, :], acc[:, :, F3 + H3:cols]))
        attention_max(nc, "l3m", c, order, order.other, src_d, H3, 1, dst_scores, score, top, x, c.x_d)
        parts, rest = box.sb("parts", [P, NB, 3 * H3], BF16), box.sb("rest", [P, NB, H3])
        split_top(nc, "l3b", top, parts[:, :, :].rearrange("p b (a h) -> p b a h", a=3), rest)
        attention_sum(nc, "l3a", c, order, order.other, rows_d, F3, H3, score, parts, acc, x)

        def divide(dve):
            nc.vector.tensor_scalar(rden[:, :, :], acc[:, :, F3:F3 + H3], 1e-30, None, ALU.max)
            dve.drain()
            nc.vector.reciprocal(rden[:, :, :], rden[:, :, :])
            dve.drain()
            m = acc[:, :, 0:F3].rearrange("p b (h d) -> p b h d", h=H3)
            r = rden[:, :, :].rearrange("p b (h o) -> p b h o", o=1).broadcast_to([P, NB, H3, D3])
            nc.vector.tensor_tensor(m, m, r, ALU.mult)
            dve.drain()
            nc.vector.tensor_tensor(acc[:, :, 0:F3], acc[:, :, 0:F3], over_nodes(gat_b[:, :], F3), ALU.add)
            dve.drain()
            nc.vector.tensor_scalar(acc[:, :, 0:F3], acc[:, :, 0:F3], 0.0, None, ALU.max)

        on_vector(nc, "l3d", [(x[:, :, :], c.x_d.rearrange("(b p) d -> p b d", p=P))], divide)
        relu = box.sb("relu", [P, 2, D])

        def finish(dve, b, ps):
            r = relu[:, 0, :]
            nc.vector.tensor_tensor(r, ps, lin_b[:, :], ALU.add)
            dve.drain()
            out = flat(x[:, bass.ds(b, 1), :])
            nc.vector.scalar_tensor_tensor(out=out, in0=r, scalar=0.0, in1=out, op0=ALU.max, op1=ALU.add)
            return dve.drain()

        project(nc, "l3o", c, [(acc, 1, None)], [lin[:, :]], D, finish)


def build(nc, a, out_d, layers=4):
    c = Consts()
    c.x_d = nc.dram_tensor("x_parked", [NPAD, D], F32).ap()
    with Box(nc, "k") as top:
        setup_constants(nc, top, c)
        by_dst, by_src = Order(), Order()
        for name, o in (("dst", by_dst), ("src", by_src)):
            o.tile_bucket = top.sb(f"bucket_{name}", [1, T + RING], I32)
            o.local = top.sb(f"local_{name}", [P, T + G])
            o.weight = top.sb(f"weight_{name}", [P, T + G])
            o.other = top.sb(f"other_{name}", [P, T + RING], I32)
            o.rel_other = o.type8 = None
        by_dst.rel_other = top.sb("rel_other", [P, T + RING], I32)
        by_dst.type8 = top.sb("type8", [P, T + G])
        c.rdeg = top.sb("rdeg", [P, NB])
        c.rdeg_made = False
        rec_dst_d = nc.dram_tensor("rec_dst", [P * T, 4], I32).ap()
        c.rec_src_d = nc.dram_tensor("rec_src", [P * T + (T - EC) * P, 4], I32).ap()
        c.todo_d = nc.dram_tensor("todo", [P, T, 5], I32).ap()
        sort_edges(nc, c, (a["dst"], a["src"]), a["edge_type_8"], a["edge_type_11"], a["L2_gnn_alpha"], rec_dst_d,
                   c.rec_src_d[0:P * T, :], c.todo_d, by_dst, by_src)
        x = top.sb("x", [P, NB, D])
        acc = top.sb("acc", [P, NB, ACCW])
        load_nodes(nc, "ld", x, a["x"])
        h0_d = nc.dram_tensor("h0", [NPAD, D], F32).ap()
        h1_d = nc.dram_tensor("h1", [NPAD, D], F32).ap()
        with Box(nc, "b0") as b:
            h = b.sb("h", [P, NB, D])
            normalize(nc, "n0", c, x, h, h0_d)
        gather_sum(nc, "g0", c, by_dst, by_dst.other, h0_d, acc, D, count=True)
        with Box(nc, "b1") as b:
            h = b.sb("h", [P, NB, D])
            sage(nc, "s0", c, x, h, acc, h0_d, a["L0_gnn_w1_l"], a["L0_gnn_w1_r"], a["L0_gnn_b1"], False)
            store_nodes(nc, "st0", h, h1_d)
        gather_sum(nc, "g1", c, by_dst, by_dst.other, h1_d, acc, D)
        with Box(nc, "b2") as b:
            h = b.sb("h", [P, NB, D])
            sage(nc, "s1", c, x, h, acc, h1_d, a["L0_gnn_w2_l"], a["L0_gnn_w2_r"], a["L0_gnn_b2"], True)
        if layers > 1:
            layer1(nc, c, a, x, acc, by_dst)
        if layers > 2:
            layer2(nc, c, a, x, acc, by_dst, by_src)
        if layers > 3:
            layer3(nc, c, a, x, acc, by_dst)
        store_nodes(nc, "out", x, out_d, rows=N)


_INS = ['x', 'src', 'dst', 'edge_type_11', 'edge_type_8', 'L0_gnn_w1_l', 'L0_gnn_w1_r', 'L0_gnn_b1', 'L0_gnn_w2_l',
        'L0_gnn_w2_r', 'L0_gnn_b2', 'L1_gnn_W', 'L1_gnn_attn_src', 'L1_gnn_attn_dst', 'L2_gnn_weight', 'L2_gnn_bias',
        'L2_gnn_alpha', 'L3_gnn_W', 'L3_gnn_attn_l', 'L3_gnn_attn_r', 'L3_gnn_gat_bias', 'L3_gnn_lin_W', 'L3_gnn_lin_b']
_OUTS = [((N, D), 'float32')]
LAYERS = 4


def kernel(**inputs):
    import numpy as _np
    import concourse.bacc as _bacc
    from concourse import mybir as _mybir
    from concourse.bass_utils import run_bass_kernel_spmd as _run

    nc = _bacc.Bacc("TRN2", target_bir_lowering=False, num_devices=1)
    arrays, args = {}, {}
    for name in _INS:
        a = _np.ascontiguousarray(inputs[name])
        arrays[f"in_{name}_dram"] = a
        args[name] = nc.dram_tensor(f"in_{name}_dram", a.shape, _mybir.dt.from_np(a.dtype), kind="ExternalInput").ap()
    out = nc.dram_tensor("out_0_dram", _OUTS[0][0], _mybir.dt.from_np(_np.dtype(_OUTS[0][1])), kind="ExternalOutput").ap()
    build(nc, args, out, LAYERS)
    r = _run(nc, [arrays], core_ids=[0])
    return r.results[0]["out_0_dram"]
```

```python
import math
from contextlib import ExitStack, contextmanager

import concourse.bass as bass
from concourse import mybir

F32 = mybir.dt.float32
BF16 = mybir.dt.bfloat16
I32 = mybir.dt.int32
ALU = mybir.AluOpType
ACT = mybir.ActivationFunctionType
AX_X = mybir.AxisListType.X

P = 128
N, D, E = 6250, 256, 100000
NB = -(-N // P)
NPAD = NB * P
LAST = N - (NB - 1) * P
EC = E // P
EREST = E - EC * P
CE = EC + 1
G = 8
RING = 2 * G
T = -(-(E // P + NB) // RING) * RING
NIT = T // RING
NH = T // G
U = 7
NI = NB // U
R8, H1, D1 = 8, 8, 32
R11 = 11
H3, D3 = 2, 64
F3 = H3 * D3
BITS = P.bit_length()
ACCW = D + H1
NEG = 1e30
EPS = 1e-5
SCAT_HALVES = ((0, 6), (6, 11))
SG = 11
NSG = EC // SG


class Box:

    def __init__(self, nc, tag):
        self.nc, self.tag, self.stack, self.sems = nc, tag, ExitStack(), []

    def __enter__(self):
        return self

    def __exit__(self, *a):
        if self.sems and a[0] is None:
            self.nc.clear_and_free_semaphores(self.sems)
            self.nc.all_engine_barrier()
        return self.stack.__exit__(*a)

    def sb(self, name, shape, dt=F32):
        return self.stack.enter_context(self.nc.sbuf_tensor(f"{self.tag}_{name}", shape, dt))

    def ps(self, name, shape, dt=F32):
        return self.stack.enter_context(self.nc.psum_tensor(f"{self.tag}_{name}", shape, dt))

    def sem(self, name):
        self.sems.append(self.nc.alloc_semaphore(f"{self.tag}_{name}"))
        return self.sems[-1]


def setup_constants(nc, box, c):
    c.iota = box.sb("iota", [P, P])
    c.ident = box.sb("ident", [P, P])
    c.identb = box.sb("identb", [P, P], BF16)
    c.below = box.sb("below", [P, P])
    c.upto = box.sb("upto", [P, P])
    c.ones = box.sb("ones", [P, P])
    diff = box.sb("diff", [P, P])
    made = box.sem("indices_made")
    with nc.Block() as block:

        @block.gpsimd
        def _(pool):
            pool.iota(c.iota[:, :], pattern=[[1, P]], base=0, channel_multiplier=0,
                      allow_small_or_imprecise_dtypes=True).then_inc(made, 1)
            pool.iota(diff[:, :], pattern=[[1, P]], base=0, channel_multiplier=-1,
                      allow_small_or_imprecise_dtypes=True).then_inc(made, 1)

        @block.vector
        def _(dve):
            nc.vector.memset(c.ones[:, :], 1.0)
            dve.wait_ge(made, 2)
            nc.vector.tensor_scalar(c.ident[:, :], diff[:, :], 0.0, None, ALU.is_equal)
            nc.vector.tensor_scalar(c.identb[:, :], diff[:, :], 0.0, None, ALU.is_equal)
            nc.vector.tensor_scalar(c.below[:, :], diff[:, :], 0.0, None, ALU.is_gt)
            nc.vector.tensor_scalar(c.upto[:, :], diff[:, :], 0.0, None, ALU.is_ge)


def sort_edges(nc, c, ends, t8_d, t11_d, alpha_d, rec_d, pads_d, todo_d, by_dst, by_src,
               x, x_d, h0_d):
    with Box(nc, "so") as box:
        raw = [box.sb(f"end{k}", [P, CE], I32) for k in range(2)]
        t8 = box.sb("t8", [P, CE], I32)
        t11 = box.sb("t11", [P, CE], I32)
        bucket_i = box.sb("bucket_i", [P, CE], I32)
        bucket = box.sb("bucket", [P, CE])
        bucketb = box.sb("bucketb", [P, CE], BF16)
        matchb = box.sb("matchb", [P, CE], BF16)
        rec = box.sb("rec", [P, CE, 4], I32)
        todo = box.sb("todo", [P, T, 5], I32)
        spare = box.sb("spare", [P, T], I32)
        pads = box.sb("pads", [P, T, 4], I32)
        onesw = box.sb("onesw", [P, CE], BF16)
        match = box.sb("match", [P, CE])
        run = box.sb("run", [P, CE])
        pos = box.sb("pos", [P, CE])
        posi = box.sb("posi", [P, CE], I32)
        slot_t = box.sb("slot_t", [P, CE], I32)
        addr = box.sb("addr", [P, CE], I32)
        cnt = box.sb("cnt", [P, NB])
        tot_i = box.sb("tot_i", [P, NB], I32)
        tiles = box.sb("tiles", [P, NB])
        bucket_end = box.sb("bucket_end", [P, NB])
        start = box.sb("start", [P, NB])
        nT_i = box.sb("nT_i", [NB, 1], I32)
        nT = box.sb("nT", [NB, 1])
        endT = box.sb("endT", [NB, 1])
        tile_no = box.sb("tile_no", [NB, T])
        after = box.sb("after", [NB, T])
        alpha = box.sb("alpha", [P, R11])
        scratch = box.sb("scratch", [P, T])
        rec_ring = box.sb("rec_ring", [P, SG, 4], I32)
        addr_ring = box.sb("addr_ring", [P, SG], I32)
        ps_tot = box.ps("ps_tot", [P, 512])[:, 0:NB]
        ps_low = box.ps("ps_low", [P, 512])[:, 0:NB]
        ps_nT = box.ps("ps_nT", [P, 512])[0:NB, 0:1]
        ps_end = box.ps("ps_end", [P, 512])[0:NB, 0:1]
        ps_bk = box.ps("ps_bk", [P, 512])[0:1, 0:T // 2]
        ps_bk2 = box.ps("ps_bk2", [P, 512])[0:1, 0:T // 2]
        filled, loaded, padded, counted, summed, nt_ready, end_summed, after_ready, bk_summed, iota_made = (
            box.sem(x) for x in ("filled", "loaded", "padded", "counted", "summed", "nt_ready",
                                 "end_summed", "after_ready", "bk_summed", "iota_made"))
        placed, ring_full, reloaded = box.sem("placed"), box.sem("ring_full"), box.sem("reloaded")
        scattered = [box.sem(f"scattered{h}") for h in range(2)]
        last_out, held, todo_ready, todo_stored, x_loaded, h_made, h_stored = (
            box.sem(n) for n in ("last_out", "held", "todo_ready", "todo_stored", "x_loaded", "h_made", "h_stored"))
        stats = box.sb("stats", [P, NB, 6])
        mv = box.sb("mv", [P, NB, 2])
        rstd = box.sb("rstd", [P, NB])
        shift = box.sb("shift", [P, NB])
        var = box.sb("var", [P, NB])
        guess = box.sb("guess", [P, NB], I32)
        with nc.Block() as block:

            @block.sync
            def _(sp):
                sp.wait_ge(filled, 1)
                sources = ((ends[0], raw[0]), (ends[1], raw[1]), (t8_d, t8), (t11_d, t11))
                for d, s in sources:
                    sp.dma_start(s[:, 0:EC], d[0:EC * P].rearrange("(p c) -> p c", p=P)).then_inc(loaded, 16)
                    sp.dma_start(s[0:EREST, EC:CE], d[EC * P:E].rearrange("(p c) -> p c", c=1)).then_inc(loaded, 16)
                sp.dma_start(alpha[:, :], alpha_d.rearrange("r o -> o r").broadcast_to([P, R11])).then_inc(loaded, 16)
                for d in (rec_d, pads_d):
                    sp.dma_start(d.rearrange("(p t) f -> p t f", p=P), pads[:, :, :]).then_inc(padded, 16)
                for src, dst in node_rows(x_d, x):
                    sp.dma_start(dst, src).then_inc(x_loaded, 16)
                sp.wait_ge(todo_ready, 1)
                sp.dma_start(todo_d, todo[:, :, :]).then_inc(todo_stored, 16)
                sp.wait_ge(h_made, 1)
                sp.dma_start(h0_d.rearrange("(b p) d -> p b d", p=P), x[:, :, :]).then_inc(h_stored, 16)
                for h, (a, b) in enumerate(SCAT_HALVES):
                    sp.wait_ge(scattered[h], 16 * (b - a) * NSG)
                sp.wait_ge(last_out, 16)
                sp.dma_start(pads[:, :, :], rec_d.rearrange("(p t) f -> p t f", p=P)).then_inc(reloaded, 16)
                sp.wait_ge(todo_stored, 16)
                sp.wait_ge(h_stored, 16)

            @block.gpsimd
            def _(pool):
                pool.iota(tile_no[:, :], pattern=[[1, T]], base=0, channel_multiplier=0,
                          allow_small_or_imprecise_dtypes=True).then_inc(iota_made, 1)
                pool.iota(spare[:, :], pattern=[[P, T]], base=P * T - EC * P, channel_multiplier=1).then_inc(iota_made, 1)
                pool.wait_ge(padded, 32)
                with nc.gpsimd.Fori(0, NSG) as g:
                    for h, (a, b) in enumerate(SCAT_HALVES):
                        hold(pool, ring_full, g * 2 + (h + 1), held)
                        for u in range(a, b):
                            pool.indirect_dma_start(
                                out=rec_d, out_offset=bass.IndirectOffsetOnAxis(ap=addr_ring[:, u:u + 1], axis=0),
                                in_=rec_ring[:, u, :], in_offset=None).then_inc(scattered[h], 16)
                pool.indirect_dma_start(
                    out=rec_d, out_offset=bass.IndirectOffsetOnAxis(ap=addr[0:EREST, EC:CE], axis=0),
                    in_=rec[0:EREST, EC, :], in_offset=None).then_inc(last_out, 16)

            @block.scalar
            def _(act):
                act.wait_ge(placed, 1)

                def stage(g, a, b):
                    nc.scalar.copy(rec_ring[:, a:b, :].rearrange("p c f -> p (c f)"),
                                   rec[:, :, :].rearrange("p c f -> p (c f)")[:, bass.ds((g * SG + a) * 4, (b - a) * 4)])
                    nc.scalar.copy(addr_ring[:, a:b], addr[:, bass.ds(g * SG + a, b - a)])
                    act.drain().then_inc(ring_full, 1)

                for a, b in SCAT_HALVES:
                    stage(0, a, b)
                with nc.scalar.Fori(0, NSG - 1) as g:
                    for h, (a, b) in enumerate(SCAT_HALVES):
                        act.wait_ge(scattered[h], g * (16 * (b - a)) + 16 * (b - a))
                        stage(g + 1, a, b)

            @block.tensor
            def _(pe):
                for k in range(2):
                    pe.wait_ge(counted, k + 1)
                    nc.tensor.matmul(ps_tot[:, :], c.ones[:, :], cnt[:, :], start=True, stop=True)
                    nc.tensor.matmul(ps_low[:, :], c.below[:, :], cnt[:, :], start=True, stop=True)
                    nc.tensor.matmul(ps_nT[:, :], cnt[:, :], c.ones[:, 0:1], start=True, stop=True).then_inc(summed, 1)
                    pe.wait_ge(nt_ready, k + 1)
                    nc.tensor.matmul(ps_end[:, :], c.upto[0:NB, 0:NB], nT[:, :], start=True, stop=True).then_inc(end_summed, 1)
                    pe.wait_ge(after_ready, k + 1)
                    nc.tensor.matmul(ps_bk[:, :], c.ones[0:NB, 0:1], after[:, 0:T // 2], start=True, stop=True)
                    nc.tensor.matmul(ps_bk2[:, :], c.ones[0:NB, 0:1], after[:, T // 2:T], start=True, stop=True).then_inc(bk_summed, 1)

            @block.vector
            def _(dve):
                for k in range(2):
                    nc.vector.memset(raw[k][:, EC:CE], P * (P - 1))
                nc.vector.memset(t8[:, EC:CE], 0)
                nc.vector.memset(t11[:, EC:CE], 0)
                nc.vector.memset(pads[:, :, :], 0)
                nc.vector.memset(x[:, NB - 1, :], 0.0)
                dve.drain()
                nc.vector.memset(pads[:, :, 1:2], -1)
                nc.vector.memset(onesw[:, :], 1.0)
                nc.vector.memset(pos[:, :], 0.0)
                dve.drain().then_inc(filled, 1)
                nc.vector.memset(todo[:, :, :], 0)
                dve.wait_ge(iota_made, 2)
                dve.drain()
                nc.vector.tensor_copy(todo[:, :, 4], spare[:, :])
                dve.wait_ge(loaded, 16 * 9)

                def place(k, records):
                    nc.vector.tensor_scalar(bucket_i[:, :], raw[k][:, :], 7, None, ALU.arith_shift_right)
                    nc.vector.tensor_copy(records[:, :, 0], raw[1 - k][:, :])
                    nc.vector.tensor_scalar(records[:, :, 1], raw[k][:, :], P - 1, None, ALU.bitwise_and)
                    nc.vector.tensor_copy(records[:, :, 2], t8[:, :])
                    nc.vector.tensor_copy(records[:, :, 3], t11[:, :])
                    dve.drain()
                    nc.vector.tensor_copy(bucket[:, :], bucket_i[:, :])
                    nc.vector.tensor_copy(bucketb[:, :], bucket_i[:, :])
                    dve.drain()
                    with nc.vector.Fori(0, NB) as b:
                        nc.vector.tensor_scalar(matchb[:, :], bucketb[:, :], c.iota[:, bass.ds(b, 1)], 0.0,
                                                ALU.is_equal, ALU.add, accum_out=cnt[:, bass.ds(b, 1)])
                        dve.drain()
                    dve.drain().then_inc(counted, 1)
                    dve.wait_ge(summed, k + 1)
                    nc.vector.tensor_scalar(tot_i[:, :], ps_tot[:, :], float(P - 1), None, ALU.add)
                    nc.vector.tensor_scalar(nT_i[:, :], ps_nT[:, :], float(P - 1), None, ALU.add)
                    dve.drain()
                    nc.vector.tensor_scalar(tot_i[:, :], tot_i[:, :], 7, None, ALU.arith_shift_right)
                    nc.vector.tensor_scalar(nT_i[:, :], nT_i[:, :], 7, None, ALU.arith_shift_right)
                    dve.drain()
                    nc.vector.tensor_copy(tiles[:, :], tot_i[:, :])
                    nc.vector.tensor_copy(nT[:, :], nT_i[:, :])
                    dve.drain().then_inc(nt_ready, 1)
                    nc.vector.tensor_tensor_scan(bucket_end[:, :], onesw[:, 0:NB], tiles[:, :], 0.0, ALU.mult, ALU.add)
                    dve.drain()
                    nc.vector.tensor_tensor(start[:, :], bucket_end[:, :], tiles[:, :], ALU.subtract)
                    dve.drain()
                    nc.vector.tensor_scalar(start[:, :], start[:, :], float(P), -1.0, ALU.mult, ALU.add)
                    dve.drain()
                    nc.vector.tensor_tensor(start[:, :], start[:, :], ps_low[:, :], ALU.add)
                    dve.drain()
                    with nc.vector.Fori(0, NB) as b:
                        nc.vector.tensor_scalar(match[:, :], bucket[:, :], c.iota[:, bass.ds(b, 1)], None, ALU.is_equal)
                        dve.drain()
                        nc.vector.tensor_tensor_scan(run[:, :], onesw[:, :], match[:, :], start[:, bass.ds(b, 1)],
                                                     ALU.mult, ALU.add)
                        dve.drain()
                        nc.vector.copy_predicated(pos[:, :], match[:, :].bitcast(I32), run[:, :])
                        dve.drain()
                    nc.vector.tensor_copy(posi[:, :], pos[:, :])
                    dve.drain()
                    nc.vector.tensor_scalar(slot_t[:, :], posi[:, :], 7, None, ALU.arith_shift_right)
                    nc.vector.tensor_scalar(posi[:, :], posi[:, :], P - 1, None, ALU.bitwise_and)
                    dve.drain()

                def row(out, lanes, a, b):
                    nc.vector.scalar_tensor_tensor(out=out, in0=posi[0:lanes, a:b], scalar=float(T),
                                                   in1=slot_t[0:lanes, a:b], op0=ALU.mult, op1=ALU.add)

                def tile_buckets(k, order):
                    dve.wait_ge(end_summed, k + 1)
                    nc.vector.tensor_copy(endT[:, :], ps_end[:, :])
                    dve.drain()
                    nc.vector.tensor_scalar(after[:, :], tile_no[:, :], endT[:, :], None, ALU.is_ge)
                    nc.vector.memset(order.tile_bucket[:, :], 0)
                    dve.drain().then_inc(after_ready, 1)
                    dve.wait_ge(bk_summed, k + 1)
                    nc.vector.tensor_scalar(order.tile_bucket[:, 0:T // 2], ps_bk[:, :], float(NB - 1), None, ALU.min)
                    nc.vector.tensor_scalar(order.tile_bucket[:, T // 2:T], ps_bk2[:, :], float(NB - 1), None, ALU.min)

                place(0, rec)
                row(addr[:, :], P, 0, CE)
                dve.drain().then_inc(placed, 1)
                tile_buckets(0, by_dst)
                place(1, todo[:, 0:CE, :])
                row(todo[:, 0:EC, 4], P, 0, EC)
                row(todo[0:EREST, EC:CE, 4], EREST, EC, CE)
                dve.drain().then_inc(todo_ready, 1)
                tile_buckets(1, by_src)
                dve.wait_ge(x_loaded, 32)
                statistics(nc, dve, x, stats, mv)
                nc.vector.tensor_scalar(var[:, :], mv[:, :, 1], EPS, None, ALU.add)
                dve.drain()
                nc.vector.tensor_scalar(guess[:, :], var[:, :].bitcast(I32), 1, None, ALU.arith_shift_right)
                dve.drain()
                nc.vector.tensor_scalar(rstd[:, :].bitcast(I32), guess[:, :], -1.0, float(0x5f3759df), ALU.mult, ALU.add)
                dve.drain()
                for _ in range(5):
                    nc.vector.tensor_tensor(shift[:, :], rstd[:, :], rstd[:, :], ALU.mult)
                    dve.drain()
                    nc.vector.tensor_tensor(shift[:, :], shift[:, :], var[:, :], ALU.mult)
                    dve.drain()
                    nc.vector.tensor_scalar(shift[:, :], shift[:, :], -0.5, 1.5, ALU.mult, ALU.add)
                    dve.drain()
                    nc.vector.tensor_tensor(rstd[:, :], rstd[:, :], shift[:, :], ALU.mult)
                    dve.drain()
                nc.vector.scalar_tensor_tensor(out=shift[:, :], in0=mv[:, :, 0], scalar=-1.0, in1=rstd[:, :],
                                               op0=ALU.mult, op1=ALU.mult)
                dve.drain()
                with nc.vector.Fori(0, NI) as i:
                    for u in range(U):
                        row_x = flat(x[:, bass.ds(i * U + u, 1), :])
                        nc.vector.tensor_scalar(row_x, row_x, rstd[:, bass.ds(i * U + u, 1)],
                                                shift[:, bass.ds(i * U + u, 1)], ALU.mult, ALU.add)
                dve.drain()
                nc.vector.tensor_scalar(x[:, :, :], x[:, :, :], 0.0, None, ALU.max)
                dve.drain().then_inc(h_made, 1)
                dve.wait_ge(reloaded, 16)
                unpack(nc, dve, pads, alpha, scratch, by_dst)


def node_rows(x_d, x):
    return ((x_d[0:(NB - 1) * P, :].rearrange("(b p) d -> p b d", p=P), x[:, 0:NB - 1, :]),
            (x_d[(NB - 1) * P:N, :], x[0:LAST, NB - 1, :]))


def statistics(nc, dve, x, stats, mv):
    with nc.vector.Fori(0, NI) as i:
        for u in range(U):
            nc.vector.bn_stats(flat(stats[:, bass.ds(i * U + u, 1), :]), flat(x[:, bass.ds(i * U + u, 1), :]))
    dve.drain()
    for b in range(NB):
        nc.vector.bn_aggr(mv[:, b, :], stats[:, b, :])
    dve.drain()


def unpack(nc, dve, records, alpha, scratch, out):
    nc.vector.memset(out.local[:, T:T + G], -1.0)
    nc.vector.memset(out.other[:, T:], 0)
    nc.vector.tensor_copy(out.other[:, 0:T], records[:, :, 0])
    nc.vector.tensor_copy(out.local[:, 0:T], records[:, :, 1])
    nc.vector.memset(out.weight[:, :], 0.0)
    if out.rel_other is not None:
        nc.vector.scalar_tensor_tensor(out=out.rel_other[:, 0:T], in0=records[:, :, 0], scalar=float(R8),
                                       in1=records[:, :, 2], op0=ALU.mult, op1=ALU.add)
        nc.vector.memset(out.rel_other[:, T:], 0)
        nc.vector.memset(out.type8[:, T:T + G], 0.0)
        nc.vector.tensor_copy(out.type8[:, 0:T], records[:, :, 2])
    dve.drain()
    for r in range(R11):
        nc.vector.tensor_scalar(scratch[:, :], records[:, :, 3], float(r), alpha[:, r:r + 1], ALU.is_equal, ALU.mult)
        dve.drain()
        nc.vector.tensor_tensor(out.weight[:, 0:T], out.weight[:, 0:T], scratch[:, :], ALU.add)
        dve.drain()


def wait_past(eng, sem, count):
    if not isinstance(count, int) or count > 0:
        eng.wait_ge(sem, count)


def hold(engine, sem, count, held):
    engine.wait_ge(sem, count)
    engine.sem_inc(held, 1)


class Order:
    pass


class Consts:
    pass


def gather_sum(nc, tag, c, order, index, table, acc, width, weighted=False, count=False, clear=True, load=()):
    cols = width + (1 if count else 0)
    with Box(nc, tag) as box:
        rows = box.sb("rows", [P, RING, ACCW])
        hot = box.sb("hot", [P, RING, P])
        idx = box.sb("idx", [P, RING], I32)
        part = [box.ps(f"part{k}", [P, 512]) for k in range(4)]
        staged = box.sem("indices_staged")
        held = box.sem("held")
        landed = [box.sem(f"rows_landed{h}") for h in range(2)]
        hot_made = box.sem("hot_made")
        summed = box.sem("tiles_summed")
        added = box.sem("parts_added")
        got = box.sem("got")
        with nc.Block() as block:

            @block.sync
            def _(sp):
                for src, dst in load:
                    sp.dma_start(dst, src).then_inc(got, 16)
                if load:
                    sp.wait_ge(got, 16 * len(load))

            @block.gpsimd
            def _(pool):
                with nc.gpsimd.Fori(0, NIT) as g:
                    for h in range(2):
                        pool.wait_ge(staged, g * 2 + (h + 1))
                        for u in range(h * G, h * G + G):
                            if u % 4 == 0:
                                hold(pool, summed, g * RING + (u + 4), held)
                            pool.indirect_dma_start(
                                out=rows[:, u, 0:width], out_offset=None, in_=table,
                                in_offset=bass.IndirectOffsetOnAxis(ap=idx[:, u:u + 1], axis=0)).then_inc(landed[h], 16)

            @block.scalar
            def _(act):
                with nc.scalar.Fori(0, NIT) as g:
                    for h in range(2):
                        act.wait_ge(summed, g * RING + (h + 1) * G)
                        nc.scalar.copy(idx[:, h * G:h * G + G],
                                       index[:, bass.ds(g * RING + h * G, G)]).then_inc(staged, 1)

            @block.tensor
            def _(pe):
                pe.sem_inc(summed, RING)
                with nc.tensor.Fori(0, NIT) as g:
                    for u in range(RING):
                        if u % G == 0:
                            pe.wait_ge(landed[u // G], g * (16 * G) + 16 * G)
                        pe.wait_ge(hot_made, g * RING + (u + 1))
                        pe.wait_ge(added, g * RING + (u + 1))
                        nc.tensor.matmul(part[u % 4][:, 0:cols], hot[:, u, :], rows[:, u, 0:cols],
                                         start=True, stop=True).then_inc(summed, 1)

            @block.vector
            def _(dve):
                if clear:
                    nc.vector.memset(acc[:, :, :], 0.0)
                if count:
                    nc.vector.memset(rows[:, :, width:width + 1], 1.0)
                dve.drain()
                dve.sem_inc(added, 4)

                def one_hots(tile0, h):
                    for u in range(h * G, h * G + G):
                        t = tile0 + (u - h * G)
                        nc.vector.tensor_scalar(hot[:, u, :], c.iota[:, :], order.local[:, bass.ds(t, 1)],
                                                order.weight[:, bass.ds(t, 1)] if weighted else None,
                                                ALU.is_equal, ALU.mult if weighted else ALU.bypass).then_inc(hot_made, 1)

                one_hots(0, 0)
                with nc.vector.Fori(0, NIT) as g:
                    for h in range(2):
                        dve.wait_ge(summed, g * RING + (h + 2) * G)
                        one_hots(g * RING + (h + 1) * G, 1 - h)
                        buckets = buckets_of(nc, mybir.EngineType.DVE, order, g * RING + h * G)
                        for u in range(h * G, h * G + G):
                            dve.wait_ge(summed, g * RING + (RING + u + 1))
                            dve.wait_ge(added, g * RING + (u + 4))
                            a = acc[:, bass.ds(buckets[u % G], 1), 0:cols].rearrange("p o c -> p (o c)")
                            nc.vector.tensor_tensor(a, a, part[u % 4][:, 0:cols], ALU.add).then_inc(added, 1)


def normalize(nc, tag, c, x, h, load=(), meanwhile=None):
    with Box(nc, tag) as box:
        stats = box.sb("stats", [P, NB, 6])
        mv = box.sb("mv", [P, NB, 2])
        rstd = box.sb("rstd", [P, NB])
        shift = box.sb("shift", [P, NB])
        var_ready, std_ready, scale_ready, loaded = (
            box.sem(n) for n in ("var_ready", "std_ready", "scale_ready", "loaded"))
        with nc.Block() as block:

            @block.vector
            def _(dve):
                statistics(nc, dve, x, stats, mv)
                nc.vector.tensor_scalar(rstd[:, :], mv[:, :, 1], EPS, None, ALU.add)
                dve.drain().then_inc(var_ready, 1)
                dve.wait_ge(std_ready, 1)
                nc.vector.reciprocal(rstd[:, :], rstd[:, :])
                dve.drain()
                nc.vector.scalar_tensor_tensor(out=shift[:, :], in0=mv[:, :, 0], scalar=-1.0, in1=rstd[:, :],
                                               op0=ALU.mult, op1=ALU.mult)
                dve.drain().then_inc(scale_ready, 1)
                if meanwhile:
                    dve.wait_ge(loaded, 16 * len(load))
                    meanwhile(dve)

            @block.scalar
            def _(act):
                act.wait_ge(var_ready, 1)
                nc.scalar.activation(rstd[:, :], rstd[:, :], ACT.Sqrt)
                act.drain().then_inc(std_ready, 1)
                act.wait_ge(scale_ready, 1)
                with nc.scalar.Fori(0, NI) as i:
                    for u in range(U):
                        b = i * U + u
                        nc.scalar.activation(h[:, bass.ds(b, 1), 0:D].rearrange("p o d -> p (o d)"),
                                             x[:, bass.ds(b, 1), :].rearrange("p o d -> p (o d)"),
                                             ACT.Relu, bias=shift[:, bass.ds(b, 1)],
                                             scale=rstd[:, bass.ds(b, 1)])

            @block.sync
            def _(sp):
                for dst, src in load:
                    sp.dma_start(dst, src).then_inc(loaded, 16)


def transpose_weights(nc, tag, c, pairs, raw=None):
    with Box(nc, tag) as box:
        raw = raw or [box.sb(f"raw{k}", [P, w_d.shape[0] // P, w_d.shape[1]]) for k, (w_d, _) in enumerate(pairs)]
        turned = [box.ps(f"turned{k}", [P, 512]) for k in range(2)]
        loaded, turns, copied = box.sem("loaded"), box.sem("turned"), box.sem("copied")
        blocks = [(raw[k][:, oc, fc * P:(fc + 1) * P], wT[:, fc, oc * P:(oc + 1) * P])
                  for k, (w_d, wT) in enumerate(pairs)
                  for fc in range(w_d.shape[1] // P) for oc in range(w_d.shape[0] // P)]
        with nc.Block() as block:

            @block.sync
            def _(sp):
                for k, (w_d, _) in enumerate(pairs):
                    sp.dma_start(raw[k][:, :, :], w_d.rearrange("(c p) f -> p c f", p=P)).then_inc(loaded, 16)

            @block.tensor
            def _(pe):
                pe.wait_ge(loaded, 16 * len(pairs))
                for n, (src, _) in enumerate(blocks):
                    if n >= 2:
                        pe.wait_ge(copied, n - 1)
                    nc.tensor.transpose(turned[n % 2][:, 0:P], src, c.ident[:, :]).then_inc(turns, 1)

            @block.vector
            def _(dve):
                for n, (_, dst) in enumerate(blocks):
                    dve.wait_ge(turns, n + 1)
                    nc.vector.tensor_copy(dst, turned[n % 2][:, 0:P]).then_inc(copied, 1)


def project(nc, tag, c, sources, weights, cols, finish, before=None, load=None, store=()):
    chunks = sum(n for _, n, _ in sources)
    with Box(nc, tag) as box:
        stage = box.sb("stage", [P, 4, chunks * P])
        turned_sb = box.sb("turned_sb", [P, 4, chunks * P])
        turned = [box.ps(f"turned{k}", [P, 512]) for k in range(2)]
        result = [box.ps(f"result{k}", [P, 512]) for k in range(2)]
        ready, staged, turns, copied, product, finished, got, stored = (
            box.sem(n) for n in ("ready", "staged", "turned", "copied", "product", "finished", "got", "stored"))
        with nc.Block() as block:

            @block.sync
            def _(sp):
                for dst, src in load or []:
                    sp.dma_start(dst, src).then_inc(got, 16)
                stores = 0
                for i in range(NI if store else 0):
                    sp.wait_ge(finished, 2 + (i + 1) * U)
                    for src, d in store:
                        stores += store_buckets(sp, src, d, i * U, (i + 1) * U, stored)
                if stores:
                    sp.wait_ge(stored, 16 * stores)

            @block.scalar
            def _(act):
                act.wait_ge(ready, 1)
                with nc.scalar.Fori(0, NI) as i:
                    for u in range(U):
                        b = i * U + u
                        act.wait_ge(copied, b + (U - 2))
                        at = 0
                        for k, (src, n, scale) in enumerate(sources):
                            a = src[:, bass.ds(b, 1), 0:n * P].rearrange("p o d -> p (o d)")
                            last = nc.scalar.activation(stage[:, u % 4, at:at + n * P], a, ACT.Copy,
                                                        scale=1.0 if scale is None else scale[:, bass.ds(b, 1)])
                            last.then_inc(staged, 1)
                            at += n * P

            @block.tensor
            def _(pe):
                def turn(b, u):
                    pe.wait_ge(staged, b * len(sources) + len(sources))
                    pe.wait_ge(copied, b + (U if u == 0 else U - 1))
                    for k in range(chunks):
                        last = nc.tensor.transpose(turned[u % 2][:, k * P:(k + 1) * P],
                                                   stage[:, u % 4, k * P:(k + 1) * P], c.ident[:, :])
                    last.then_inc(turns, 1)

                pe.wait_ge(ready, 1)
                with nc.tensor.Fori(0, NI) as i:
                    turn(i * U, 0)
                    for u in range(U):
                        b = i * U + u
                        if u + 1 < U:
                            turn(b + 1, u + 1)
                        pe.wait_ge(copied, b + U + 1)
                        pe.wait_ge(finished, b + (2 if u == 0 else 1))
                        for k in range(chunks):
                            last = nc.tensor.matmul(result[u % 2][:, 0:cols], turned_sb[:, u % 4, k * P:(k + 1) * P],
                                                    weights[k], start=(k == 0), stop=(k == chunks - 1))
                        last.then_inc(product, 1)

            @block.vector
            def _(dve):
                if load:
                    dve.wait_ge(got, 16 * len(load))
                if before:
                    before(dve)
                dve.sem_inc(copied, U)
                dve.sem_inc(finished, 2)
                dve.drain().then_inc(ready, 1)

                def copy_turned(b, u):
                    dve.wait_ge(turns, b + 1)
                    nc.vector.tensor_copy(turned_sb[:, u % 4, :], turned[u % 2][:, 0:chunks * P]).then_inc(copied, 1)

                with nc.vector.Fori(0, NI) as i:
                    copy_turned(i * U, 0)
                    for u in range(U):
                        b = i * U + u
                        if u + 1 < U:
                            copy_turned(b + 1, u + 1)
                        dve.wait_ge(product, b + 1)
                        finish(dve, b, result[u % 2][:, 0:cols]).then_inc(finished, 1)


def flat(ap):
    return ap.rearrange("p o d -> p (o d)")


def buckets_of(nc, engine, order, tile, n=G):
    _, values = nc.values_load_multi_w_load_instructions(
        order.tile_bucket[0:1, bass.ds(tile, n)], engines=[engine], min_val=0, max_val=NB - 1,
        skip_runtime_bounds_check_because="a count of buckets, clipped to NB - 1 where it is made")
    return values


def there(k):
    return not isinstance(k, int) or k < NH


def each_half(engine, step):
    with engine.Fori(0, NH // 4 - 1) as g:
        for hh in range(4):
            step(g, hh)
    for hh in range(4):
        step(NH // 4 - 1, hh)


def attention_max(nc, tag, c, order, index, table, H, R, dst_scores, score, top, x, x_d, later=None):
    with Box(nc, tag) as box:
        src = box.sb("src", [P, 4, G, H])
        hot = box.sb("hot", [P, 2, G, P], BF16)
        hotT = box.sb("hotT", [P, G, P])
        typed = box.sb("typed", [P, G, R])
        picked = box.sb("picked", [P, G, R, H])
        s = box.sb("s", [P, G, H])
        rest = box.sb("rest", [P, G, H])
        rows = 3 * H + 2 * BITS
        parts = box.sb("parts", [P, G, rows], BF16)
        partsT = box.sb("partsT", [rows, G * P], BF16)
        pick = box.sb("pick", [P, H, rows], BF16)
        pickT = box.sb("pickT", [rows, H * P], BF16)
        head_diff = box.sb("head_diff", [P, H, 3, H])
        node = box.sb("node", [P, 1], I32)
        bit = box.sb("bit", [P, BITS], I32)
        node_bits = box.sb("node_bits", [P, 1, BITS], I32)
        local = box.sb("local", [P, G], I32)
        edge_bits = box.sb("edge_bits", [P, G, BITS], I32)
        tile_top = box.sb("tile_top", [P, G, H])
        idx = box.sb("idx", [P, 4, G], I32)
        todo = box.sb("todo", [P, 2, G, 5], I32)
        ps_hot = box.ps("ps_hot", [P, G, P], BF16)
        ps_dst = box.ps("ps_dst", [P, 512])
        ps_parts = box.ps("ps_parts", [P, G * P], BF16)[0:rows, :]
        together = H1 // H
        groups = G // together
        big = [box.ps(f"big{k}", [P, together * H * P]) for k in range(2)]
        names = ("ready", "held", "staged", "hot_made", "hot_turned", "hot_copied", "dst_spread", "scored",
                 "parts_turned", "parts_copied", "masked", "reduced", "topped", "indices_made", "pick_made", "x_stored")
        (ready, held, staged, hot_made, hot_turned, hot_copied, dst_spread, scored, parts_turned, parts_copied,
         masked, reduced, topped, indices_made, pick_made, x_stored) = (box.sem(n) for n in names)
        landed = [box.sem(f"landed{h}") for h in range(4)]
        fed = [box.sem(f"fed{h}") for h in range(2)]
        scattered = [box.sem(f"scattered{h}") for h in range(2)]
        with nc.Block() as block:

            @block.sync
            def _(sp):
                sp.dma_start(x_d.rearrange("(b p) d -> p b d", p=P), x[:, :, :]).then_inc(x_stored, 16)

                def feed(k, h):
                    sp.dma_start(todo[:, h, :, :], later[0][:, bass.ds(k * G, G), :]).then_inc(fed[h], 16)

                def feed_ahead(g, hh):
                    k = g * 4 + hh
                    if there(k + 2):
                        sp.wait_ge(scattered[hh % 2], g * (32 * G) + 16 * G * (hh // 2 + 1))
                        feed(k + 2, hh % 2)

                if later:
                    feed(0, 0)
                    feed(1, 1)
                    each_half(nc.sync, feed_ahead)
                    for h in range(2):
                        sp.wait_ge(scattered[h], 16 * G * (NH // 2))
                sp.wait_ge(x_stored, 16)

            @block.gpsimd
            def _(pool):
                pool.iota(head_diff[:, :, :, :], pattern=[[-1, H], [0, 3], [1, H]], base=0, channel_multiplier=0,
                          allow_small_or_imprecise_dtypes=True).then_inc(indices_made, 1)
                pool.iota(node[:, :], pattern=[[0, 1]], base=0, channel_multiplier=1).then_inc(indices_made, 1)
                pool.wait_ge(ready, 1)

                def gather(g, hh):
                    k, h = g * 4 + hh, hh % 2
                    pool.wait_ge(staged, k + 1)
                    hold(pool, scored, k + 1, held)
                    for u in range(G):
                        pool.indirect_dma_start(
                            out=src[:, hh, u, :], out_offset=None, in_=table,
                            in_offset=bass.IndirectOffsetOnAxis(ap=idx[:, hh, u:u + 1], axis=0)).then_inc(landed[hh], 16)
                    if later:
                        hold(pool, fed[h], (g * 2 + hh // 2) * 16 + 16, held)
                        for u in range(G):
                            pool.indirect_dma_start(
                                out=later[1], out_offset=bass.IndirectOffsetOnAxis(ap=todo[:, h, u, 4:5], axis=0),
                                in_=todo[:, h, u, 0:4], in_offset=None).then_inc(scattered[h], 16)

                each_half(nc.gpsimd, gather)

            @block.scalar
            def _(act):
                act.wait_ge(parts_turned, 1)
                nc.scalar.copy(pickT[:, :], ps_parts[:, 0:H * P]).then_inc(parts_copied, 1)
                act.wait_ge(ready, 1)

                def stage_indices(k, h):
                    nc.scalar.copy(idx[:, h, :], index[:, bass.ds(k * G, G)]).then_inc(staged, 1)

                def copy_hots(k):
                    act.wait_ge(hot_turned, k + 1)
                    wait_past(act, dst_spread, k)
                    nc.scalar.copy(hotT[:, :, :], ps_hot[:, :, :]).then_inc(hot_copied, 1)

                def copy_parts(k):
                    act.wait_ge(parts_turned, k + 2)
                    wait_past(act, masked, k * groups)
                    nc.scalar.copy(partsT[:, :], ps_parts[:, :]).then_inc(parts_copied, 1)

                for k in range(3):
                    stage_indices(k, k)
                copy_hots(0)
                copy_hots(1)
                copy_parts(0)

                def step(g, hh):
                    k = g * 4 + hh
                    if there(k + 3):
                        act.wait_ge(scored, k + 4)
                        stage_indices(k + 3, (hh + 3) % 4)
                    if there(k + 2):
                        copy_hots(k + 2)
                    if there(k + 1):
                        copy_parts(k + 1)

                each_half(nc.scalar, step)

            @block.tensor
            def _(pe):
                pe.wait_ge(pick_made, 1)
                for hd in range(H):
                    last = nc.tensor.transpose(ps_parts[:, hd * P:(hd + 1) * P], pick[:, hd, :], c.identb[:, :])
                last.then_inc(parts_turned, 1)
                pe.wait_ge(ready, 1)

                def turn_hots(k, h):
                    pe.wait_ge(hot_made, k + 1)
                    wait_past(pe, hot_copied, k)
                    for u in range(G):
                        last = nc.tensor.transpose(ps_hot[:, u, :], hot[:, h, u, :], c.identb[:, :])
                    last.then_inc(hot_turned, 1)

                def spread(k):
                    buckets = buckets_of(nc, mybir.EngineType.PE, order, k * G)
                    pe.wait_ge(hot_copied, k + 1)
                    pe.wait_ge(scored, k + 4)
                    for u in range(G):
                        last = nc.tensor.matmul(ps_dst[:, u * R * H:(u + 1) * R * H], hotT[:, u, :],
                                                flat(dst_scores[:, bass.ds(buckets[u], 1), :]), start=True, stop=True)
                    last.then_inc(dst_spread, 1)

                def turn_parts(k):
                    pe.wait_ge(scored, k + 5)
                    hold(pe, parts_copied, k + 1, held)
                    for u in range(G):
                        last = nc.tensor.transpose(ps_parts[:, u * P:(u + 1) * P], parts[:, u, :], c.identb[:, :])
                    last.then_inc(parts_turned, 1)

                def mask_scores(k):
                    pe.wait_ge(parts_copied, k + 2)
                    for i in range(groups):
                        pe.wait_ge(reduced, k * groups + (i + 1))
                        for n in range(together * H):
                            u, hd = i * together + n // H, n % H
                            last = nc.tensor.matmul(big[i % 2][:, n * P:(n + 1) * P], pickT[:, hd * P:(hd + 1) * P],
                                                    partsT[:, u * P:(u + 1) * P], start=True, stop=True)
                        last.then_inc(masked, 1)

                for k in range(2):
                    turn_hots(k, k)
                    spread(k)
                turn_parts(0)

                def step(g, hh):
                    k = g * 4 + hh
                    if there(k + 2):
                        turn_hots(k + 2, hh % 2)
                    mask_scores(k)
                    if there(k + 2):
                        spread(k + 2)
                    if there(k + 1):
                        turn_parts(k + 1)

                each_half(nc.tensor, step)

            @block.vector
            def _(dve):
                dve.wait_ge(indices_made, 2)
                for i in range(BITS):
                    nc.vector.memset(bit[:, i:i + 1], 1 << i)
                dve.drain()
                nc.vector.tensor_scalar(pick[:, :, 0:3 * H].rearrange("p h (a x) -> p h a x", a=3),
                                        head_diff[:, :, :, :], 0.0, None, ALU.is_equal)
                nc.vector.tensor_tensor(node_bits[:, 0, :], node[:, 0:1].broadcast_to([P, BITS]), bit[:, :], ALU.bitwise_and)
                dve.drain()
                lacks = node_bits[:, :, :].broadcast_to([P, H, BITS])
                nc.vector.tensor_scalar(pick[:, :, 3 * H:3 * H + BITS], lacks, 0.0, None, ALU.is_equal)
                nc.vector.tensor_scalar(pick[:, :, 3 * H + BITS:rows], lacks, 0.0, None, ALU.is_gt)
                dve.drain().then_inc(pick_made, 1)
                dve.sem_inc(scored, 4)
                dve.sem_inc(reduced, 2)
                dve.sem_inc(topped, 1)
                dve.drain().then_inc(ready, 1)

                def one_hots(k, h):
                    nc.vector.tensor_tensor(
                        hot[:, h, :, :], c.iota[:, :].rearrange("p (o n) -> p o n", o=1).broadcast_to([P, G, P]),
                        order.local[:, bass.ds(k * G, G)].rearrange("p (u o) -> p u o", o=1).broadcast_to([P, G, P]),
                        ALU.is_equal).then_inc(hot_made, 1)

                def score_half(k, slot, landed_at):
                    if R > 1:
                        nc.vector.tensor_tensor(
                            typed[:, :, :], order.type8[:, bass.ds(k * G, G)].rearrange("p (u o) -> p u o", o=1).broadcast_to([P, G, R]),
                            c.iota[:, 0:R].rearrange("p (o r) -> p o r", o=1).broadcast_to([P, G, R]), ALU.is_equal)
                        dve.drain()
                    nc.vector.tensor_scalar(local[:, :], order.local[:, bass.ds(k * G, G)], 1.0, None, ALU.mult)
                    dve.drain()
                    nc.vector.tensor_tensor(edge_bits[:, :, :], local[:, :].rearrange("p (u o) -> p u o", o=1).broadcast_to([P, G, BITS]),
                                            bit[:, :].rearrange("p (o i) -> p o i", o=1).broadcast_to([P, G, BITS]), ALU.bitwise_and)
                    dve.wait_ge(dst_spread, k + 1)
                    if R > 1:
                        nc.vector.tensor_tensor(
                            picked[:, :, :, :], ps_dst[:, 0:G * R * H].rearrange("p (u r h) -> p u r h", u=G, r=R),
                            typed[:, :, :].rearrange("p u (r o) -> p u r o", o=1).broadcast_to([P, G, R, H]), ALU.mult)
                        dve.drain()
                        nc.vector.reduce_sum(s[:, :, :], picked[:, :, :, :].rearrange("p u r h -> p u h r"), AX_X)
                        dve.drain()
                    dve.wait_ge(landed[slot], landed_at)
                    near = s[:, :, :] if R > 1 else ps_dst[:, 0:G * H].rearrange("p (u h) -> p u h", u=G)
                    nc.vector.tensor_tensor(s[:, :, :], near, src[:, slot, :, :], ALU.add)
                    dve.drain()
                    out = score[:, bass.ds(k * G, G), :]
                    nc.vector.scalar_tensor_tensor(out=out, in0=s[:, :, :], scalar=0.2, in1=s[:, :, :],
                                                   op0=ALU.mult, op1=ALU.max)
                    dve.drain()
                    dve.wait_ge(parts_turned, k + 1)
                    high, middle, low = (parts[:, :, i * H:(i + 1) * H] for i in range(3))
                    nc.vector.tensor_scalar(high, out, 1.0, None, ALU.mult)
                    nc.vector.tensor_scalar(parts[:, :, 3 * H:3 * H + BITS], edge_bits[:, :, :], 0.0, -NEG, ALU.is_gt, ALU.mult)
                    nc.vector.tensor_scalar(parts[:, :, 3 * H + BITS:rows], edge_bits[:, :, :], 0.0, -NEG, ALU.is_equal, ALU.mult)
                    dve.drain()
                    nc.vector.tensor_tensor(rest[:, :, :], out, high, ALU.subtract)
                    dve.drain()
                    nc.vector.tensor_copy(middle, rest[:, :, :])
                    dve.drain()
                    nc.vector.tensor_tensor(low, rest[:, :, :], middle, ALU.subtract)
                    dve.drain().then_inc(scored, 1)

                one_hots(0, 0)
                one_hots(1, 1)
                score_half(0, 0, 16 * G)
                one_hots(2, 0)
                score_half(1, 1, 16 * G)

                def step(g, hh):
                    k = g * 4 + hh
                    dve.wait_ge(topped, k * G + 1)
                    for i in range(groups):
                        dve.wait_ge(masked, k * groups + (i + 1))
                        nc.vector.reduce_max(tile_top[:, i * together:(i + 1) * together, :].rearrange("p u h -> p (u h)"),
                                             big[i % 2][:, :].rearrange("p (n e) -> p n e", e=P), AX_X).then_inc(reduced, 1)
                    if there(k + 3):
                        one_hots(k + 3, (hh + 3) % 2)
                    buckets = buckets_of(nc, mybir.EngineType.DVE, order, k * G)
                    dve.wait_ge(reduced, k * groups + (groups + 2))
                    for u in range(G):
                        dve.wait_ge(topped, k * G + (u + 1))
                        a = flat(top[:, bass.ds(buckets[u], 1), :])
                        nc.vector.tensor_tensor(a, a, tile_top[:, u, :], ALU.max).then_inc(topped, 1)
                    if there(k + 2):
                        score_half(k + 2, (hh + 2) % 4, g * (16 * G) + ((hh + 2) // 4 + 1) * 16 * G)

                each_half(nc.vector, step)


def attention_sum(nc, tag, c, order, index, table, width, H, score, top, acc, x):
    cols = width + H
    with Box(nc, tag) as box:
        room = x[:, :, :].rearrange("p b d -> p (b d)")
        rows = room[:, 0:4 * G * ACCW].rearrange("p (u c) -> p u c", c=ACCW)
        hot = room[:, 4 * G * ACCW:4 * G * (ACCW + P)].rearrange("p (u n) -> p u n", n=P)
        hotT = box.sb("hotT", [P, G, P], BF16)
        near = box.sb("near", [P, G, H])
        below = box.sb("below", [P, 2, G, H])
        idx = box.sb("idx", [P, 4, G], I32)
        ps_hot = box.ps("ps_hot", [P, G, P])
        ps_top = box.ps("ps_top", [P, 512])
        part = [box.ps(f"part{k}", [P, 512]) for k in range(4)]
        names = ("held", "staged", "hot_made", "hot_turned", "hot_copied", "top_spread", "lowered", "weighed",
                 "messages", "summed", "added")
        (held, staged, hot_made, hot_turned, hot_copied, top_spread, lowered, weighed, messages, summed,
         added) = (box.sem(n) for n in names)
        landed = [box.sem(f"landed{h}") for h in range(4)]
        with nc.Block() as block:

            @block.gpsimd
            def _(pool):
                def gather(g, hh):
                    k = g * 4 + hh
                    pool.wait_ge(staged, k + 1)
                    for u in range(G):
                        if u % 4 == 0:
                            hold(pool, summed, k * G + (u + 4), held)
                        pool.indirect_dma_start(
                            out=rows[:, hh * G + u, 0:width], out_offset=None, in_=table,
                            in_offset=bass.IndirectOffsetOnAxis(ap=idx[:, hh, u:u + 1], axis=0)).then_inc(landed[hh], 16)

                each_half(nc.gpsimd, gather)

            @block.scalar
            def _(act):
                def stage_indices(k, slot):
                    nc.scalar.copy(idx[:, slot, :], index[:, bass.ds(k * G, G)]).then_inc(staged, 1)

                def weigh(k, slot):
                    act.wait_ge(hot_turned, k + 1)
                    wait_past(act, top_spread, k)
                    nc.scalar.copy(hotT[:, :, :], ps_hot[:, :, :]).then_inc(hot_copied, 1)
                    act.wait_ge(lowered, k + 1)
                    act.wait_ge(summed, k * G + G)
                    nc.scalar.activation(rows[:, slot * G:slot * G + G, width:cols], below[:, slot % 2, :, :],
                                         ACT.Exp).then_inc(weighed, 1)

                for k in range(3):
                    stage_indices(k, k)
                weigh(0, 0)
                weigh(1, 1)

                def step(g, hh):
                    k = g * 4 + hh
                    if there(k + 3):
                        wait_past(act, messages, k * 2)
                        stage_indices(k + 3, (hh + 3) % 4)
                    if there(k + 2):
                        weigh(k + 2, (hh + 2) % 4)

                each_half(nc.scalar, step)

            @block.tensor
            def _(pe):
                pe.sem_inc(summed, 4 * G)

                def turn_hots(k, slot):
                    pe.wait_ge(hot_made, k + 1)
                    wait_past(pe, hot_copied, k)
                    for u in range(G):
                        last = nc.tensor.transpose(ps_hot[:, u, :], hot[:, slot * G + u, :], c.ident[:, :])
                    last.then_inc(hot_turned, 1)

                def spread(k):
                    buckets = buckets_of(nc, mybir.EngineType.PE, order, k * G)
                    pe.wait_ge(hot_copied, k + 1)
                    wait_past(pe, lowered, k)
                    for u in range(G):
                        last = nc.tensor.matmul(ps_top[:, u * 3 * H:(u + 1) * 3 * H], hotT[:, u, :],
                                                flat(top[:, bass.ds(buckets[u], 1), :]), start=True, stop=True)
                    last.then_inc(top_spread, 1)

                for k in range(2):
                    turn_hots(k, k)
                    spread(k)

                def step(g, hh):
                    k = g * 4 + hh
                    if there(k + 2):
                        turn_hots(k + 2, (hh + 2) % 4)
                    for u in range(G):
                        if u == G // 2 and there(k + 2):
                            spread(k + 2)
                        if u % 4 == 0:
                            pe.wait_ge(messages, k * 2 + (u // 4 + 1))
                        pe.wait_ge(added, k * G + (u + 1))
                        nc.tensor.matmul(part[u % 4][:, 0:cols], hot[:, hh * G + u, :], rows[:, hh * G + u, 0:cols],
                                         start=True, stop=True).then_inc(summed, 1)

                each_half(nc.tensor, step)

            @block.vector
            def _(dve):
                nc.vector.memset(acc[:, :, :], 0.0)
                dve.sem_inc(added, 4)
                dve.drain()

                def one_hots(k, slot):
                    nc.vector.tensor_tensor(
                        hot[:, slot * G:slot * G + G, :], c.iota[:, :].rearrange("p (o n) -> p o n", o=1).broadcast_to([P, G, P]),
                        order.local[:, bass.ds(k * G, G)].rearrange("p (u o) -> p u o", o=1).broadcast_to([P, G, P]),
                        ALU.is_equal).then_inc(hot_made, 1)

                def lower(k, h):
                    dve.wait_ge(top_spread, k + 1)
                    nc.vector.reduce_sum(near[:, :, :], ps_top[:, 0:G * 3 * H].rearrange("p (u a h) -> p u h a", u=G, a=3), AX_X)
                    dve.drain()
                    nc.vector.tensor_tensor(below[:, h, :, :], score[:, bass.ds(k * G, G), :], near[:, :, :], ALU.subtract)
                    dve.drain()
                    nc.vector.tensor_scalar(below[:, h, :, :], below[:, h, :, :], 0.0, None, ALU.min).then_inc(lowered, 1)

                def weigh_rows(k, slot, u0, landed_at):
                    dve.wait_ge(landed[slot], landed_at)
                    dve.wait_ge(weighed, k + 1)
                    u = slot * G + u0
                    m = rows[:, u:u + 4, 0:width].rearrange("p u (h d) -> p u h d", h=H)
                    w = rows[:, u:u + 4, width:cols].rearrange("p u (h o) -> p u h o", o=1)
                    nc.vector.tensor_tensor(m, m, w.broadcast_to([P, 4, H, width // H]), ALU.mult).then_inc(messages, 1)

                for k in range(3):
                    one_hots(k, k)
                lower(0, 0)
                lower(1, 1)
                for u0 in range(0, G, 4):
                    weigh_rows(0, 0, u0, 16 * G)

                def step(g, hh):
                    k = g * 4 + hh
                    buckets = buckets_of(nc, mybir.EngineType.DVE, order, k * G)

                    def add(u0):
                        for u in range(u0, u0 + 4):
                            dve.wait_ge(summed, k * G + (4 * G + u + 1))
                            dve.wait_ge(added, k * G + (u + 4))
                            a = acc[:, bass.ds(buckets[u], 1), 0:cols].rearrange("p o c -> p (o c)")
                            nc.vector.tensor_tensor(a, a, part[u % 4][:, 0:cols], ALU.add).then_inc(added, 1)

                    for u0 in range(0, G, 4):
                        if there(k + 1):
                            weigh_rows(k + 1, (hh + 1) % 4, u0, g * (16 * G) + 16 * G * ((hh + 1) // 4 + 1))
                        if u0 and there(k + 3):
                            one_hots(k + 3, (hh + 3) % 4)
                        add(u0)
                        if not u0 and there(k + 2):
                            lower(k + 2, hh % 2)

                each_half(nc.vector, step)


def split_top(nc, tag, top, parts, rest):
    def body(dve):
        nc.vector.tensor_copy(parts[:, :, 0, :], top[:, :, :])
        dve.drain()
        nc.vector.tensor_tensor(rest[:, :, :], top[:, :, :], parts[:, :, 0, :], ALU.subtract)
        dve.drain()
        nc.vector.tensor_copy(parts[:, :, 1, :], rest[:, :, :])
        dve.drain()
        nc.vector.tensor_tensor(parts[:, :, 2, :], rest[:, :, :], parts[:, :, 1, :], ALU.subtract)

    on_vector(nc, tag, [], body)


def store_buckets(sp, src, dst_d, b0, b1, stored):
    full = min(b1, dst_d.shape[0] // P)
    sp.dma_start(dst_d[b0 * P:full * P, :].rearrange("(b p) d -> p b d", p=P), src[:, b0:full, :]).then_inc(stored, 16)
    if full < b1:
        sp.dma_start(dst_d[full * P:, :], src[0:LAST, full, :]).then_inc(stored, 16)
    return 1 + (full < b1)


def store_nodes(nc, tag, src, dst_d):
    with Box(nc, tag) as box:
        stored = box.sem("stored")
        with nc.Block() as block:

            @block.sync
            def _(sp):
                sp.wait_ge(stored, 16 * store_buckets(sp, src, dst_d, 0, NB, stored))


def sage(nc, tag, c, x, h, acc, own_d, wl_d, wr_d, b_d, residual, store=()):
    with Box(nc, tag) as box:
        wlT = box.sb("wlT", [P, 2, D])
        wrT = box.sb("wrT", [P, 2, D])
        bias = box.sb("bias", [P, D])
        transpose_weights(nc, tag + "w", c, [(wl_d, wlT), (wr_d, wrT)])

        def before(dve):
            if c.rdeg_made:
                return
            nc.vector.tensor_scalar(c.rdeg[:, :], acc[:, :, D], 1.0, None, ALU.max)
            dve.drain()
            nc.vector.reciprocal(c.rdeg[:, :], c.rdeg[:, :])
            c.rdeg_made = True

        def finish(dve, b, ps):
            if not residual:
                out = flat(h[:, bass.ds(b, 1), :])
                nc.vector.tensor_tensor(out, ps, bias[:, :], ALU.add)
                dve.drain()
                return nc.vector.tensor_scalar(out, out, 0.0, None, ALU.max)
            out = flat(x[:, bass.ds(b, 1), :])
            nc.vector.tensor_tensor(out, out, ps, ALU.add)
            dve.drain()
            return nc.vector.tensor_tensor(out, out, bias[:, :], ALU.add)

        project(nc, tag + "p", c, [(acc, 2, c.rdeg), (h, 2, None)],
                [wlT[:, 0, :], wlT[:, 1, :], wrT[:, 0, :], wrT[:, 1, :]], D, finish, before=before, store=store,
                load=[(bias[:, :], b_d.rearrange("(o d) -> o d", o=1).broadcast_to([P, D])),
                      (h[:, :, :], own_d.rearrange("(b p) d -> p b d", p=P))])


def fold_attention(nc, tag, c, lhs, attn_ds, heads, width, dst):
    blocks, rels = heads * width // P, len(lhs[0])
    with Box(nc, tag) as box:
        offset = box.sb("offset", [P, blocks, heads])
        inside = box.sb("inside", [P, blocks, heads])
        attn = box.sb("attn", [P, 2, blocks])
        spread = box.sb("spread", [P, blocks, 2, heads])
        folded = [box.ps(f"folded{k}", [P, 512]) for k in range(len(lhs))]
        made, loaded, ready, done = (box.sem(n) for n in ("made", "loaded", "ready", "done"))
        with nc.Block() as block:

            @block.gpsimd
            def _(pool):
                pool.iota(offset[:, :, :], pattern=[[P, blocks], [-width, heads]], base=0, channel_multiplier=1,
                          allow_small_or_imprecise_dtypes=True).then_inc(made, 1)

            @block.sync
            def _(sp):
                for s, d in enumerate(attn_ds):
                    flat_d = d.rearrange("h d -> (h d)")
                    for k in range(blocks):
                        sp.dma_start(attn[:, s, k:k + 1],
                                     flat_d[k * P:(k + 1) * P].rearrange("(p c) -> p c", c=1)).then_inc(loaded, 16)

            @block.vector
            def _(dve):
                dve.wait_ge(made, 1)
                dve.wait_ge(loaded, 32 * blocks)
                nc.vector.tensor_scalar(inside[:, :, :], offset[:, :, :], 0.0, None, ALU.is_ge)
                dve.drain()
                nc.vector.scalar_tensor_tensor(out=inside[:, :, :], in0=offset[:, :, :], scalar=float(width),
                                               in1=inside[:, :, :], op0=ALU.is_lt, op1=ALU.mult)
                dve.drain()
                for s in range(2):
                    for k in range(blocks):
                        nc.vector.tensor_scalar(spread[:, k, s, :], inside[:, k, :], attn[:, s, k:k + 1], None, ALU.mult)
                dve.drain().then_inc(ready, 1)
                dve.wait_ge(done, 1)
                n = rels * 2 * heads
                for fc in range(len(lhs)):
                    for s in range(2):
                        nc.vector.tensor_copy(
                            dst[:, fc, s, :, :],
                            folded[fc][:, 0:n].rearrange("p (r s h) -> p r s h", r=rels, s=2)[:, :, s, :])

            @block.tensor
            def _(pe):
                pe.wait_ge(ready, 1)
                for fc in range(len(lhs)):
                    for r in range(rels):
                        at = r * 2 * heads
                        for k in range(blocks):
                            last = nc.tensor.matmul(folded[fc][:, at:at + 2 * heads], lhs[fc][r][k],
                                                    spread[:, k, :, :].rearrange("p s h -> p (s h)"),
                                                    start=(k == 0), stop=(k == blocks - 1))
                last.then_inc(done, 1)


def relation_tables(nc, tag, c, h, wT, scoreT, rows_d, src_scores, dst_scores):
    RH = R8 * H1
    with Box(nc, tag) as box:
        stage = box.sb("stage", [P, 4, D])
        turned_sb = box.sb("turned_sb", [P, 4, D])
        out = box.sb("out", [P, 2, R8 * D])
        turned = [box.ps(f"turned{k}", [P, 512]) for k in range(2)]
        result = [box.ps(f"result{k}", [P, 512]) for k in range(5)]
        ready, staged, turns, copied, made_a, made_v, product = (
            box.sem(n) for n in ("ready", "staged", "turned", "copied", "made_a", "made_v", "product"))
        stored, slots_free = box.sem("stored"), box.sem("slots_free")
        with nc.Block() as block:

            @block.sync
            def _(sp):
                with nc.sync.Fori(0, NI) as i:
                    for u in range(U):
                        b = i * U + u
                        sp.wait_ge(made_a, b * 2 + 4)
                        sp.wait_ge(made_v, b * 3 + 5 + 3)
                        sp.dma_start(rows_d[bass.ds(b * P, P), :], out[:, u % 2, :]).then_inc(stored, 16)
                        sp.wait_ge(stored, b * 16 + 16)
                        sp.sem_inc(slots_free, 1)

            @block.scalar
            def _(act):
                act.wait_ge(ready, 1)

                def stage_block(b, u):
                    act.wait_ge(copied, b + (U - 2))
                    nc.scalar.copy(stage[:, u % 4, :], flat(h[:, bass.ds(b, 1), 0:D])).then_inc(staged, 1)

                with nc.scalar.Fori(0, NI) as i:
                    stage_block(i * U, 0)
                    for u in range(U):
                        b = i * U + u
                        if u + 1 < U:
                            stage_block(b + 1, u + 1)
                        act.wait_ge(slots_free, b + (2 if u == 0 else 1))
                        for j in range(2):
                            act.wait_ge(product, b * 5 + (j + 1))
                            nc.scalar.copy(out[:, u % 2, j * 512:(j + 1) * 512], result[j][:, :]).then_inc(made_a, 1)

            @block.tensor
            def _(pe):
                def turn(b, u):
                    pe.wait_ge(staged, b + 1)
                    pe.wait_ge(copied, b + (U if u == 0 else U - 1))
                    for k in range(2):
                        last = nc.tensor.transpose(turned[u % 2][:, k * P:(k + 1) * P],
                                                   stage[:, u % 4, k * P:(k + 1) * P], c.ident[:, :])
                    last.then_inc(turns, 1)

                pe.wait_ge(ready, 1)
                with nc.tensor.Fori(0, NI) as i:
                    turn(i * U, 0)
                    for u in range(U):
                        b = i * U + u
                        if u + 1 < U:
                            turn(b + 1, u + 1)
                        pe.wait_ge(copied, b + U + 1)
                        for j in range(5):
                            if j < 2:
                                pe.wait_ge(made_a, b * 2 + 2)
                            else:
                                pe.wait_ge(made_v, b * 3 + 5)
                            w = wT[:, :, j * 512:(j + 1) * 512] if j < 4 else scoreT
                            n = 512 if j < 4 else 2 * RH
                            for k in range(2):
                                last = nc.tensor.matmul(result[j][:, 0:n], turned_sb[:, u % 4, k * P:(k + 1) * P],
                                                        w[:, k, :], start=(k == 0), stop=(k == 1))
                            last.then_inc(product, 1)

            @block.vector
            def _(dve):
                dve.sem_inc(copied, U)
                dve.sem_inc(made_v, 5)
                dve.sem_inc(made_a, 2)
                dve.sem_inc(slots_free, 2)
                dve.drain().then_inc(ready, 1)

                def copy_turned(b, u):
                    dve.wait_ge(turns, b + 1)
                    nc.vector.tensor_copy(turned_sb[:, u % 4, :], turned[u % 2][:, 0:D]).then_inc(copied, 1)

                with nc.vector.Fori(0, NI) as i:
                    copy_turned(i * U, 0)
                    for u in range(U):
                        b = i * U + u
                        if u + 1 < U:
                            copy_turned(b + 1, u + 1)
                        dve.wait_ge(slots_free, b + (2 if u == 0 else 1))
                        for j in range(2, 4):
                            dve.wait_ge(product, b * 5 + (j + 1))
                            nc.vector.tensor_copy(out[:, u % 2, j * 512:(j + 1) * 512], result[j][:, :]).then_inc(made_v, 1)
                        dve.wait_ge(product, b * 5 + 5)
                        nc.vector.tensor_scalar(flat(src_scores[:, bass.ds(b, 1), :]), result[4][:, 0:RH], 1.0, None, ALU.mult)
                        nc.vector.tensor_scalar(flat(dst_scores[:, bass.ds(b, 1), :]), result[4][:, RH:2 * RH], 1.0,
                                                None, ALU.mult)
                        dve.drain().then_inc(made_v, 1)


def on_vector(nc, tag, loads, body):
    with Box(nc, tag) as box:
        loaded = box.sem("loaded")
        with nc.Block() as block:

            @block.sync
            def _(sp):
                for dst, src in loads:
                    sp.dma_start(dst, src).then_inc(loaded, 16)

            @block.vector
            def _(dve):
                if loads:
                    dve.wait_ge(loaded, 16 * len(loads))
                body(dve)


def row_bias(d, n):
    return d.rearrange("(o d) -> o d", o=1).broadcast_to([P, n])


def over_nodes(ap, n):
    return ap.rearrange("p (o d) -> p o d", o=1).broadcast_to([P, NB, n])


def layer1(nc, c, a, x, acc, order):
    rows_d = nc.dram_tensor("l1_rows", [NPAD, R8 * D], F32).ap()
    src_d = nc.dram_tensor("l1_src", [NPAD, R8 * H1], F32).ap()
    with Box(nc, "l1") as box:
        dst_scores = box.sb("dst_scores", [P, NB, R8 * H1])
        with Box(nc, "l1t") as b:
            wT = b.sb("wT", [P, 2, R8 * D])
            scoreT = b.sb("scoreT", [P, 2, 2 * R8 * H1])
            src_scores = b.sb("src_scores", [P, NB, R8 * H1])
            raw = acc[:, 0:2 * R8, 0:D]
            transpose_weights(nc, "l1x", c, [(a["L1_gnn_W"].rearrange("r o f -> (r o) f"), wT)], [raw])
            fold_attention(nc, "l1f", c,
                           [[[raw[:, 2 * r + k, fc * P:(fc + 1) * P] for k in range(2)] for r in range(R8)] for fc in range(2)],
                           (a["L1_gnn_attn_src"], a["L1_gnn_attn_dst"]), H1, D1,
                           scoreT[:, :, :].rearrange("p k (s r h) -> p k s r h", s=2, r=R8))
            normalize(nc, "n1", c, x, acc)
            relation_tables(nc, "l1p", c, acc, wT, scoreT, rows_d, src_scores, dst_scores)
            store_nodes(nc, "l1s", src_scores, src_d)
        score = box.sb("score", [P, T + G, H1])
        top = box.sb("top", [P, NB, H1])
        on_vector(nc, "l1z", [], lambda dve: nc.vector.memset(top[:, :, :], 0.0))
        attention_max(nc, "l1m", c, order, order.rel_other, src_d.rearrange("n (r h) -> (n r) h", r=R8), H1, R8,
                      dst_scores, score, top, x, c.x_d, later=(c.todo_d, c.rec_src_d))
        parts, rest = box.sb("parts", [P, NB, 3 * H1], BF16), box.sb("rest", [P, NB, H1])
        split_top(nc, "l1b", top, parts[:, :, :].rearrange("p b (a h) -> p b a h", a=3), rest)
        attention_sum(nc, "l1a", c, order, order.rel_other, rows_d.rearrange("n (r d) -> (n r) d", r=R8), D, H1,
                      score, parts, acc, x)
        rden = box.sb("rden", [P, NB, H1])

        def divide(dve):
            nc.vector.tensor_scalar(rden[:, :, :], acc[:, :, D:D + H1], 1e-12, None, ALU.add)
            dve.drain()
            nc.vector.reciprocal(rden[:, :, :], rden[:, :, :])
            dve.drain()
            m = acc[:, :, 0:D].rearrange("p b (h d) -> p b h d", h=H1)
            r = rden[:, :, :].rearrange("p b (h o) -> p b h o", o=1).broadcast_to([P, NB, H1, D1])
            nc.vector.tensor_tensor(m, m, r, ALU.mult)
            dve.drain()
            nc.vector.tensor_tensor(x[:, :, :], x[:, :, :], acc[:, :, 0:D], ALU.add)

        on_vector(nc, "l1d", [(x[:, :, :], c.x_d.rearrange("(b p) d -> p b d", p=P))], divide)


def layer2(nc, c, a, x, acc, by_dst, by_src):
    support_d = nc.dram_tensor("support", [NPAD, D], F32).ap()
    with Box(nc, "l2u") as box:
        records = box.sb("records", [P, T, 4], I32)
        scratch = box.sb("scratch", [P, T])
        alpha = box.sb("alpha", [P, R11])
        normalize(nc, "n2", c, x, acc,
                  load=[(records[:, :, :], c.rec_src_d[0:P * T, :].rearrange("(p t) f -> p t f", p=P)),
                        (alpha[:, :], a["L2_gnn_alpha"].rearrange("r o -> o r").broadcast_to([P, R11]))],
                  meanwhile=lambda dve: unpack(nc, dve, records, alpha, scratch, by_src))
    with Box(nc, "l2") as box:
        w = box.sb("w", [P, 2, D])
        bias = box.sb("bias", [P, D])
        project(nc, "l2p", c, [(acc, 2, None)], [w[:, 0, :], w[:, 1, :]], D,
                lambda dve, b, ps: nc.vector.tensor_scalar(flat(acc[:, bass.ds(b, 1), 0:D]), ps, 1.0, None, ALU.mult),
                load=[(w[:, :, :], a["L2_gnn_weight"].rearrange("(c p) o -> p c o", p=P)),
                      (bias[:, :], row_bias(a["L2_gnn_bias"], D))],
                store=[(acc[:, :, 0:D], support_d)])
        gather_sum(nc, "l2d", c, by_dst, by_dst.other, support_d, acc, D, weighted=True)
        gather_sum(nc, "l2r", c, by_src, by_src.other, support_d, acc, D, weighted=True, clear=False)

        def add(dve):
            nc.vector.tensor_tensor(acc[:, :, 0:D], acc[:, :, 0:D], over_nodes(bias[:, :], D), ALU.add)
            dve.drain()
            nc.vector.tensor_tensor(x[:, :, :], x[:, :, :], acc[:, :, 0:D], ALU.add)

        on_vector(nc, "l2a", [], add)


def layer3(nc, c, a, x, acc, order, out_d):
    rows_d = nc.dram_tensor("l3_rows", [NPAD, F3], F32).ap()
    src_d = nc.dram_tensor("l3_src", [NPAD, H3], F32).ap()
    with Box(nc, "l3") as box:
        w = box.sb("w", [P, 2, F3 + 2 * H3])
        wT = box.sb("wT", [P, 1, D])
        folded = box.sb("folded", [P, 2, 2, 1, H3])
        dst_scores = box.sb("dst_scores", [P, NB, H3])
        score = box.sb("score", [P, T + G, H3])
        top = box.sb("top", [P, NB, H3])
        rden = box.sb("rden", [P, NB, H3])
        lin = box.sb("lin", [P, D])
        lin_b = box.sb("lin_b", [P, D])
        gat_b = box.sb("gat_b", [P, F3])
        w_d = a["L3_gnn_W"]
        transpose_weights(nc, "l3x", c, [(w_d, wT)])
        fold_attention(nc, "l3f", c, [[[wT[:, 0, fc * P:(fc + 1) * P]]] for fc in range(2)],
                       (a["L3_gnn_attn_l"], a["L3_gnn_attn_r"]), H3, D3, folded)

        def prepare(dve):
            nc.vector.tensor_copy(w[:, :, F3:], folded[:, :, :, :, :].rearrange("p k s r h -> p k (s r h)"))
            nc.vector.memset(top[:, :, :], -NEG)

        on_vector(nc, "l3w", [(w[:, :, 0:F3], w_d.rearrange("(c p) o -> p c o", p=P)),
                              (lin[:, :], a["L3_gnn_lin_W"]), (lin_b[:, :], row_bias(a["L3_gnn_lin_b"], D)),
                              (gat_b[:, :], row_bias(a["L3_gnn_gat_bias"], F3))], prepare)
        normalize(nc, "n3", c, x, acc)
        cols = F3 + 2 * H3
        project(nc, "l3p", c, [(acc, 2, None)], [w[:, 0, :], w[:, 1, :]], cols,
                lambda dve, b, ps: nc.vector.tensor_scalar(flat(acc[:, bass.ds(b, 1), 0:cols]), ps, 1.0, None, ALU.mult),
                store=[(acc[:, :, 0:F3], rows_d), (acc[:, :, F3:F3 + H3], src_d)])
        on_vector(nc, "l3c", [], lambda dve: nc.vector.tensor_copy(dst_scores[:, :, :], acc[:, :, F3 + H3:cols]))
        attention_max(nc, "l3m", c, order, order.other, src_d, H3, 1, dst_scores, score, top, x, c.x_d)
        parts, rest = box.sb("parts", [P, NB, 3 * H3], BF16), box.sb("rest", [P, NB, H3])
        split_top(nc, "l3b", top, parts[:, :, :].rearrange("p b (a h) -> p b a h", a=3), rest)
        attention_sum(nc, "l3a", c, order, order.other, rows_d, F3, H3, score, parts, acc, x)

        def divide(dve):
            nc.vector.tensor_scalar(rden[:, :, :], acc[:, :, F3:F3 + H3], 1e-30, None, ALU.max)
            dve.drain()
            nc.vector.reciprocal(rden[:, :, :], rden[:, :, :])
            dve.drain()
            m = acc[:, :, 0:F3].rearrange("p b (h d) -> p b h d", h=H3)
            r = rden[:, :, :].rearrange("p b (h o) -> p b h o", o=1).broadcast_to([P, NB, H3, D3])
            nc.vector.tensor_tensor(m, m, r, ALU.mult)
            dve.drain()
            nc.vector.tensor_tensor(acc[:, :, 0:F3], acc[:, :, 0:F3], over_nodes(gat_b[:, :], F3), ALU.add)
            dve.drain()
            nc.vector.tensor_scalar(acc[:, :, 0:F3], acc[:, :, 0:F3], 0.0, None, ALU.max)

        on_vector(nc, "l3d", [(x[:, :, :], c.x_d.rearrange("(b p) d -> p b d", p=P))], divide)
        relu = box.sb("relu", [P, D])

        def finish(dve, b, ps):
            r = relu[:, :]
            nc.vector.tensor_tensor(r, ps, lin_b[:, :], ALU.add)
            dve.drain()
            out = flat(x[:, bass.ds(b, 1), :])
            nc.vector.scalar_tensor_tensor(out=out, in0=r, scalar=0.0, in1=out, op0=ALU.max, op1=ALU.add)
            return dve.drain()

        project(nc, "l3o", c, [(acc, 1, None)], [lin[:, :]], D, finish, store=[(x, out_d)])


def build(nc, a, out_d):
    c = Consts()
    c.x_d = nc.dram_tensor("x_parked", [NPAD, D], F32).ap()
    with Box(nc, "k") as top:
        setup_constants(nc, top, c)
        by_dst, by_src = Order(), Order()
        for name, o in (("dst", by_dst), ("src", by_src)):
            o.tile_bucket = top.sb(f"bucket_{name}", [1, T + RING], I32)
            o.local = top.sb(f"local_{name}", [P, T + G])
            o.weight = top.sb(f"weight_{name}", [P, T + G])
            o.other = top.sb(f"other_{name}", [P, T + RING], I32)
            o.rel_other = o.type8 = None
        by_dst.rel_other = top.sb("rel_other", [P, T + RING], I32)
        by_dst.type8 = top.sb("type8", [P, T + G])
        c.rdeg = top.sb("rdeg", [P, NB])
        c.rdeg_made = False
        rec_dst_d = nc.dram_tensor("rec_dst", [P * T, 4], I32).ap()
        c.rec_src_d = nc.dram_tensor("rec_src", [P * T + (T - EC) * P, 4], I32).ap()
        h0_d = nc.dram_tensor("h0", [NPAD, D], F32).ap()
        h1_d = nc.dram_tensor("h1", [NPAD, D], F32).ap()
        x = top.sb("x", [P, NB, D])
        c.todo_d = nc.dram_tensor("todo", [P, T, 5], I32).ap()
        sort_edges(nc, c, (a["dst"], a["src"]), a["edge_type_8"], a["edge_type_11"], a["L2_gnn_alpha"], rec_dst_d,
                   c.rec_src_d[0:P * T, :], c.todo_d, by_dst, by_src, x, a["x"], h0_d)
        acc = top.sb("acc", [P, NB, ACCW])
        gather_sum(nc, "g0", c, by_dst, by_dst.other, h0_d, acc, D, count=True, load=node_rows(a["x"], x))
        with Box(nc, "b1") as b:
            h = b.sb("h", [P, NB, D])
            sage(nc, "s0", c, x, h, acc, h0_d, a["L0_gnn_w1_l"], a["L0_gnn_w1_r"], a["L0_gnn_b1"], False,
                 store=[(h, h1_d)])
        gather_sum(nc, "g1", c, by_dst, by_dst.other, h1_d, acc, D)
        with Box(nc, "b2") as b:
            h = b.sb("h", [P, NB, D])
            sage(nc, "s1", c, x, h, acc, h1_d, a["L0_gnn_w2_l"], a["L0_gnn_w2_r"], a["L0_gnn_b2"], True)
        layer1(nc, c, a, x, acc, by_dst)
        layer2(nc, c, a, x, acc, by_dst, by_src)
        layer3(nc, c, a, x, acc, by_dst, out_d)


_INS = ['x', 'src', 'dst', 'edge_type_11', 'edge_type_8', 'L0_gnn_w1_l', 'L0_gnn_w1_r', 'L0_gnn_b1', 'L0_gnn_w2_l',
        'L0_gnn_w2_r', 'L0_gnn_b2', 'L1_gnn_W', 'L1_gnn_attn_src', 'L1_gnn_attn_dst', 'L2_gnn_weight', 'L2_gnn_bias',
        'L2_gnn_alpha', 'L3_gnn_W', 'L3_gnn_attn_l', 'L3_gnn_attn_r', 'L3_gnn_gat_bias', 'L3_gnn_lin_W', 'L3_gnn_lin_b']
_OUTS = [((N, D), 'float32')]


def kernel(**inputs):
    import numpy as _np
    import concourse.bacc as _bacc
    from concourse import mybir as _mybir
    from concourse.bass_utils import run_bass_kernel_spmd as _run

    nc = _bacc.Bacc("TRN2", target_bir_lowering=False, num_devices=1)
    arrays, args = {}, {}
    for name in _INS:
        a = _np.ascontiguousarray(inputs[name])
        arrays[f"in_{name}_dram"] = a
        args[name] = nc.dram_tensor(f"in_{name}_dram", a.shape, _mybir.dt.from_np(a.dtype), kind="ExternalInput").ap()
    out = nc.dram_tensor("out_0_dram", _OUTS[0][0], _mybir.dt.from_np(_np.dtype(_OUTS[0][1])), kind="ExternalOutput").ap()
    build(nc, args, out)
    r = _run(nc, [arrays], core_ids=[0])
    return r.results[0]["out_0_dram"]
```
